# Optimizing a Trainium2 kernel written in Bass

```python
import numpy as np
import jax
import jax.numpy as jnp

def _softmax(x, axis=-1):
    return jax.nn.softmax(x, axis=axis)

def _gelu(x):
    return jax.nn.gelu(x, approximate=True)

def _silu(x):
    return jax.nn.silu(x)

def _sigmoid(x):
    return jax.nn.sigmoid(x)

def _layernorm(x, axis=-1, eps=1e-05):
    m = jnp.mean(x, axis=axis, keepdims=True)
    v = jnp.var(x, axis=axis, keepdims=True)
    return (x - m) / jnp.sqrt(v + eps)

def _scatter_add(tgt, idx, src, axis=0):
    return tgt.at[idx].add(src)

def _segment_sum(src, seg, n):
    return jax.ops.segment_sum(src, seg, n)
kernel_name = 'mk_lm_tower_d1_tok_ids1024_r4_4b7766'

def setup_inputs(seed: int=0):
    np.random.seed(seed)
    _w = jnp.asarray

    def _rec_inputs():
        import jax
        import jax.numpy as jnp
        _rk = jax.random.key(seed)
        x = jax.random.randint(jax.random.fold_in(_rk, 1), (2, 2048), 0, 12564, jnp.int32)
        return x
    x = _rec_inputs()

    def _L0_tok_setup():
        import jax, jax.numpy as jnp
        import numpy as np
        D_M = 256
        VOCAB = 50257
        BASE = 10000.0
        B, S = (8, 1024)

        def _positional_encoding(seq_len, d_m, base, dtype):
            pos = jnp.arange(seq_len, dtype=dtype)
            i = jnp.arange(d_m // 2, dtype=dtype)
            inv_freq = jnp.power(jnp.asarray(base, dtype), -2.0 * i / d_m)
            ang = pos[:, None] * inv_freq[None, :]
            pe = jnp.stack([jnp.sin(ang), jnp.cos(ang)], axis=-1)
            return pe.reshape(seq_len, d_m)
        key = jax.random.key(seed)
        k1, k2 = jax.random.split(key)
        x = jax.random.randint(k1, (B, S), 0, VOCAB, dtype=jnp.int64)
        emb_table = jax.random.normal(k2, (VOCAB, D_M), dtype=jnp.float32)
        return {'x': x, 'emb_table': emb_table}
    _L0_tok_all = _L0_tok_setup()
    _L0_tok_in = {k: v for k, v in _L0_tok_all.items() if k in ('emb_table',)}
    del _L0_tok_all

    def _L0_attn_setup():
        import jax, jax.numpy as jnp
        import numpy as np
        D_MODEL = 256
        NHEAD = 16
        WIN = 128
        key = jax.random.key(seed)
        k0, k1, k2 = jax.random.split(key, 3)
        B, S = (4, 1024)
        x = jax.random.normal(k0, (B, S, D_MODEL), dtype=jnp.float32)
        Wqkv = jax.random.normal(k1, (D_MODEL, 3 * D_MODEL), dtype=jnp.float32) * 0.02
        bqkv = jnp.zeros((3 * D_MODEL,), dtype=jnp.float32)
        Wout = jax.random.normal(k2, (D_MODEL, D_MODEL), dtype=jnp.float32) * 0.02
        bout = jnp.zeros((D_MODEL,), dtype=jnp.float32)
        return {'x': x, 'Wqkv': Wqkv, 'bqkv': bqkv, 'Wout': Wout, 'bout': bout}
    _L0_attn_all = _L0_attn_setup()
    _L0_attn_in = {k: v for k, v in _L0_attn_all.items() if k in ('Wqkv', 'bqkv', 'Wout', 'bout')}
    del _L0_attn_all

    def _L0_ffn_setup():
        import jax, jax.numpy as jnp
        import numpy as np
        N_EMBED = 256
        FFN_HIDDEN = 1024
        NUM_EXPERTS = 8
        TOP_K = 2
        key = jax.random.key(seed)
        ks = jax.random.split(key, 8)
        d, f, E = (N_EMBED, FFN_HIDDEN, NUM_EXPERTS)
        s_d = 1.0 / np.sqrt(d)
        s_f = 1.0 / np.sqrt(f)
        return {'x': jax.random.normal(ks[0], (2, 512, d), dtype=jnp.float32), 'Wg': jax.random.uniform(ks[1], (d, E), jnp.float32, -s_d, s_d), 'bg': jax.random.uniform(ks[2], (E,), jnp.float32, -s_d, s_d), 'W1': jax.random.uniform(ks[3], (E, d, f), jnp.float32, -s_d, s_d), 'b1': jax.random.uniform(ks[4], (E, f), jnp.float32, -s_d, s_d), 'W2': jax.random.uniform(ks[5], (E, f, d), jnp.float32, -s_f, s_f), 'b2': jax.random.uniform(ks[6], (E, d), jnp.float32, -s_f, s_f)}
    _L0_ffn_all = _L0_ffn_setup()
    _L0_ffn_in = {k: v for k, v in _L0_ffn_all.items() if k in ('Wg', 'bg', 'W1', 'b1', 'W2', 'b2')}
    del _L0_ffn_all
    return {'x': x, 'L0_tok_emb_table': _L0_tok_in['emb_table'], 'L0_attn_Wqkv': _L0_attn_in['Wqkv'], 'L0_attn_bqkv': _L0_attn_in['bqkv'], 'L0_attn_Wout': _L0_attn_in['Wout'], 'L0_attn_bout': _L0_attn_in['bout'], 'L0_ffn_Wg': _L0_ffn_in['Wg'], 'L0_ffn_bg': _L0_ffn_in['bg'], 'L0_ffn_W1': _L0_ffn_in['W1'], 'L0_ffn_b1': _L0_ffn_in['b1'], 'L0_ffn_W2': _L0_ffn_in['W2'], 'L0_ffn_b2': _L0_ffn_in['b2']}

def reference(x, L0_tok_emb_table, L0_attn_Wqkv, L0_attn_bqkv, L0_attn_Wout, L0_attn_bout, L0_ffn_Wg, L0_ffn_bg, L0_ffn_W1, L0_ffn_b1, L0_ffn_W2, L0_ffn_b2):
    import jax
    import jax.numpy as jnp

    def _L0_tok_ref(x, emb_table):
        import jax, jax.numpy as jnp
        import numpy as np
        D_M = 256
        VOCAB = 50257
        BASE = 10000.0
        B, S = (8, 1024)

        def _positional_encoding(seq_len, d_m, base, dtype):
            pos = jnp.arange(seq_len, dtype=dtype)
            i = jnp.arange(d_m // 2, dtype=dtype)
            inv_freq = jnp.power(jnp.asarray(base, dtype), -2.0 * i / d_m)
            ang = pos[:, None] * inv_freq[None, :]
            pe = jnp.stack([jnp.sin(ang), jnp.cos(ang)], axis=-1)
            return pe.reshape(seq_len, d_m)
        emb = emb_table[x]
        pe = _positional_encoding(x.shape[1], emb_table.shape[1], BASE, emb_table.dtype)
        return emb + pe[None, :, :]

    def _L0_attn_ref(x, Wqkv, bqkv, Wout, bout):
        import jax, jax.numpy as jnp
        import numpy as np
        D_MODEL = 256
        NHEAD = 16
        WIN = 128
        B, S, dm = x.shape
        H, W = (NHEAD, WIN)
        Dh = dm // H
        nb = S // W
        qkv = (x @ Wqkv + bqkv).reshape(B, S, 3, H, Dh)
        q = qkv[:, :, 0].transpose(0, 2, 1, 3)
        k = qkv[:, :, 1].transpose(0, 2, 1, 3)
        v = qkv[:, :, 2].transpose(0, 2, 1, 3)
        qb = q.reshape(B, H, nb, W, Dh)
        kb = k.reshape(B, H, nb, W, Dh)
        vb = v.reshape(B, H, nb, W, Dh)
        kp = jnp.pad(kb, ((0, 0), (0, 0), (1, 1), (0, 0), (0, 0)))
        vp = jnp.pad(vb, ((0, 0), (0, 0), (1, 1), (0, 0), (0, 0)))
        kwin = jnp.concatenate([kp[:, :, :-2], kp[:, :, 1:-1], kp[:, :, 2:]], axis=3)
        vwin = jnp.concatenate([vp[:, :, :-2], vp[:, :, 1:-1], vp[:, :, 2:]], axis=3)
        scale = jnp.float32(1.0 / np.sqrt(dm))
        scores = jnp.einsum('bhnqd,bhnkd->bhnqk', qb, kwin) * scale
        n = jnp.arange(nb)[:, None, None]
        i = jnp.arange(W)[None, :, None]
        j = jnp.arange(3 * W)[None, None, :]
        qpos = n * W + i
        kpos = n * W - W + j
        mask = (jnp.abs(kpos - qpos) <= W) & (kpos >= 0) & (kpos < S)
        scores = jnp.where(mask[None, None], scores, jnp.float32(-1e+30))
        attn = jax.nn.softmax(scores, axis=-1)
        out = jnp.einsum('bhnqk,bhnkd->bhnqd', attn, vwin)
        out = out.reshape(B, H, S, Dh).transpose(0, 2, 1, 3).reshape(B, S, dm)
        return out @ Wout + bout

    def _L0_ffn_ref(x, Wg, bg, W1, b1, W2, b2):
        import jax, jax.numpy as jnp
        import numpy as np
        N_EMBED = 256
        FFN_HIDDEN = 1024
        NUM_EXPERTS = 8
        TOP_K = 2
        gate_scores = jax.nn.softmax(x @ Wg + bg, axis=-1)
        topk_scores, topk_idx = jax.lax.top_k(gate_scores, TOP_K)
        topk_scores = topk_scores / (jnp.sum(topk_scores, axis=-1, keepdims=True) + 1e-08)
        onehot = jax.nn.one_hot(topk_idx, NUM_EXPERTS, dtype=x.dtype)
        combine_w = jnp.einsum('bsk,bske->bse', topk_scores, onehot)
        output = jnp.zeros_like(x)
        for e in range(NUM_EXPERTS):
            h = jax.nn.gelu(x @ W1[e] + b1[e])
            y = h @ W2[e] + b2[e]
            output = output + y * combine_w[..., e:e + 1]
        return output
    h = _L0_tok_ref(x, L0_tok_emb_table)
    h = h + _L0_attn_ref(_layernorm(h, axis=-1), L0_attn_Wqkv, L0_attn_bqkv, L0_attn_Wout, L0_attn_bout)
    h = h + _L0_ffn_ref(_layernorm(h, axis=-1), L0_ffn_Wg, L0_ffn_bg, L0_ffn_W1, L0_ffn_b1, L0_ffn_W2, L0_ffn_b2)
    return h

_drawn_inputs = setup_inputs


def setup_inputs(seed=0):
    import zlib

    import numpy as np

    out = dict(_drawn_inputs(seed))
    spreads = {'L0_attn_bqkv': (0.0, 0.267), 'L0_attn_bout': (0.0, 0.1)}
    factors = {'L0_ffn_b1': 7.459, 'L0_ffn_b2': 5.223}
    for name, (base, spread) in spreads.items():
        noise = np.random.default_rng([zlib.crc32(name.encode()), seed]).standard_normal(out[name].shape)
        drawn = base * np.exp(spread * noise) if base else spread * noise
        out[name] = jnp.asarray(drawn.astype(out[name].dtype))
    for name, factor in factors.items():
        out[name] = (out[name] * factor).astype(out[name].dtype)
    return out
```

```python
from contextlib import ExitStack

import concourse.bass as bass
from concourse import mybir

F32 = mybir.dt.float32
F16 = mybir.dt.float16
BF16 = mybir.dt.bfloat16
I32 = mybir.dt.int32
U32 = mybir.dt.uint32
ALU = mybir.AluOpType
ACT = mybir.ActivationFunctionType
AX_X = mybir.AxisListType.X

P = 128
B, S, D = 2, 2048, 256
TOKENS = B * S
TILES = TOKENS // P
NB = S // P
DC = D // P
H, DH = 16, 16
PAIRS = H // 2
VW = DH + 1
E, F = 8, 1024
FC = F // P
TOPK = 2
GROUP = 4
GROUPS = TILES // GROUP
GT = GROUP * P
BLOCKS = B * (NB + 2)
PADDED = BLOCKS * P
REGION = TOKENS + P
SLOTS = TOPK * TOKENS // P + E - 1
SLOTS_RUN = SLOTS + SLOTS % 2
EPS = 1e-5
XS = 256.0
WS = 256.0
PS = XS * WS
HS = 16.0
YS = HS * WS
SCALE = 1.0 / D ** 0.5
NEG_BITS = 0xF149
ONES_ROW = 112

OB_QKV, OB_OUT, OB_G, OB_2 = 0, 3 * D, 4 * D, 4 * D + E
NBIAS = 4 * D + E + E * D
BIAS_ROUNDS = ((0, OB_2, PS), (OB_2, E * D // 2, YS), (OB_2 + E * D // 2, E * D // 2, YS))


def build(nc, x_idx, emb, pe_tab, wqkv, wout, wg, w1, b1, w2, biases, part_sel,
          mask_tab, valid_row, iota8, slot_iota, region_base, part_col, out):
    dram = lambda n, s, d: nc.dram_tensor(n, s, d, kind="Internal").ap()
    q_stack = dram("q_stack", (2, 3 * P, TOKENS), F16)
    k_stack = dram("k_stack", (2, 3 * P, PADDED), F16)
    v_rows = dram("v_rows", (PADDED, H * VW), F32)
    h1_rows = dram("h1_rows", (TOKENS, D), F32)
    h2_rows = dram("h2_rows", (TOKENS, D), F32)
    x_lists = dram("x_lists", (E * REGION, 2 * D), F16)
    b2_parts = dram("b2_parts", (3, E * D), BF16)
    y_slots = dram("y_slots", (SLOTS_RUN * P, D), F32)

    with ExitStack() as top:
        def keep(name, shape, dt):
            return top.enter_context(nc.sbuf_tensor(name, shape, dt))

        def sem(name):
            return top.enter_context(nc.semaphore(name))

        psum = top.enter_context(nc.psum_tensor("psum", [P, 8, 512], F32))
        psum16 = psum[:].bitcast(F16)
        w1_16 = keep("w1_16", [P, E * DC * 2 * F], F16)
        w2_16 = keep("w2_16", [P, E * FC * 2 * D], F16)
        b1_col = keep("b1_col", [P, E * FC], F32)
        wo16 = keep("wo16", [P, DC, 2, D], F16)
        wg16 = keep("wg16", [P, DC, 2, E], F16)
        bias3 = keep("bias3", [3, OB_2], BF16)
        ones3 = keep("ones3", [3, P], BF16)
        ident16 = keep("ident16", [P, P], F16)
        ident32 = keep("ident32", [P, P], F32)
        before = keep("before", [P, P], BF16)
        ones_sq = keep("ones_sq", [P, P], BF16)
        minus_half = keep("minus_half", [P, 1], F32)
        iota_e = keep("iota_e", [P, E], F32)
        base = keep("base", [P, 2, E], F32)
        pos_all = keep("pos_all", [P, TILES * TOPK], F32)
        y_pos = keep("y_pos", [P, TILES * TOPK], I32)
        w_all = keep("w_all", [P, TILES * TOPK], F32)
        slot_tab = keep("slot_tab", [1, 2, SLOTS_RUN], I32)

        s_passed = sem("waits_passed")

        with ExitStack() as ph:
            def sb(name, shape, dt):
                return ph.enter_context(nc.sbuf_tensor(name, shape, dt))

            idx_all = sb("idx_all", [P, TILES], I32)
            idx_col = sb("idx_col", [P, GROUP], I32)
            h_t = sb("h_t", [P, GROUP, D], F32)
            pe_t = sb("pe_t", [P, GROUP, D], F32)
            xs_t = sb("xs_t", [P, GROUP, D], F32)
            x16 = sb("x16", [P, GROUP, 2, D], F16)
            stat = sb("stat", [P, GROUP, 6], F32)
            mv = sb("mv", [P, GROUP, 2], F32)
            rstd = sb("rstd", [P, GROUP, 2], F32)
            xT = sb("xT", [P, 2, 2 * DC, GT], F16)
            qk16 = sb("qk16", [P, 4, 2, GT], F16)
            v_t = sb("v_t", [P, GROUP, H, VW], F32)
            wq16 = sb("wq16", [P, DC, 2, 3 * D], F16)
            w_in = sb("w_in", [P, 2, F], F32)
            wq_in = sb("wq_in", [P, DC, 3 * D], F32)
            wo_in = sb("wo_in", [P, DC, D], F32)
            wg_in = sb("wg_in", [P, DC, E], F32)
            brow = sb("brow", [3, 4 * D + E], F32)
            bs3 = sb("bs3", [3, 4 * D + E], BF16)
            sel = sb("sel", [3, 3], F32)
            b2_3 = sb("b2_3", [3, E * D], BF16)
            ones_g = sb("ones_g", [3, GT], BF16)
            zero16 = sb("zero16", [P, 3 * P], F16)
            zero32 = sb("zero32", [P, H * VW], F32)

            s_small = sem("small_loaded")
            s_b1 = sem("b1_loaded")
            s_bias_in = sem("bias_loaded")
            s_bias_step = sem("bias_step")
            s_bias = sem("bias_split")
            s_b2_out = sem("b2_parts_stored")
            s_const = sem("constants_made")
            s_zero = sem("zeros_made")
            s_pad = sem("padding_stored")
            s_idx = sem("index_column_copied")
            s_emb = [sem(f"embedding_gathered{u}") for u in range(GROUP)]
            s_pe = [sem(f"position_loaded{u}") for u in range(GROUP)]
            s_h = sem("h_added")
            s_h_out = [sem(f"h_stored{u}") for u in range(GROUP)]
            s_stat, s_mv, s_var, s_rstd = sem("ln1_stats"), sem("ln1_mean_var"), sem("ln1_inv_std"), sem("ln1_inv_std_scaled")
            s_xs, s_hi, s_lo = sem("ln1_out"), sem("x_hi"), sem("x_lo")
            s_tr = sem("x_transposed")
            s_xT = sem("xT_copied")
            s_qk = sem("qk_projected")
            s_qk_hi, s_qk_lo = sem("qk_hi"), sem("qk_lo")
            s_qk_out = sem("qk_stored")
            s_v = [sem(f"v_projected{r}") for r in range(2)]
            s_v_cp = sem("v_copied")
            s_v_out = sem("v_stored")
            s_w_in = [sem(f"expert_weights_loaded{r}") for r in range(2)]
            s_w_hi = [sem(f"expert_weights_hi{r}") for r in range(2)]
            s_w_lo = [sem(f"expert_weights_lo{r}") for r in range(2)]
            s_wq_hi, s_wq_lo = sem("wqkv_hi"), sem("wqkv_lo")
            s_ones = sem("v_ones_set")

            block = ph.enter_context(nc.Block())

            @block.sync
            def _(sp):
                for dst, src in ((idx_all[:], x_idx), (wq_in[:], wqkv.rearrange("(c p) n -> p c n", p=P)),
                                 (wo_in[:], wout.rearrange("(c p) n -> p c n", p=P)),
                                 (wg_in[:], wg.rearrange("(c p) n -> p c n", p=P)), (iota_e[:], iota8),
                                 (base[:, 0, :], region_base)):
                    sp.dma_start(dst, src).then_inc(s_small, 16)
                sp.dma_start(sel[:], part_sel).then_inc(s_bias_in, 16)
                for n, (at, size, _) in enumerate(BIAS_ROUNDS):
                    wait(sp, s_bias, n)
                    sp.dma_start(brow[:, 0:size], biases[:, at:at + size]).then_inc(s_bias_in, 16)

                def turn(g):
                    for u in range(GROUP):
                        wait(sp, s_h, g * GROUP)
                        sp.dma_start(pe_t[:, u, :], pe_tab[bass.ds((g * GROUP + u) * P, P), :]).then_inc(s_pe[u], 16)
                    for u in range(GROUP):
                        r = u % 2
                        wait(sp, s_w_hi[r], g * 2 + u // 2)
                        wait(sp, s_w_lo[r], g * 2 + u // 2)
                        if u < 2:
                            sp.dma_start(w_in[:, r, :], w1[bass.ds(g * D + u * P, P), :]).then_inc(s_w_in[r], 16)
                        else:
                            src = w2[bass.ds(g * F + (u - 2) * 4 * P, 4 * P), :].rearrange("(c p) n -> p c n", p=P)
                            sp.dma_start(w_in[:, r, :].rearrange("p (c n) -> p c n", c=4), src).then_inc(s_w_in[r], 16)
                    for u in range(GROUP):
                        wait(sp, s_h, g * GROUP + u + 1)
                        sp.dma_start(h1_rows[bass.ds((g * GROUP + u) * P, P), :], h_t[:, u, :]).then_inc(s_h_out[u], 16)
                    for m in range(4):
                        wait(sp, s_qk_lo, g * 4 + m + 1)
                        for part in range(3):
                            lo = (part == 2) if m < 2 else (part == 1)
                            src = qk16[:, m, int(lo), :]
                            if m < 2:
                                dst = q_stack[m % 2, part * P:(part + 1) * P, bass.ds(g * GT, GT)]
                            else:
                                dst = k_stack[m % 2, part * P:(part + 1) * P, bass.ds(g * GT + P + (g // (NB // GROUP)) * 2 * P, GT)]
                            sp.dma_start(dst, src).then_inc(s_qk_out, 16)
                    wait(sp, s_v_cp, g * GROUP + GROUP)
                    sp.dma_start(v_rows[bass.ds(g * GT + P + (g // (NB // GROUP)) * 2 * P, GT), :].rearrange("(u p) n -> p u n", p=P),
                                 v_t[:].rearrange("p u h w -> p u (h w)")).then_inc(s_v_out, 16)

                turns(sp, GROUPS, turn)
                sp.wait_ge(s_bias, len(BIAS_ROUNDS))
                sp.dma_start(b2_parts, b2_3[:]).then_inc(s_b2_out, 16)
                sp.wait_ge(s_b2_out, 16)
                sp.wait_ge(s_qk_out, GROUPS * 12 * 16)
                sp.wait_ge(s_v_out, GROUPS * 16)
                for u in range(GROUP):
                    sp.wait_ge(s_h_out[u], GROUPS * 16)

            @block.gpsimd
            def _(pool):
                g_ = nc.gpsimd
                g_.memset(minus_half[:], -0.5).then_inc(s_zero, 1)
                g_.memset(ident16[:], 0.0).then_inc(s_zero, 1)
                g_.memset(ident32[:], 0.0).then_inc(s_zero, 1)
                g_.memset(before[:], 0.0).then_inc(s_zero, 1)
                g_.memset(zero16[:], 0.0).then_inc(s_zero, 1)
                g_.memset(zero32[:], 0.0).then_inc(s_zero, 1)
                g_.memset(ones_sq[:], 1.0).then_inc(s_const, 1)
                g_.memset(ones3[:], 1.0).then_inc(s_const, 1)
                g_.memset(ones_g[:], 1.0).then_inc(s_const, 1)
                pool.wait_ge(s_zero, 6)
                g_.affine_select(out=ident16[:], in_=ident16[:], compare_op=ALU.not_equal, fill=1.0, base=0,
                                 pattern=[[-1, P]], channel_multiplier=1).then_inc(s_const, 1)
                g_.affine_select(out=ident32[:], in_=ident32[:], compare_op=ALU.not_equal, fill=1.0, base=0,
                                 pattern=[[-1, P]], channel_multiplier=1).then_inc(s_const, 1)
                g_.affine_select(out=before[:], in_=before[:], compare_op=ALU.is_ge, fill=1.0, base=0,
                                 pattern=[[-1, P]], channel_multiplier=1).then_inc(s_const, 1)
                for b in range(B):
                    for blk in (b * (NB + 2), b * (NB + 2) + NB + 1):
                        for a in range(2):
                            pool.dma_start(k_stack[a, :, blk * P:(blk + 1) * P].rearrange("(c p) t -> p c t", p=P),
                                           zero16[:].rearrange("p (c t) -> p c t", c=3)).then_inc(s_pad, 16)
                        pool.dma_start(v_rows[blk * P:(blk + 1) * P, :], zero32[:]).then_inc(s_pad, 16)
                pool.wait_ge(s_small, 6 * 16)

                def turn(g):
                    for u in range(GROUP):
                        wait(pool, s_emb[u], g * 16)
                        g_.tensor_copy(idx_col[:, u:u + 1], idx_all[:, bass.ds(g * GROUP + u, 1)]).then_inc(s_idx, 1)
                        held(pool, s_passed, (s_idx, g * GROUP + u + 1), (s_h_out[u], g * 16), (s_xs, g * GROUP))
                        g_.indirect_dma_start(h_t[:, u, :], None, emb, bass.IndirectOffsetOnAxis(idx_col[:, u:u + 1], 0)).then_inc(s_emb[u], 16)
                    for u in range(GROUP):
                        wait(pool, s_var, g * GROUP + u + 1)
                        g_.tensor_tensor(rstd[:, u, 1:2], rstd[:, u, 0:1], minus_half[:], ALU.pow).then_inc(s_rstd, 1)

                turns(pool, GROUPS, turn)
                pool.wait_ge(s_pad, 12 * 16)

            @block.scalar
            def _(act):
                a_ = nc.scalar
                act.dma_start(b1_col[:], b1).then_inc(s_b1, 16)
                act.wait_ge(s_b1, 16)
                act.wait_ge(s_small, 6 * 16)
                for n, (w16, w_f) in enumerate(((wq16, wq_in), (wo16, wo_in), (wg16, wg_in))):
                    a_.activation(w16[:, :, 0, :], w_f[:], ACT.Copy, scale=WS).then_inc(s_wq_hi, 1)

                def turn(i):
                    for par in range(2):
                        g = i * 2 + par
                        for u in range(GROUP):
                            t = g * GROUP + u
                            wait(act, s_xs, t + 1)
                            wait(act, s_tr, g * GROUP)
                            a_.copy(x16[:, u, 0, :], xs_t[:, u, :]).then_inc(s_hi, 1)
                        for u in range(GROUP):
                            t = g * GROUP + u
                            wait(act, s_tr, t + 1)
                            wait(act, s_v[par], i * GROUP)
                            a_.copy(xT[:, par, :, u * P:(u + 1) * P],
                                    psum16[:, u % 2, 0:4 * P].rearrange("p (c t) -> p c t", c=4)).then_inc(s_xT, 1)
                        for m in range(4):
                            wait(act, s_qk, g * 4 + m + 1)
                            wait(act, s_qk_out, g * (12 * 16))
                            a_.activation(qk16[:, m, 0, :], psum[:, 2 + m % 2, :], ACT.Copy, scale=1.0 / PS).then_inc(s_qk_hi, 1)
                        for u in range(GROUP):
                            wait(act, s_v[par], i * GROUP + u + 1)
                            wait(act, s_v_out, g * 16)
                            if par == 0 and u == 0:
                                wait(act, s_ones, 1)
                            a_.activation(v_t[:, u, :, 0:DH], psum[:, 4 + u % 2, 0:D].rearrange("p (h d) -> p h d", h=H),
                                          ACT.Copy, scale=1.0 / PS).then_inc(s_v_cp, 1)
                        for u in range(GROUP):
                            r = u % 2
                            wait(act, s_w_in[r], (g * 2 + u // 2 + 1) * 16)
                            if u < 2:
                                a_.activation(w1_16[:, bass.ds(g * (DC * 2 * F) + u * 2 * F, F)], w_in[:, r, :],
                                              ACT.Copy, scale=WS).then_inc(s_w_hi[r], 1)
                            else:
                                a_.activation(w2_16[:, bass.ds(g * (FC * 2 * D) + (u - 2) * (4 * 2 * D), 8 * D)].rearrange(
                                    "p (c h n) -> p c h n", c=4, h=2)[:, :, 0, :],
                                    w_in[:, r, :].rearrange("p (c n) -> p c n", c=4), ACT.Copy, scale=WS).then_inc(s_w_hi[r], 1)

                turns(act, GROUPS // 2, turn)

            @block.vector
            def _(dve):
                v_ = nc.vector
                v_.memset(v_t[:, :, :, DH:VW], 1.0 / XS).then_inc(s_ones, 1)
                for n, (w16, w_f) in enumerate(((wq16, wq_in), (wo16, wo_in), (wg16, wg_in))):
                    dve.wait_ge(s_wq_hi, n + 1)
                    v_.scalar_tensor_tensor(out=w16[:, :, 1, :], in0=w_f[:], scalar=WS, in1=w16[:, :, 0, :],
                                            op0=ALU.mult, op1=ALU.subtract).then_inc(s_wq_lo, 1)
                for n, (at, size, scale) in enumerate(BIAS_ROUNDS):
                    dve.wait_ge(s_bias_in, (n + 2) * 16)
                    parts = b2_3[:, at - OB_2:at - OB_2 + size] if n else bias3[:]
                    split_bias(dve, v_, brow[:, 0:size], bs3[:, 0:size], parts, scale, sel,
                               s_bias_step, n * BIAS_STEPS, s_bias)

                def tile(g, u):
                    t = g * GROUP + u
                    dve.wait_ge(s_emb[u], g * 16 + 16)
                    dve.wait_ge(s_pe[u], g * 16 + 16)
                    v_.tensor_tensor(h_t[:, u, :], h_t[:, u, :], pe_t[:, u, :], ALU.add).then_inc(s_h, 1)
                    dve.wait_ge(s_h, t + 1)
                    v_.bn_stats(stat[:, u, :], h_t[:, u, :]).then_inc(s_stat, 1)
                    held(dve, s_passed, (s_stat, t + 1))
                    v_.bn_aggr(mv[:, u, :], stat[:, u, :]).then_inc(s_mv, 1)
                    dve.wait_ge(s_mv, t + 1)
                    v_.tensor_scalar(rstd[:, u, 0:1], mv[:, u, 1:2], EPS, XS ** -2, ALU.add, ALU.mult).then_inc(s_var, 1)

                def scale(g, u):
                    t = g * GROUP + u
                    dve.wait_ge(s_rstd, t + 1)
                    v_.tensor_scalar(xs_t[:, u, :], h_t[:, u, :], mv[:, u, 0:1], rstd[:, u, 1:2],
                                     ALU.subtract, ALU.mult).then_inc(s_xs, 1)

                def turn(g):
                    for u in range(GROUP):
                        wait(dve, s_hi, g * GROUP)
                        wait(dve, s_lo, g * GROUP)
                        tile(g, u)
                    for u in range(GROUP):
                        scale(g, u)
                    for u in range(GROUP):
                        t = g * GROUP + u
                        wait(dve, s_hi, t + 1)
                        v_.tensor_tensor(x16[:, u, 1, :], xs_t[:, u, :], x16[:, u, 0, :], ALU.subtract).then_inc(s_lo, 1)
                    for m in range(4):
                        wait(dve, s_qk_hi, g * 4 + m + 1)
                        v_.scalar_tensor_tensor(out=qk16[:, m, 1, :], in0=psum[:, 2 + m % 2, :], scalar=1.0 / PS,
                                                in1=qk16[:, m, 0, :], op0=ALU.mult, op1=ALU.subtract).then_inc(s_qk_lo, 1)
                    for u in range(GROUP):
                        r = u % 2
                        wait(dve, s_w_hi[r], g * 2 + u // 2 + 1)
                        if u < 2:
                            at = lambda hl: w1_16[:, bass.ds(g * (DC * 2 * F) + (u * 2 + hl) * F, F)]
                            v_.scalar_tensor_tensor(out=at(1), in0=w_in[:, r, :], scalar=WS, in1=at(0),
                                                    op0=ALU.mult, op1=ALU.subtract).then_inc(s_w_lo[r], 1)
                        else:
                            at = lambda hl: w2_16[:, bass.ds(g * (FC * 2 * D) + (u - 2) * (4 * 2 * D), 8 * D)].rearrange(
                                "p (c h n) -> p c h n", c=4, h=2)[:, :, hl, :]
                            v_.scalar_tensor_tensor(out=at(1), in0=w_in[:, r, :].rearrange("p (c n) -> p c n", c=4), scalar=WS,
                                                    in1=at(0), op0=ALU.mult, op1=ALU.subtract).then_inc(s_w_lo[r], 1)

                turns(dve, GROUPS, turn)

            @block.tensor
            def _(pe):
                pe.wait_ge(s_const, 6)
                pe.wait_ge(s_wq_lo, 3)
                pe.wait_ge(s_bias, 1)

                def turn(i):
                    for par in range(2):
                        g = i * 2 + par
                        for u in range(GROUP):
                            t = g * GROUP + u
                            wait(pe, s_lo, t + 1)
                            if u >= 2:
                                wait(pe, s_xT, t - 1)
                            else:
                                wait(pe, s_xT, g * GROUP)
                            for c in range(2 * DC):
                                last = nc.tensor.transpose(psum16[:, u % 2, c * P:(c + 1) * P],
                                                           x16[:, u, c // DC, (c % DC) * P:(c % DC + 1) * P], ident16[:])
                            last.then_inc(s_tr, 1)
                        wait(pe, s_xT, g * GROUP + GROUP)
                        for m in range(4):
                            wait(pe, s_qk_lo, g * 4 + (m - 1 if m >= 2 else 0))
                            ps = psum[:, 2 + m % 2, :]
                            nc.tensor.matmul(ps, bias3[:, OB_QKV + m * P:OB_QKV + (m + 1) * P], ones_g[:], start=True, stop=False)
                            for c in range(DC):
                                for wl, xl in ((0, 0), (0, 1), (1, 0)):
                                    last = nc.tensor.matmul(ps, wq16[:, c, wl, m * P:(m + 1) * P], xT[:, par, xl * DC + c, :],
                                                            start=False, stop=(c == DC - 1 and wl == 1))
                            last.then_inc(s_qk, 1)
                        for u in range(GROUP):
                            wait(pe, s_v_cp, g * GROUP + (u - 1 if u >= 2 else 0))
                            ps = psum[:, 4 + u % 2, 0:D]
                            nc.tensor.matmul(ps, ones3[:, 0:P], bias3[:, OB_QKV + 2 * D:OB_QKV + 3 * D], start=True, stop=False)
                            for c in range(DC):
                                for wl, xl in ((0, 0), (0, 1), (1, 0)):
                                    last = nc.tensor.matmul(ps, xT[:, par, xl * DC + c, u * P:(u + 1) * P], wq16[:, c, wl, 2 * D:3 * D],
                                                            start=False, stop=(c == DC - 1 and wl == 1))
                            last.then_inc(s_v[par], 1)

                turns(pe, GROUPS // 2, turn)
        shared = Shared(b1_col=b1_col, b2_parts=b2_parts, base=base, before=before, bias3=bias3,
                        h1_rows=h1_rows, h2_rows=h2_rows, ident16=ident16, ident32=ident32, iota_e=iota_e,
                        k_stack=k_stack, mask_tab=mask_tab, minus_half=minus_half, nc=nc, ones3=ones3,
                        ones_sq=ones_sq, out=out, part_col=part_col, pos_all=pos_all, psum=psum,
                        psum16=psum16, q_stack=q_stack, s_passed=s_passed, sem=sem, slot_iota=slot_iota,
                        slot_tab=slot_tab, v_rows=v_rows, valid_row=valid_row, w1_16=w1_16, w2_16=w2_16,
                        w_all=w_all, wg16=wg16, wo16=wo16, x_lists=x_lists, y_pos=y_pos, y_slots=y_slots)
        attend(shared)
        plan(shared)
        experts(shared)
        combine(shared)


class Shared:

    def __init__(self, b1_col, b2_parts, base, before, bias3, h1_rows, h2_rows, ident16, ident32, iota_e,
                 k_stack, mask_tab, minus_half, nc, ones3, ones_sq, out, part_col, pos_all, psum, psum16,
                 q_stack, s_passed, sem, slot_iota, slot_tab, v_rows, valid_row, w1_16, w2_16, w_all, wg16,
                 wo16, x_lists, y_pos, y_slots):
        self.b1_col = b1_col
        self.b2_parts = b2_parts
        self.base = base
        self.before = before
        self.bias3 = bias3
        self.h1_rows = h1_rows
        self.h2_rows = h2_rows
        self.ident16 = ident16
        self.ident32 = ident32
        self.iota_e = iota_e
        self.k_stack = k_stack
        self.mask_tab = mask_tab
        self.minus_half = minus_half
        self.nc = nc
        self.ones3 = ones3
        self.ones_sq = ones_sq
        self.out = out
        self.part_col = part_col
        self.pos_all = pos_all
        self.psum = psum
        self.psum16 = psum16
        self.q_stack = q_stack
        self.s_passed = s_passed
        self.sem = sem
        self.slot_iota = slot_iota
        self.slot_tab = slot_tab
        self.v_rows = v_rows
        self.valid_row = valid_row
        self.w1_16 = w1_16
        self.w2_16 = w2_16
        self.w_all = w_all
        self.wg16 = wg16
        self.wo16 = wo16
        self.x_lists = x_lists
        self.y_pos = y_pos
        self.y_slots = y_slots


BIAS_STEPS = 8


def split_bias(dve, v_, row, tmp, out3, scale, sel, step, n, done):
    def then(ins, last=False):
        nonlocal n
        if last:
            ins.then_inc(done, 1)
            return
        ins.then_inc(step, 1)
        n += 1
        dve.wait_ge(step, n)

    then(v_.tensor_scalar(row, row, scale, None, ALU.mult))
    then(v_.tensor_copy(tmp, row))
    then(v_.tensor_scalar(out3, tmp, sel[:, 0:1], None, ALU.mult))
    then(v_.tensor_tensor(row, row, tmp, ALU.subtract))
    then(v_.tensor_copy(tmp, row))
    then(v_.scalar_tensor_tensor(out=out3, in0=tmp, scalar=sel[:, 1:2], in1=out3, op0=ALU.mult, op1=ALU.add))
    then(v_.tensor_tensor(row, row, tmp, ALU.subtract))
    then(v_.tensor_copy(tmp, row))
    then(v_.scalar_tensor_tensor(out=out3, in0=tmp, scalar=sel[:, 2:3], in1=out3, op0=ALU.mult, op1=ALU.add), last=True)


def held(eng, s_passed, *waits):
    for sem, v in waits:
        wait(eng, sem, v)
    eng.sem_inc(s_passed, 1)


def wait(eng, semaphore, value):
    if not isinstance(value, int) or value > 0:
        eng.wait_ge(semaphore, value)


def turns(eng, count, turn):
    turn(0)
    with eng.Fori(1, count) as i:
        turn(i)


ROUTE_STEPS = 16


def attend(k):
    nc, sem, psum, psum16 = k.nc, k.sem, k.psum, k.psum16
    ident16, ident32, bias3, ones3 = k.ident16, k.ident32, k.bias3, k.ones3
    with ExitStack() as ph:
        def sb(name, shape, dt):
            return ph.enter_context(nc.sbuf_tensor(name, shape, dt))

        RING = 4
        ks = sb("ks", [P, RING, PAIRS, 3 * P], F16)
        qz = sb("qz", [P, RING, PAIRS, 2, P], F16)
        vs = sb("vs", [P, 2, 3, H, VW], F32)
        masks = sb("masks", [P, 2, 3 * P], BF16)
        h1 = sb("h1", [P, 2, D], F32)
        mx = sb("mx", [P, 2, H], F32)
        mT = sb("mT", [H, P], F16)
        junk = sb("junk", [P, 3 * P], BF16)
        probs = sb("probs", [P, 4, 3, 2, P], F32)
        oT = sb("oT", [P, 4 * P], F32)
        rcp = sb("rcp", [P, H, 1], F32)
        a16 = sb("a16", [P, 2, D], F16)
        h2 = sb("h2", [P, D], F32)
        stat = sb("stat2", [P, 6], F32)
        mv = sb("mv2", [P, 2], F32)
        rstd = sb("rstd2", [P, 2], F32)
        xs2 = sb("xs2", [P, D], F32)
        x16 = sb("x16_2", [P, 2, 2 * D], F16)
        actT = sb("actT", [P, 2 * DC, P], F16)
        g8 = sb("g8", [P, 12, E], F32)
        gs = sb("gs", [P, 8], F32)
        gi = sb("gi", [P, 8], U32)
        member = sb("member", [P, E], BF16)
        pos_t = sb("pos_t", [P, 2, TOPK], I32)

        s_zero = sem("q_zeroed")
        s_stack = [sem(f"stacks_loaded{u}") for u in range(RING)]
        s_mask = [sem(f"mask_loaded{r}") for r in range(2)]
        s_vl = [sem(f"values_loaded{r}") for r in range(2)]
        s_h1 = [sem(f"h1_loaded{r}") for r in range(2)]
        s_sc, s_max = sem("scores_made"), sem("row_max_taken")
        s_mtr, s_mT = sem("max_transposed"), sem("max_negated")
        s_mrow = [sem(f"max_row_placed{u}") for u in range(RING)]
        s_pt, s_exp, s_sel, s_pv = sem("scores_T_made"), sem("exp_made"), sem("probs_masked"), sem("values_summed")
        s_oT, s_otr = sem("outputs_copied"), sem("outputs_transposed")
        s_rcp, s_att, s_ahi, s_alo = sem("sums_inverted"), sem("outputs_normalised"), sem("outputs_hi"), sem("outputs_lo")
        s_atr, s_aT, s_wo = sem("att_transposed"), sem("aT_copied"), sem("att_projected")
        s_h2 = sem("h2_added")
        s_h2o = sem("h2_stored")
        s_ln = sem("ln2_steps")
        s_var, s_rstd = sem("ln2_variance"), sem("ln2_inv_std")
        s_xlo, s_xtr, s_x2T, s_gate = sem("x2_split"), sem("x2_transposed"), sem("x2T_copied"), sem("gate_logits")
        s_gm, s_ge = sem("gate_max_negated"), sem("gate_exp")
        s_rt = sem("route_steps")
        s_mem, s_rank, s_pos = sem("members_marked"), sem("ranks_made"), sem("positions_made")
        s_sc1 = [sem(f"rows_scattered{r}") for r in range(2)]
        s_po = sem("output_bank_zeroed")

        block = ph.enter_context(nc.Block())

        def ahead(i, u, n):
            return i + (u + n) // RING, (u + n) % RING

        def over_tiles(eng, step):
            for u in range(RING):
                step(0, u, u)
            with eng.Fori(1, TILES // RING - 1) as i:
                for u in range(RING):
                    step(i, u, i * RING + u)
            for u in range(RING):
                step(TILES // RING - 1, u, TILES - RING + u)

        def known(t, n):
            return not isinstance(t, int) or 0 <= t + n < TILES

        def flat_pt(p):
            return psum[:].rearrange("p b n -> p (b n)")[:, (2 + 2 * (p % 2)) * 512:(2 + 2 * (p % 2)) * 512 + 3 * 2 * P]

        @block.sync
        def _(sp):
            def load(i, u):
                t = i * RING + u
                wait(sp, s_pv, (t - RING) * PAIRS + PAIRS)
                at = t * P + (t // NB) * 2 * P
                for a in range(2):
                    sp.dma_start(ks[a * 64:a * 64 + 48, u, :, :],
                                 k.k_stack[a, :, bass.ds(at, 3 * P)].rearrange("(r p) t -> r p t", p=PAIRS)).then_inc(s_stack[u], 16)
                    sp.dma_start(qz[a * 64:a * 64 + 48, u, :, a, :],
                                 k.q_stack[a, :, bass.ds(t * P, P)].rearrange("(r p) t -> r p t", p=PAIRS)).then_inc(s_stack[u], 16)
                sp.dma_start(ks[ONES_ROW:ONES_ROW + 1, u, :, :],
                             k.valid_row[:, :, bass.ds(at, 3 * P)]).then_inc(s_stack[u], 16)

            def load_mask(i, u):
                t = i * RING + u
                r = u % 2
                wait(sp, s_max, (t - 1) * H)
                sp.dma_start(masks[:, r, :], k.mask_tab[bass.ds(t * P, P), :].bitcast(BF16)).then_inc(s_mask[r], 16)

            def load_values(i, u):
                t = i * RING + u
                r = u % 2
                at = t * P + (t // NB) * 2 * P
                wait(sp, s_pv, (t - 1) * PAIRS)
                sp.dma_start(vs[:, r, :, :, :].rearrange("p j h w -> p j (h w)"),
                             k.v_rows[bass.ds(at, 3 * P), :].rearrange("(j p) n -> p j n", p=P)).then_inc(s_vl[r], 16)

            def load_residual(i, u):
                t = i * RING + u
                r = u % 2
                wait(sp, s_h2, t - 1)
                sp.dma_start(h1[:, r, :], k.h1_rows[bass.ds(t * P, P), :]).then_inc(s_h1[r], 16)

            def max_row(i, u):
                t = i * RING + u
                wait(sp, s_mT, t + 1)
                sp.dma_start(qz[ONES_ROW:ONES_ROW + 1, u, :, :, :].rearrange("o p a t -> o (p a) t"),
                             mT[:]).then_inc(s_mrow[u], 16)

            def store(i, u):
                t = i * RING + u
                wait(sp, s_h2, t + 1)
                sp.dma_start(k.h2_rows[bass.ds(t * P, P), :], h2[:]).then_inc(s_h2o, 16)

            def body(i, u, t):
                if known(t, 3):
                    load(*ahead(i, u, 3))
                    load_mask(*ahead(i, u, 3))
                load_residual(i, u)
                if known(t, 1):
                    load_values(*ahead(i, u, 1))
                if known(t, -2):
                    store(*ahead(i, u, -2))
                if known(t, 2):
                    max_row(*ahead(i, u, 2))

            sp.wait_ge(s_zero, 2)
            for t in range(3):
                load(0, t)
                load_mask(0, t) if t < 2 else None
            load_values(0, 0)
            for t in range(2):
                max_row(0, t)
            load_mask(0, 2)
            over_tiles(sp, body)
            for u in (RING - 2, RING - 1):
                store(TILES // RING - 1, u)
            sp.wait_ge(s_h2o, TILES * 16)

        @block.gpsimd
        def _(pool):
            g_ = nc.gpsimd
            g_.memset(qz[:], 0.0).then_inc(s_zero, 1)
            g_.memset(ks[:], 0.0).then_inc(s_zero, 1)

            def inv_std(t):
                wait(pool, s_var, t + 1)
                g_.tensor_tensor(rstd[:, 1:2], rstd[:, 0:1], k.minus_half[:], ALU.pow).then_inc(s_rstd, 1)

            def scatter(i, u, t):
                held(pool, k.s_passed, (s_pos, t + 1))
                for c in range(TOPK):
                    g_.indirect_dma_start(k.x_lists, bass.IndirectOffsetOnAxis(pos_t[:, u % 2, c:c + 1], 0), x16[:, u % 2, :], None)\
                      .then_inc(s_sc1[u % 2], 16)

            def body(i, u, t):
                for p in range(PAIRS):
                    held(pool, k.s_passed, (s_exp, t * PAIRS + p + 1))
                    pr = probs[:, p % 4, :, :, :]
                    g_.affine_select(out=pr[:, 0, :, :], in_=pr[:, 0, :, :], compare_op=ALU.is_ge, fill=0.0, base=0,
                                     pattern=[[0, 2], [-1, P]], channel_multiplier=1).then_inc(s_sel, 1)
                    g_.affine_select(out=pr[:, 2, :, :], in_=pr[:, 2, :, :], compare_op=ALU.is_ge, fill=0.0, base=0,
                                     pattern=[[0, 2], [1, P]], channel_multiplier=-1).then_inc(s_sel, 1)
                    if p == 5 and known(t, -2):
                        scatter(*ahead(i, u, -2), t - 2)
                if known(t, -1):
                    inv_std(t - 1)

            over_tiles(pool, body)
            last = TILES // RING - 1
            scatter(last, RING - 2, TILES - 2)
            inv_std(TILES - 1)
            scatter(last, RING - 1, TILES - 1)
            for r in range(2):
                pool.wait_ge(s_sc1[r], TILES // 2 * TOPK * 16)

        @block.scalar
        def _(act):
            a_ = nc.scalar

            def out_copy(t):
                wait(act, s_pv, t * PAIRS + PAIRS)
                wait(act, s_otr, t)
                a_.copy(oT[:], psum[:, 6, :]).then_inc(s_oT, 1)

            def att_copy(t):
                wait(act, s_atr, t + 1)
                a_.copy(actT[:].rearrange("p c t -> p (c t)"), psum16[:, 7, 0:4 * P]).then_inc(s_aT, 1)

            def x_copy(t):
                wait(act, s_xtr, t + 1)
                a_.copy(actT[:].rearrange("p c t -> p (c t)"), psum16[:, 7, 0:4 * P]).then_inc(s_x2T, 1)

            def gate_exp(t):
                wait(act, s_gm, t + 1)
                wait(act, s_rt, t * ROUTE_STEPS)
                a_.activation(g8[:, 1, :], psum[:, 7, 0:E], ACT.Exp, bias=gs[:, 0:1], scale=1.0 / PS,
                              accum_out=gs[:, 1:2]).then_inc(s_ge, 1)

            def body(i, u, t):
                for p in range(PAIRS):
                    wait(act, s_pt, t * PAIRS + p + 1)
                    wait(act, s_pv, t * PAIRS + p - 3)
                    a_.activation(probs[:, p % 4, :, :, :].rearrange("p j a t -> p (j a t)"),
                                  flat_pt(p), ACT.Exp, scale=SCALE).then_inc(s_exp, 1)
                    if p == 1:
                        if known(t, -1):
                            out_copy(t - 1)
                        if known(t, -2):
                            x_copy(t - 2)
                    if p == 3 and known(t, -2):
                        gate_exp(t - 2)
                    if p == 6 and known(t, -1):
                        att_copy(t - 1)

            over_tiles(act, body)
            out_copy(TILES - 1)
            x_copy(TILES - 2)
            gate_exp(TILES - 2)
            att_copy(TILES - 1)
            x_copy(TILES - 1)
            gate_exp(TILES - 1)

        @block.vector
        def _(dve):
            v_ = nc.vector
            v_.memset(psum[:, 6, :], 0.0).then_inc(s_po, 1)

            def maxima(i, u, t, s):
                r = u % 2
                if s == 0:
                    wait(dve, s_mask[r], (i * 2 + u // 2 + 1) * 16)
                    wait(dve, s_mtr, t - 1)
                held(dve, k.s_passed, (s_sc, t * H + s + 1), (s_max, t * H + s))
                v_.tensor_tensor_reduce(out=junk[:], in0=psum[:, s % 2, 0:3 * P], in1=masks[:, r, :], scale=1.0,
                                        scalar=-3.0e38, op0=ALU.add, op1=ALU.max, accum_out=mx[:, r, s:s + 1]).then_inc(s_max, 1)

            def negate_max(t):
                wait(dve, s_mtr, t + 1)
                v_.tensor_scalar(mT[:], psum[0:H, 0, 0:P], -1.0, -60000.0, ALU.mult, ALU.max).then_inc(s_mT, 1)

            def normalise(t):
                wait(dve, s_otr, t + 1)
                wait(dve, s_alo, t)
                bank = psum[:, 7, :]
                v_.reciprocal(rcp[:], bank.rearrange("p (s w) -> p s w", w=32)[:, :, DH:VW]).then_inc(s_rcp, 1)
                wait(dve, s_rcp, t + 1)
                v_.tensor_tensor(xs2[:].rearrange("p (a q d) -> p q a d", a=2, d=DH),
                                 bank.rearrange("p (q a w) -> p q a w", a=2, w=32)[:, :, :, 0:DH],
                                 rcp[:].rearrange("p (q a) o -> p q a o", a=2).to_broadcast([P, PAIRS, 2, DH]),
                                 ALU.mult).then_inc(s_att, 1)
                wait(dve, s_att, t + 1)
                v_.tensor_copy(a16[:, 0, :], xs2[:]).then_inc(s_ahi, 1)
                wait(dve, s_ahi, t + 1)
                v_.tensor_tensor(a16[:, 1, :], xs2[:], a16[:, 0, :], ALU.subtract).then_inc(s_alo, 1)

            def residual(i, u, t):
                r = u % 2
                n = i * 2 + u // 2
                wait(dve, s_wo, t + 1)
                wait(dve, s_xlo, t)
                wait(dve, s_h1[r], (n + 1) * 16)
                wait(dve, s_h2o, t * 16)
                v_.scalar_tensor_tensor(out=h2[:], in0=psum[:, 7, 0:D], scalar=1.0 / PS, in1=h1[:, r, :],
                                        op0=ALU.mult, op1=ALU.add).then_inc(s_h2, 1)
                wait(dve, s_h2, t + 1)
                v_.bn_stats(stat[:], h2[:]).then_inc(s_ln, 1)
                held(dve, k.s_passed, (s_ln, t * 4 + 1))
                v_.bn_aggr(mv[:], stat[:]).then_inc(s_ln, 1)
                wait(dve, s_ln, t * 4 + 2)
                v_.tensor_scalar(rstd[:, 0:1], mv[:, 1:2], EPS, XS ** -2, ALU.add, ALU.mult).then_inc(s_var, 1)

            def norm2(i, u, t):
                r = u % 2
                n = i * 2 + u // 2
                wait(dve, s_rstd, t + 1)
                v_.tensor_scalar(xs2[:], h2[:], mv[:, 0:1], rstd[:, 1:2], ALU.subtract, ALU.mult).then_inc(s_ln, 1)
                wait(dve, s_ln, t * 4 + 3)
                wait(dve, s_sc1[r], n * TOPK * 16)
                v_.tensor_copy(x16[:, r, 0:D], xs2[:]).then_inc(s_ln, 1)
                wait(dve, s_ln, t * 4 + 4)
                v_.tensor_tensor(x16[:, r, D:2 * D], xs2[:], x16[:, r, 0:D], ALU.subtract).then_inc(s_xlo, 1)

            def gate_max(t):
                held(dve, k.s_passed, (s_gate, t + 1))
                v_.max(g8[:, 0, :], psum[:, 7, 0:E]).then_inc(s_rt, 1)
                wait(dve, s_rt, t * ROUTE_STEPS + 1)
                wait(dve, s_ge, t)
                v_.tensor_scalar(gs[:, 0:1], g8[:, 0, 0:1], -1.0 / PS, None, ALU.mult).then_inc(s_gm, 1)

            def route(t):
                step = [1]

                def then(ins):
                    ins.then_inc(s_rt, 1)
                    step[0] += 1
                    held(dve, k.s_passed, (s_rt, t * ROUTE_STEPS + step[0]))

                wait(dve, s_ge, t + 1)
                then(v_.reciprocal(gs[:, 2:3], gs[:, 1:2]))
                then(v_.tensor_scalar(g8[:, 2, :], g8[:, 1, :], gs[:, 2:3], None, ALU.mult))
                then(v_.max(g8[:, 3, :], g8[:, 2, :]))
                then(v_.max_index(gi[:], g8[:, 3, :], g8[:, 2, :]))
                then(v_.tensor_copy(g8[:, 4, :], gi[:]))
                then(v_.tensor_scalar(g8[:, 5, :], k.iota_e[:], g8[:, 4, 0:1], None, ALU.is_equal))
                then(v_.tensor_scalar(g8[:, 6, :], k.iota_e[:], g8[:, 4, 1:2], None, ALU.is_equal))
                then(v_.scalar_tensor_tensor(out=gs[:, 3:4], in0=g8[:, 3, 0:1], scalar=1e-8, in1=g8[:, 3, 1:2],
                                             op0=ALU.add, op1=ALU.add))
                then(v_.reciprocal(gs[:, 4:5], gs[:, 3:4]))
                then(v_.tensor_scalar(k.w_all[:, bass.ds(t * TOPK, TOPK)], g8[:, 3, 0:TOPK], gs[:, 4:5], None, ALU.mult))
                wait(dve, s_rank, t)
                v_.tensor_tensor(member[:], g8[:, 5, :], g8[:, 6, :], ALU.add).then_inc(s_mem, 1)
                return step

            def place(i, u, t):
                step = [11]

                def then(ins):
                    ins.then_inc(s_rt, 1)
                    step[0] += 1
                    wait(dve, s_rt, t * ROUTE_STEPS + step[0])

                r, n = u % 2, i * 2 + u // 2
                wait(dve, s_rank, t + 1)
                wait(dve, s_pos, t)
                then(v_.tensor_tensor(g8[:, 7, :], psum[:, 7, 16:16 + E], k.base[:, r, :], ALU.add))
                then(v_.tensor_tensor(k.base[:, 1 - r, :], psum[:, 7, 16 + E:16 + 2 * E], k.base[:, r, :], ALU.add))
                for c in range(TOPK):
                    then(v_.tensor_tensor_reduce(out=g8[:, 8 + c, :], in0=g8[:, 5 + c, :], in1=g8[:, 7, :], scale=1.0, scalar=0.0,
                                                 op0=ALU.mult, op1=ALU.add, accum_out=g8[:, 10, c:c + 1]))
                then(v_.tensor_copy(k.pos_all[:, bass.ds(t * TOPK, TOPK)], g8[:, 10, 0:TOPK]))
                wait(dve, s_sc1[r], n * TOPK * 16)
                v_.tensor_copy(pos_t[:, r, :], g8[:, 10, 0:TOPK]).then_inc(s_pos, 1)
                assert step[0] == ROUTE_STEPS

            for t in range(2):
                for s in range(H):
                    maxima(0, t, t, s)
                if t:
                    wait(dve, s_mrow[t - 1], 16)
                negate_max(t)

            def step(i, u, t):
                j, w = ahead(i, u, 1)
                for p in range(PAIRS):
                    if known(t, 2):
                        for s in (2 * p, 2 * p + 1):
                            maxima(*ahead(i, u, 2), t + 2, s)
                    if known(t, -2):
                        if p == 0:
                            norm2(*ahead(i, u, -2), t - 2)
                        if p == 2:
                            gate_max(t - 2)
                        if p == 3:
                            route(t - 2)
                        if p == 4:
                            place(*ahead(i, u, -2), t - 2)
                    if p == 5 and known(t, -1):
                        normalise(t - 1)
                if known(t, 2):
                    wait(dve, s_mrow[w], (j + 1) * 16)
                    negate_max(t + 2)
                if known(t, -1):
                    residual(*ahead(i, u, -1), t - 1)

            over_tiles(dve, step)
            last = TILES // RING - 1
            norm2(last, RING - 2, TILES - 2)
            gate_max(TILES - 2)
            route(TILES - 2)
            place(last, RING - 2, TILES - 2)
            normalise(TILES - 1)
            residual(last, RING - 1, TILES - 1)
            norm2(last, RING - 1, TILES - 1)
            gate_max(TILES - 1)
            route(TILES - 1)
            place(last, RING - 1, TILES - 1)

        @block.tensor
        def _(pe):
            def scores(i, u, t, s):
                p, a = s // 2, s % 2
                if s == 0:
                    wait(pe, s_stack[u], (i + 1) * 5 * 16)
                    wait(pe, s_mT, t)
                wait(pe, s_max, t * H + s - 1)
                nc.tensor.matmul(psum[:, s % 2, 0:3 * P], qz[0:ONES_ROW, u, p, a, :], ks[0:ONES_ROW, u, p, :],
                                 start=True, stop=True).then_inc(s_sc, 1)

            def max_transpose(u, t):
                wait(pe, s_max, t * H + H)
                nc.tensor.transpose(psum[0:H, 0, 0:P], mx[:, u % 2, :], ident32[:]).then_inc(s_mtr, 1)

            def scores_t(i, u, t, p):
                if p == 0:
                    wait(pe, s_mrow[u], (i + 1) * 16)
                wait(pe, s_exp, t * PAIRS + p - 1)
                for j in range(3):
                    at = (2 + 2 * (p % 2)) * 512 + j * 2 * P
                    last = nc.tensor.matmul(psum[:, at // 512, at % 512:at % 512 + 2 * P], ks[0:ONES_ROW + 1, u, p, j * P:(j + 1) * P],
                                            qz[0:ONES_ROW + 1, u, p, :, :], start=True, stop=True)
                last.then_inc(s_pt, 1)

            def values(i, u, t, p):
                if p == 0:
                    wait(pe, s_vl[u % 2], (i * 2 + u // 2 + 1) * 16)
                    wait(pe, s_oT, t)
                wait(pe, s_sel, (t * PAIRS + p + 1) * 2)
                for j in range(3):
                    for a in range(2):
                        s = 2 * p + a
                        last = nc.tensor.matmul(psum[32 * (s % 4):32 * (s % 4) + VW, 6, (s // 4) * P:(s // 4 + 1) * P],
                                                vs[:, u % 2, j, a * PAIRS + p, :], probs[:, p % 4, j, a, :],
                                                start=(j == 0), stop=(j == 2), skip_group_check=True)
                last.then_inc(s_pv, 1)

            def out_transpose(t):
                wait(pe, s_oT, t + 1)
                wait(pe, s_rt, t * ROUTE_STEPS)
                for b in range(4):
                    last = nc.tensor.transpose(psum[:, 7, b * P:(b + 1) * P], oT[:, b * P:(b + 1) * P], ident32[:])
                last.then_inc(s_otr, 1)

            def att_transpose(t):
                wait(pe, s_alo, t + 1)
                for c in range(2 * DC):
                    last = nc.tensor.transpose(psum16[:, 7, c * P:(c + 1) * P], a16[:, c // DC, (c % DC) * P:(c % DC + 1) * P], ident16[:])
                last.then_inc(s_atr, 1)

            def three_pass(ps, left, right, bias_l, bias_r):
                nc.tensor.matmul(ps, bias_l, bias_r, start=True, stop=False)
                for c in range(DC):
                    for wl, xl in ((0, 0), (0, 1), (1, 0)):
                        last = nc.tensor.matmul(ps, left[:, xl * DC + c, :], right[:, c, wl, :],
                                                start=False, stop=(c == DC - 1 and wl == 1))
                return last

            def project(t):
                wait(pe, s_aT, t + 1)
                three_pass(psum[:, 7, 0:D], actT, k.wo16, ones3[:, 0:P], bias3[:, OB_OUT:OB_OUT + D]).then_inc(s_wo, 1)

            def x_transpose(u, t):
                wait(pe, s_xlo, t + 1)
                for c in range(2 * DC):
                    last = nc.tensor.transpose(psum16[:, 7, c * P:(c + 1) * P], x16[:, u % 2, c * P:(c + 1) * P], ident16[:])
                last.then_inc(s_xtr, 1)

            def gate(t):
                wait(pe, s_x2T, t + 1)
                three_pass(psum[:, 7, 0:E], actT, k.wg16, ones3[:, 0:P], bias3[:, OB_G:OB_G + E]).then_inc(s_gate, 1)

            def rank(t):
                wait(pe, s_mem, t + 1)
                nc.tensor.matmul(psum[:, 7, 16:16 + E], k.before[:], member[:], start=True, stop=True)
                nc.tensor.matmul(psum[:, 7, 16 + E:16 + 2 * E], k.ones_sq[:], member[:], start=True, stop=True).then_inc(s_rank, 1)

            pe.wait_ge(s_po, 1)
            for t in range(2):
                for s in range(H):
                    scores(0, t, t, s)
                max_transpose(t, t)

            def step(i, u, t):
                for p in range(PAIRS):
                    if known(t, 2):
                        for s in (2 * p, 2 * p + 1):
                            scores(*ahead(i, u, 2), t + 2, s)
                    scores_t(i, u, t, p)
                    if known(t, -2):
                        if p == 1:
                            x_transpose(u, t - 2)
                        if p == 2:
                            gate(t - 2)
                        if p == 4:
                            rank(t - 2)
                    if p == 5 and known(t, -1):
                        out_transpose(t - 1)
                    if p >= 2:
                        values(i, u, t, p - 2)
                    elif known(t, -1):
                        values(*ahead(i, u, -1), t - 1, p + PAIRS - 2)
                    if known(t, -1):
                        if p == 6:
                            att_transpose(t - 1)
                        if p == 7:
                            project(t - 1)
                if known(t, 2):
                    max_transpose(u, t + 2)

            over_tiles(pe, step)
            last = TILES // RING - 1
            values(last, RING - 1, TILES - 1, PAIRS - 2)
            values(last, RING - 1, TILES - 1, PAIRS - 1)
            x_transpose(RING - 2, TILES - 2)
            gate(TILES - 2)
            rank(TILES - 2)
            out_transpose(TILES - 1)
            att_transpose(TILES - 1)
            project(TILES - 1)
            x_transpose(RING - 1, TILES - 1)
            gate(TILES - 1)
            rank(TILES - 1)


def slot_table(dve, k, s_step, s_tail, s_in, pcol, tail, sl, sg, se, si, move):
    v_ = k.nc.vector
    n = SLOTS_RUN
    step = [0]

    def then(ins):
        ins.then_inc(s_step, 1)
        step[0] += 1
        dve.wait_ge(s_step, step[0])

    dve.wait_ge(s_in, 2 * 16)
    final = k.base[:, 0, :]
    v_.tensor_scalar(tail[:], final, pcol[:, 0:1], None, ALU.add).then_inc(s_tail, 1)
    up, rest, tiles, ends = (se[:, j, :] for j in range(4))
    iota, slot, exp_, skipped, row = (sl[0:1, j, :] for j in range(5))
    ends_0, tiles_0 = ends[0:1, :], tiles[0:1, :]
    then(v_.scalar_tensor_tensor(out=up, in0=k.iota_e[:], scalar=-float(REGION), in1=final,
                                 op0=ALU.mult, op1=ALU.add))
    then(v_.tensor_scalar(up, up, float(P - 1), None, ALU.add))
    then(v_.tensor_copy(si[:, 0, :], up))
    then(v_.tensor_scalar(si[:, 1, :], si[:, 0, :], P.bit_length() - 1, None, ALU.arith_shift_right))
    then(v_.tensor_copy(tiles, si[:, 1, :]))
    then(v_.tensor_copy(ends[:, 0:1], tiles[:, 0:1]))
    for e in range(1, E):
        then(v_.tensor_tensor(ends[:, e:e + 1], ends[:, e - 1:e], tiles[:, e:e + 1], ALU.add))
    then(v_.tensor_scalar(rest[:, 0:1], ends[:, E - 1:E], -1.0, None, ALU.add))
    then(v_.tensor_scalar(slot, iota, rest[0:1, 0:1], None, ALU.min))
    then(v_.tensor_tensor(sg[:, 0, :, :], slot.unsqueeze(2).to_broadcast([1, n, E]), ends_0.unsqueeze(1).to_broadcast([1, n, E]), ALU.is_ge))
    then(v_.tensor_tensor(sg[:, 1, :, :], sg[:, 0, :, :], tiles_0.unsqueeze(1).to_broadcast([1, n, E]), ALU.mult))
    then(v_.tensor_reduce(exp_, sg[:, 0, :, :], AX_X, ALU.add))
    then(v_.tensor_reduce(skipped, sg[:, 1, :, :], AX_X, ALU.add))
    then(v_.tensor_tensor(row, slot, skipped, ALU.subtract))
    then(v_.tensor_scalar(row, row, float(P), None, ALU.mult))
    then(v_.scalar_tensor_tensor(out=row, in0=exp_, scalar=float(REGION), in1=row, op0=ALU.mult, op1=ALU.add))
    then(v_.tensor_copy(k.slot_tab[:, 0, :], exp_))
    then(v_.tensor_copy(k.slot_tab[:, 1, :], row))
    gap = up
    then(v_.tensor_scalar(gap, tiles, float(P), -float(REGION), ALU.mult, ALU.add))
    for e in range(1, E):
        then(v_.tensor_scalar(move[:, 0, :], k.pos_all[:], float(e * REGION), gap[:, e - 1:e], ALU.is_ge, ALU.mult))
        then(v_.tensor_tensor(move[:, 1 + e % 2, :], move[:, 0, :], k.pos_all[:] if e == 1 else move[:, 1 + (e - 1) % 2, :], ALU.add))
    then(v_.tensor_copy(k.y_pos[:], move[:, 1 + (E - 1) % 2, :]))


def plan(k):
    nc, sem = k.nc, k.sem
    with ExitStack() as ph:
        def sb(name, shape, dt):
            return ph.enter_context(nc.sbuf_tensor(name, shape, dt))

        tail = sb("tail", [P, E], I32)
        pcol = sb("pcol", [P, 1], F32)
        zrow = sb("zrow", [P, 2 * D], F16)
        sl = sb("sl", [1, 5, SLOTS_RUN], F32)
        move = sb("move", [P, 3, TILES * TOPK], F32)
        sg = sb("sg", [1, 2, SLOTS_RUN, E], F32)
        se = sb("se", [P, 4, E], F32)
        si = sb("si", [P, 2, E], I32)
        s_in, s_zrow = sem("plan_constants_loaded"), sem("zero_row_made")
        s_tail, s_tail_out = sem("tail_rows_made"), sem("tails_zeroed")
        s_tab = sem("slot_table_steps")
        block = ph.enter_context(nc.Block())

        @block.sync
        def _(sp):
            sp.dma_start(pcol[:], k.part_col).then_inc(s_in, 16)
            sp.dma_start(sl[0:1, 0, :], k.slot_iota).then_inc(s_in, 16)

        @block.vector
        def _(dve):
            slot_table(dve, k, s_tab, s_tail, s_in, pcol, tail, sl, sg, se, si, move)

        @block.gpsimd
        def _(pool):
            nc.gpsimd.memset(zrow[:], 0.0).then_inc(s_zrow, 1)
            pool.wait_ge(s_zrow, 1)
            pool.wait_ge(s_tail, 1)
            for e in range(E):
                nc.gpsimd.indirect_dma_start(k.x_lists, bass.IndirectOffsetOnAxis(tail[:, e:e + 1], 0), zrow[:], None)\
                  .then_inc(s_tail_out, 16)
            pool.wait_ge(s_tail_out, E * 16)


def experts(k):
    nc, sem, psum, psum16 = k.nc, k.sem, k.psum, k.psum16
    with ExitStack() as ph:
        def sb(name, shape, dt):
            return ph.enter_context(nc.sbuf_tensor(name, shape, dt))

        xin = sb("xin", [P, 2, 2 * D], F16)
        xT = sb("xT_e", [P, 2, 2 * DC, P], F16)
        gel = sb("gel", [P, 2, FC, P], F32)
        h16 = sb("h16", [P, 2, 2, FC, P], F16)
        y = sb("y", [P, 2, D], F32)
        b2_3 = sb("b2_parts_e", [3, E * D], BF16)
        s_b2 = sem("b2_parts_loaded")

        s_x = [sem(f"rows_loaded{u}") for u in range(2)]
        s_tr = [sem(f"rows_transposed{u}") for u in range(2)]
        s_xT = [sem(f"rows_T_copied{u}") for u in range(2)]
        s_h = [sem(f"hidden_made{u}") for u in range(2)]
        s_g = [sem(f"gelu_made{u}") for u in range(2)]
        s_hi, s_lo = [sem(f"hidden_hi{u}") for u in range(2)], [sem(f"hidden_lo{u}") for u in range(2)]
        s_y = [sem(f"y_made{u}") for u in range(2)]
        s_yc = [sem(f"y_copied{u}") for u in range(2)]
        s_yo = [sem(f"y_stored{u}") for u in range(2)]

        block = ph.enter_context(nc.Block())

        def entry(eng, which, s):
            top = (E - 1, (E - 1) * REGION + TOKENS)[which]
            return eng.value_load(k.slot_tab[0:1, which, bass.ds(s, 1)], min_val=0, max_val=top)

        @block.sync
        def _(sp):
            sp.dma_start(b2_3[:], k.b2_parts).then_inc(s_b2, 16)

            def turn(i):
                for u in range(2):
                    row = entry(sp, 1, i * 2 + u)
                    wait(sp, s_tr[u], i)
                    sp.dma_start(xin[:, u, :], k.x_lists[bass.ds(row, P), :]).then_inc(s_x[u], 16)

            turns(sp, SLOTS_RUN // 2, turn)

        @block.gpsimd
        def _(pool):

            def turn(i):
                for u in range(2):
                    wait(pool, s_yc[u], i + 1)
                    pool.dma_start(k.y_slots[bass.ds((i * 2 + u) * P, P), :], y[:, u, :]).then_inc(s_yo[u], 16)

            turns(pool, SLOTS_RUN // 2, turn)
            for u in range(2):
                pool.wait_ge(s_yo[u], SLOTS_RUN // 2 * 16)

        @block.scalar
        def _(act):

            def turn(i):
                for u in range(2):
                    e = entry(act, 0, i * 2 + u)
                    wait(act, s_lo[u], i * 2)
                    for f in range(FC):
                        wait(act, s_h[u], i * 2 + f // 4 + 1)
                        nc.scalar.activation(gel[:, u, f, :], psum[:, 2 + 2 * u + f // 4, (f % 4) * P:(f % 4 + 1) * P],
                                             ACT.Gelu_apprx_tanh, bias=k.b1_col[:, bass.ds(e * FC + f, 1)],
                                             scale=1.0 / PS).then_inc(s_g[u], 1)

            turns(act, SLOTS_RUN // 2, turn)

        @block.vector
        def _(dve):
            v_ = nc.vector

            def y_copy(i, u):
                dve.wait_ge(s_y[u], i + 1)
                wait(dve, s_yo[u], i * 16)
                v_.tensor_scalar(y[:, u, :], psum[:, 6 + u, 0:D], 1.0 / YS, None, ALU.mult).then_inc(s_yc[u], 1)

            def split(i, u):
                for half in range(2):
                    c = slice(half * 4, half * 4 + 4)
                    dve.wait_ge(s_g[u], i * FC + half * 4 + 4)
                    if half == 0:
                        wait(dve, s_y[u], i)
                    v_.tensor_scalar(h16[:, u, 0, c, :], gel[:, u, c, :], HS, None, ALU.mult).then_inc(s_hi[u], 1)
                    dve.wait_ge(s_hi[u], i * 2 + half + 1)
                    v_.scalar_tensor_tensor(out=h16[:, u, 1, c, :], in0=gel[:, u, c, :], scalar=HS, in1=h16[:, u, 0, c, :],
                                            op0=ALU.mult, op1=ALU.subtract).then_inc(s_lo[u], 1)

            def x_copy(i, u):
                dve.wait_ge(s_tr[u], i + 1)
                wait(dve, s_h[u], i * 2)
                v_.tensor_copy(xT[:, u, :, :].rearrange("p c t -> p (c t)"), psum16[:, u, 0:4 * P]).then_inc(s_xT[u], 1)

            x_copy(0, 0)

            def step(i, u, first, last):
                if not last:
                    x_copy(*((i, 1) if u == 0 else (i + 1, 0)))
                split(i, u)
                if not first:
                    y_copy(*((i, 0) if u == 1 else (i - 1, 1)))

            step(0, 0, True, False)
            step(0, 1, False, False)
            with dve.Fori(1, SLOTS_RUN // 2 - 1) as i:
                step(i, 0, False, False)
                step(i, 1, False, False)
            step(SLOTS_RUN // 2 - 1, 0, False, False)
            step(SLOTS_RUN // 2 - 1, 1, False, True)
            y_copy(SLOTS_RUN // 2 - 1, 1)

        @block.tensor
        def _(pe):
            def transpose(i, u):
                pe.wait_ge(s_x[u], (i + 1) * 16)
                wait(pe, s_xT[u], i)
                for c in range(2 * DC):
                    last = nc.tensor.transpose(psum16[:, u, c * P:(c + 1) * P], xin[:, u, c * P:(c + 1) * P], k.ident16[:])
                last.then_inc(s_tr[u], 1)

            def hidden(i, u, e):
                pe.wait_ge(s_xT[u], i + 1)
                wait(pe, s_g[u], i * FC)
                for f in range(FC):
                    ps = psum[:, 2 + 2 * u + f // 4, (f % 4) * P:(f % 4 + 1) * P]
                    for c in range(DC):
                        for wl, xl in ((0, 0), (0, 1), (1, 0)):
                            last = nc.tensor.matmul(ps, k.w1_16[:, bass.ds(e * (DC * 2 * F) + ((c * 2 + wl) * F + f * P), P)],
                                                    xT[:, u, xl * DC + c, :], start=(c == 0 and wl == 0 and xl == 0),
                                                    stop=(c == DC - 1 and wl == 1))
                    if f % 4 == 3:
                        last.then_inc(s_h[u], 1)

            def outputs(i, u, e):
                wait(pe, s_yc[u], i)
                ps = psum[:, 6 + u, 0:D]
                nc.tensor.matmul(ps, k.ones3[:, 0:P], b2_3[:, bass.ds(e * D, D)], start=True, stop=False)
                for f in range(FC):
                    if f % 4 == 0:
                        pe.wait_ge(s_lo[u], i * 2 + f // 4 + 1)
                    for wl, hl in ((0, 0), (0, 1), (1, 0)):
                        last = nc.tensor.matmul(ps, h16[:, u, hl, f, :], k.w2_16[:, bass.ds(e * (FC * 2 * D) + (f * 2 + wl) * D, D)],
                                                start=False, stop=(f == FC - 1 and wl == 1))
                last.then_inc(s_y[u], 1)

            pe.wait_ge(s_b2, 16)
            transpose(0, 0)

            def step(i, u, first, last):
                hidden(i, u, entry(pe, 0, i * 2 + u))
                if not last:
                    transpose(*((i, 1) if u == 0 else (i + 1, 0)))
                if not first:
                    outputs(*((i, 0) if u == 1 else (i - 1, 1)), entry(pe, 0, i * 2 + u - 1))

            step(0, 0, True, False)
            step(0, 1, False, False)
            with pe.Fori(1, SLOTS_RUN // 2 - 1) as i:
                step(i, 0, False, False)
                step(i, 1, False, False)
            step(SLOTS_RUN // 2 - 1, 0, False, False)
            step(SLOTS_RUN // 2 - 1, 1, False, True)
            outputs(SLOTS_RUN // 2 - 1, 1, entry(pe, 0, SLOTS_RUN - 1))


def combine(k):
    nc, sem = k.nc, k.sem
    with ExitStack() as ph:
        def sb(name, shape, dt):
            return ph.enter_context(nc.sbuf_tensor(name, shape, dt))

        R = 4
        idx = sb("idx_c", [P, R, TOPK], I32)
        yy = sb("yy", [P, R, TOPK, D], F32)
        h2 = sb("h2_c", [P, R, D], F32)
        o1 = sb("o1", [P, R, D], F32)
        o2 = sb("o2", [P, R, D], F32)
        s_idx = sem("combine_index_copied")
        s_y = [sem(f"expert_rows_gathered{u}") for u in range(R)]
        s_h2 = [sem(f"residual_loaded{u}") for u in range(R)]
        s_o1, s_o2 = sem("first_expert_added"), sem("second_expert_added")
        s_out = [sem(f"output_stored{u}") for u in range(R)]
        block = ph.enter_context(nc.Block())

        @block.gpsimd
        def _(pool):
            g_ = nc.gpsimd

            def turn(i):
                for u in range(R):
                    t = i * R + u
                    wait(pool, s_y[u], i * (TOPK * 16))
                    g_.tensor_copy(idx[:, u, :], k.y_pos[:, bass.ds(t * TOPK, TOPK)]).then_inc(s_idx, 1)
                    held(pool, k.s_passed, (s_idx, t + 1), (s_o2, i * R))
                    for c in range(TOPK):
                        g_.indirect_dma_start(yy[:, u, c, :], None, k.y_slots,
                                              bass.IndirectOffsetOnAxis(idx[:, u, c:c + 1], 0)).then_inc(s_y[u], 16)

            turns(pool, TILES // R, turn)

        @block.sync
        def _(sp):

            def turn(i):
                for u in range(R):
                    wait(sp, s_o1, i * R)
                    sp.dma_start(h2[:, u, :], k.h2_rows[bass.ds((i * R + u) * P, P), :]).then_inc(s_h2[u], 16)

            turns(sp, TILES // R, turn)

        @block.scalar
        def _(act):

            def turn(i):
                for u in range(R):
                    wait(act, s_o2, i * R + u + 1)
                    act.dma_start(k.out[bass.ds((i * R + u) * P, P), :], o2[:, u, :]).then_inc(s_out[u], 16)

            turns(act, TILES // R, turn)
            for u in range(R):
                act.wait_ge(s_out[u], TILES // R * 16)

        @block.vector
        def _(dve):
            v_ = nc.vector

            def turn(i):
                for u in range(R):
                    t = i * R + u
                    wait(dve, s_h2[u], (i + 1) * 16)
                    wait(dve, s_y[u], (i + 1) * (TOPK * 16))
                    wait(dve, s_o2, i * R)
                    v_.scalar_tensor_tensor(out=o1[:, u, :], in0=yy[:, u, 0, :], scalar=k.w_all[:, bass.ds(t * TOPK, 1)],
                                            in1=h2[:, u, :], op0=ALU.mult, op1=ALU.add).then_inc(s_o1, 1)
                    wait(dve, s_o1, t + 1)
                    wait(dve, s_out[u], i * 16)
                    v_.scalar_tensor_tensor(out=o2[:, u, :], in0=yy[:, u, 1, :], scalar=k.w_all[:, bass.ds(t * TOPK + 1, 1)],
                                            in1=o1[:, u, :], op0=ALU.mult, op1=ALU.add).then_inc(s_o2, 1)

            turns(dve, TILES // R, turn)

def position_table(np):
    pos = np.arange(S, dtype=np.float32)
    i = np.arange(D // 2, dtype=np.float32)
    inv = np.power(10000.0, (np.float32(-2.0) * i / np.float32(D)).astype(np.float64)).astype(np.float32)
    ang = pos[:, None] * inv[None, :]
    table = np.stack([np.sin(ang.astype(np.float64)), np.cos(ang.astype(np.float64))], axis=-1)
    return np.tile(table.reshape(S, D).astype(np.float32), (B, 1))


def window_masks(np):
    n = np.arange(NB)[:, None, None]
    i = np.arange(P)[None, :, None]
    j = np.arange(3 * P)[None, None, :]
    key = n * P - P + j
    inside = (np.abs(key - (n * P + i)) <= P) & (key >= 0) & (key < S)
    return np.tile(np.where(inside, 0, NEG_BITS).reshape(NB * P, 3 * P).astype(np.uint16), (B, 1))


def kernel(x, L0_tok_emb_table, L0_attn_Wqkv, L0_attn_bqkv, L0_attn_Wout, L0_attn_bout, L0_ffn_Wg, L0_ffn_bg,
           L0_ffn_W1, L0_ffn_b1, L0_ffn_W2, L0_ffn_b2):
    import numpy as np
    import concourse.bacc as bacc
    from concourse.bass_utils import run_bass_kernel_spmd

    def by_dim(w):
        w = np.asarray(w).reshape(-1, 2, PAIRS, DH)
        return w.transpose(0, 1, 3, 2).reshape(-1, D)

    wqkv = np.asarray(L0_attn_Wqkv)
    bqkv = np.asarray(L0_attn_bqkv).reshape(1, -1)
    lay = lambda w: np.concatenate([by_dim(w[:, 0:D]), by_dim(w[:, D:2 * D]), w[:, 2 * D:]], axis=1)
    row = np.concatenate([lay(bqkv)[0], np.asarray(L0_attn_bout), np.asarray(L0_ffn_bg), np.asarray(L0_ffn_b2).reshape(-1)])
    valid = np.zeros((BLOCKS, P), np.float16)
    for b in range(B):
        valid[b * (NB + 2) + 1:b * (NB + 2) + 1 + NB] = 1
    arrays = {
        "x_idx": np.asarray(x).reshape(TILES, P).T,
        "emb": np.asarray(L0_tok_emb_table),
        "pe_tab": position_table(np),
        "wqkv": lay(wqkv),
        "wout": np.asarray(L0_attn_Wout),
        "wg": np.asarray(L0_ffn_Wg),
        "w1": np.asarray(L0_ffn_W1).reshape(E * D, F),
        "b1": np.asarray(L0_ffn_b1).reshape(E * FC, P).T,
        "w2": np.asarray(L0_ffn_W2).reshape(E * F, D),
        "biases": np.stack([row] * 3),
        "part_sel": np.eye(3, dtype=np.float32),
        "mask_tab": window_masks(np),
        "valid_row": np.tile(valid.reshape(1, 1, -1), (1, PAIRS, 1)),
        "iota8": np.tile(np.arange(E, dtype=np.float32), (P, 1)),
        "slot_iota": np.arange(SLOTS_RUN, dtype=np.float32).reshape(1, -1),
        "region_base": np.tile(np.arange(E, dtype=np.float32) * REGION, (P, 1)),
        "part_col": np.arange(P, dtype=np.float32).reshape(P, 1),
    }
    arrays = {n: np.ascontiguousarray(a) for n, a in arrays.items()}
    nc = bacc.Bacc("TRN2", target_bir_lowering=False, num_devices=1)
    ins = [nc.dram_tensor(n, a.shape, mybir.dt.from_np(a.dtype), kind="ExternalInput").ap() for n, a in arrays.items()]
    out = nc.dram_tensor("out", (TOKENS, D), F32, kind="ExternalOutput").ap()
    build(nc, *ins, out)
    r = run_bass_kernel_spmd(nc, [arrays], core_ids=[0])
    return r.results[0]["out"].reshape(B, S, D)
```

```python
from contextlib import ExitStack

import concourse.bass as bass
from concourse import mybir

F32 = mybir.dt.float32
F16 = mybir.dt.float16
BF16 = mybir.dt.bfloat16
I32 = mybir.dt.int32
U32 = mybir.dt.uint32
ALU = mybir.AluOpType
ACT = mybir.ActivationFunctionType
AX_X = mybir.AxisListType.X

P = 128
B, S, D = 2, 2048, 256
TOKENS = B * S
TILES = TOKENS // P
NB = S // P
DC = D // P
H, DH = 16, 16
PAIRS = H // 2
VW = DH + 1
E, F = 8, 1024
FC = F // P
TOPK = 2
GROUP = 4
GROUPS = TILES // GROUP
GT = GROUP * P
BLOCKS = B * (NB + 2)
PADDED = BLOCKS * P
REGION = TOKENS + P
SLOTS = TOPK * TOKENS // P + E - 1
SLOTS_RUN = SLOTS + SLOTS % 2
EPS = 1e-5
XS = 256.0
WS = 256.0
PS = XS * WS
HS = 16.0
YS = HS * WS
SCALE = 1.0 / D ** 0.5
NEG_BITS = 0xF149
ONES_ROW = 112

OB_QKV, OB_OUT, OB_G, OB_2 = 0, 3 * D, 4 * D, 4 * D + E
WROWS = 4


def build(nc, x_idx, emb, pe_tab, wqkv, wout, wg, w1, b1, w2, b2, biases, part_sel,
          mask_tab, valid_row, iota8, slot_iota, region_base, part_col, out):
    dram = lambda n, s, d: nc.dram_tensor(n, s, d, kind="Internal").ap()
    q_stack = dram("q_stack", (2, 3 * P, TOKENS), F16)
    k_stack = dram("k_stack", (2, 3 * P, PADDED), F16)
    v_rows = dram("v_rows", (PADDED, H * VW), F32)
    h1_rows = dram("h1_rows", (TOKENS, D), F32)
    h2_rows = dram("h2_rows", (TOKENS, D), F32)
    x_lists = dram("x_lists", (E * REGION, 2 * D), F16)
    y_slots = dram("y_slots", (SLOTS_RUN * P, D), F32)

    with ExitStack() as top:
        def keep(name, shape, dt):
            return top.enter_context(nc.sbuf_tensor(name, shape, dt))

        def sem(name):
            return top.enter_context(nc.semaphore(name))

        psum = top.enter_context(nc.psum_tensor("psum", [P, 8, 512], F32))
        psum16 = psum[:].bitcast(F16)
        w1_16 = keep("w1_16", [P, E * DC * 2 * F], F16)
        w2_16 = keep("w2_16", [P, E * FC * 2 * D], F16)
        b1_col = keep("b1_col", [P, E * FC], F32)
        wo16 = keep("wo16", [P, DC, 2, D], F16)
        wg16 = keep("wg16", [P, DC, 2, E], F16)
        bias3 = keep("bias3", [3, OB_2], BF16)
        ones3 = keep("ones3", [3, P], BF16)
        ident16 = keep("ident16", [P, P], F16)
        ident32 = keep("ident32", [P, P], F32)
        before = keep("before", [P, P], BF16)
        ones_sq = keep("ones_sq", [P, P], BF16)
        minus_half = keep("minus_half", [P, 1], F32)
        iota_e = keep("iota_e", [P, E], F32)
        base = keep("base", [P, 2, E], F32)
        pos_all = keep("pos_all", [P, TILES * TOPK], F32)
        y_pos = keep("y_pos", [P, TILES * TOPK], I32)
        w_all = keep("w_all", [P, TILES * TOPK], F32)
        slot_tab = keep("slot_tab", [1, 2, SLOTS_RUN], I32)

        s_passed = sem("waits_passed")

        with ExitStack() as ph:
            def sb(name, shape, dt):
                return ph.enter_context(nc.sbuf_tensor(name, shape, dt))

            idx_all = sb("idx_all", [P, TILES], I32)
            idx_col = sb("idx_col", [P, 2, GROUP], I32)
            h_t = sb("h_t", [P, 2, GROUP, D], F32)
            pe_xs = sb("pe_xs", [P, 2, GROUP, D], F32)
            x16 = sb("x16", [P, GROUP, 2, D], F16)
            stat = sb("stat", [P, GROUP, 6], F32)
            mv = sb("mv", [P, GROUP, 2], F32)
            rstd = sb("rstd", [P, GROUP, 2], F32)
            xT = sb("xT", [P, 2, 2 * DC, GT], F16)
            qk16 = sb("qk16", [P, 4, 2, GT], F16)
            v_t = sb("v_t", [P, GROUP, H, VW], F32)
            wq16 = sb("wq16", [P, DC, 2, 3 * D], F16)
            w_in = sb("w_in", [P, WROWS, F], F32)
            brow = sb("brow", [3, OB_2], F32)
            bs3 = sb("bs3", [3, OB_2], BF16)
            sel = sb("sel", [3, 3], F32)
            ones_g = sb("ones_g", [3, GT], BF16)
            zero16 = sb("zero16", [P, 3 * P], F16)
            zero32 = sb("zero32", [P, H * VW], F32)

            two = range(2)
            s_idx_in = sem("indices_loaded")
            s_small = sem("small_loaded")
            s_bias_in = sem("bias_loaded")
            s_bias_step = sem("bias_step")
            s_bias = sem("bias_split")
            s_const = sem("constants_made")
            s_zero = sem("zeros_made")
            s_pad = sem("padding_stored")
            s_idx = sem("index_column_copied")
            s_emb = [[sem(f"embedding_gathered{r}{u}") for u in range(GROUP)] for r in two]
            s_pe = [[sem(f"position_loaded{r}{u}") for u in range(GROUP)] for r in two]
            s_h = sem("h_added")
            s_h_out = [[sem(f"h_stored{r}{u}") for u in range(GROUP)] for r in two]
            s_stat, s_mv, s_var, s_rstd = sem("ln1_stats"), sem("ln1_mean_var"), sem("ln1_variance"), sem("ln1_inv_std")
            s_xs, s_hi, s_lo = sem("ln1_out"), sem("x_hi"), sem("x_lo")
            s_tr = sem("x_transposed")
            s_xT = sem("xT_copied")
            s_qk = sem("qk_projected")
            s_qk_hi, s_qk_lo = sem("qk_hi"), sem("qk_lo")
            s_qk_out = sem("qk_stored")
            s_v = [sem(f"v_projected{r}") for r in two]
            s_v_cp = sem("v_copied")
            s_v_out = sem("v_stored")
            s_w_in = [sem(f"weights_loaded{r}") for r in range(WROWS)]
            s_w_hi = [sem(f"weights_hi{r}") for r in range(WROWS)]
            s_w_lo = [sem(f"weights_lo{r}") for r in range(WROWS)]
            s_ones = sem("v_ones_set")

            block = ph.enter_context(nc.Block())

            def group_turns(eng, step):
                for r in two:
                    step(0, r)
                with eng.Fori(1, GROUPS // 2 - 1) as i:
                    for r in two:
                        step(i, r)
                for r in two:
                    step(GROUPS // 2 - 1, r)

            def after(i, r):
                return i + r, 1 - r

            def is_last(i, r):
                return isinstance(i, int) and 2 * i + r == GROUPS - 1

            def in_last_two(i):
                return isinstance(i, int) and i == GROUPS // 2 - 1

            own_weights = [(c, w_in[:, c, 0:3 * D], lambda hl, c=c: wq16[:, c, hl, :]) for c in range(DC)]
            own_weights.append((2, w_in[:, 2, 0:DC * D].rearrange("p (c n) -> p c n", c=DC), lambda hl: wo16[:, :, hl, :]))
            own_weights.append((3, w_in[:, 3, 0:DC * E].rearrange("p (c n) -> p c n", c=DC), lambda hl: wg16[:, :, hl, :]))

            def expert_row(e, r):
                if r < 2:
                    src = w_in[:, r, :]
                    return src, lambda hl: w1_16[:, bass.ds(e * (DC * 2 * F) + (r * 2 + hl) * F, F)]
                src = w_in[:, r, :].rearrange("p (c n) -> p c n", c=4)
                at = e * (FC * 2 * D) + (r - 2) * (4 * 2 * D)
                return src, lambda hl: w2_16[:, bass.ds(at, 8 * D)].rearrange("p (c h n) -> p c h n", c=4, h=2)[:, :, hl, :]

            @block.sync
            def _(sp):
                def load_positions(i, r):
                    for u in range(GROUP):
                        wait(sp, s_hi, (i * 2 + r - 2) * GROUP + u + 1)
                        wait(sp, s_lo, (i * 2 + r - 2) * GROUP + u + 1)
                        sp.dma_start(pe_xs[:, r, u, :], pe_tab[bass.ds(((i * 2 + r) * GROUP + u) * P, P), :]).then_inc(s_pe[r][u], 16)

                def load_weights(e, rows):
                    for r in rows:
                        sp.wait_ge(s_w_hi[r], e + 1)
                        sp.wait_ge(s_w_lo[r], e + 1)
                        if r < 2:
                            sp.dma_start(w_in[:, r, :], w1[bass.ds(e * D + r * P, P), :]).then_inc(s_w_in[r], 16)
                        else:
                            src = w2[bass.ds(e * F + (r - 2) * 4 * P, 4 * P), :].rearrange("(c p) n -> p c n", p=P)
                            sp.dma_start(w_in[:, r, :].rearrange("p (c n) -> p c n", c=4), src).then_inc(s_w_in[r], 16)

                def store_h(i, r):
                    for u in range(GROUP):
                        t = (i * 2 + r) * GROUP + u
                        sp.wait_ge(s_h, t + 1)
                        sp.dma_start(h1_rows[bass.ds(t * P, P), :], h_t[:, r, u, :]).then_inc(s_h_out[r][u], 16)

                def step(i, r):
                    g = i * 2 + r
                    if not in_last_two(i):
                        load_positions(i + 1, r)
                    if not is_last(i, r):
                        store_h(*after(i, r))
                    for m in range(4):
                        sp.wait_ge(s_qk_lo, g * 4 + m + 1)
                        for part in range(3):
                            lo = (part == 2) if m < 2 else (part == 1)
                            if m < 2:
                                dst = q_stack[m % 2, part * P:(part + 1) * P, bass.ds(g * GT, GT)]
                            else:
                                dst = k_stack[m % 2, part * P:(part + 1) * P, bass.ds(g * GT + P + (g // (NB // GROUP)) * 2 * P, GT)]
                            sp.dma_start(dst, qk16[:, m, int(lo), :]).then_inc(s_qk_out, 16)
                    if not is_last(i, r):
                        load_weights(g + 1, (0, 1))
                    sp.wait_ge(s_v_cp, g * 2 + 2)
                    sp.dma_start(v_rows[bass.ds(g * GT + P + (g // (NB // GROUP)) * 2 * P, GT), :].rearrange("(u p) n -> p u n", p=P),
                                 v_t[:].rearrange("p u h w -> p u (h w)")).then_inc(s_v_out, 16)
                    if not is_last(i, r):
                        load_weights(g + 1, (2, 3))

                sp.dma_start(idx_all[:], x_idx).then_inc(s_idx_in, 16)
                load_positions(0, 0)
                for c in range(DC):
                    sp.dma_start(w_in[:, c, 0:3 * D], wqkv[c * P:(c + 1) * P, :]).then_inc(s_w_in[c], 16)
                sp.dma_start(own_weights[2][1], wout.rearrange("(c p) n -> p c n", p=P)).then_inc(s_w_in[2], 16)
                sp.dma_start(own_weights[3][1], wg.rearrange("(c p) n -> p c n", p=P)).then_inc(s_w_in[3], 16)
                sp.dma_start(sel[:], part_sel).then_inc(s_bias_in, 16)
                sp.dma_start(brow[:], biases).then_inc(s_bias_in, 16)
                load_positions(0, 1)
                for dst, src in ((iota_e[:], iota8), (base[:, 0, :], region_base), (b1_col[:], b1)):
                    sp.dma_start(dst, src).then_inc(s_small, 16)
                store_h(0, 0)
                load_weights(0, range(WROWS))
                group_turns(sp, step)
                sp.wait_ge(s_small, 3 * 16)
                sp.wait_ge(s_qk_out, GROUPS * 12 * 16)
                sp.wait_ge(s_v_out, GROUPS * 16)
                for r in two:
                    for u in range(GROUP):
                        sp.wait_ge(s_h_out[r][u], GROUPS // 2 * 16)

            @block.gpsimd
            def _(pool):
                g_ = nc.gpsimd

                def gather(i, r, u):
                    t = (i * 2 + r) * GROUP + u
                    wait(pool, s_emb[r][u], i * 16)
                    g_.tensor_copy(idx_col[:, r, u:u + 1], idx_all[:, bass.ds(t, 1)]).then_inc(s_idx, 1)
                    held(pool, s_passed, (s_idx, t + 1), (s_h_out[r][u], i * 16), (s_xs, t + 1 - 2 * GROUP))
                    g_.indirect_dma_start(h_t[:, r, u, :], None, emb, bass.IndirectOffsetOnAxis(idx_col[:, r, u:u + 1], 0))\
                      .then_inc(s_emb[r][u], 16)

                def inv_std(i, r, u):
                    pool.wait_ge(s_var, (i * 2 + r) * GROUP + u + 1)
                    g_.tensor_tensor(rstd[:, u, 1:2], rstd[:, u, 0:1], minus_half[:], ALU.pow).then_inc(s_rstd, 1)

                def step(i, r):
                    for u in range(GROUP):
                        if not in_last_two(i):
                            gather(i + 1, r, u)
                        if not is_last(i, r):
                            inv_std(*after(i, r), u)

                g_.memset(minus_half[:], -0.5).then_inc(s_zero, 1)
                g_.memset(ident16[:], 0.0).then_inc(s_zero, 1)
                g_.memset(ident32[:], 0.0).then_inc(s_zero, 1)
                g_.memset(before[:], 0.0).then_inc(s_zero, 1)
                pool.wait_ge(s_idx_in, 16)
                for u in range(GROUP):
                    gather(0, 0, u)
                pool.wait_ge(s_zero, 4)
                g_.affine_select(out=ident16[:], in_=ident16[:], compare_op=ALU.not_equal, fill=1.0, base=0,
                                 pattern=[[-1, P]], channel_multiplier=1).then_inc(s_const, 1)
                g_.memset(ones3[:], 1.0).then_inc(s_const, 1)
                g_.memset(ones_g[:], 1.0).then_inc(s_const, 1)
                for u in range(GROUP):
                    inv_std(0, 0, u)
                for u in range(GROUP):
                    gather(0, 1, u)
                g_.affine_select(out=ident32[:], in_=ident32[:], compare_op=ALU.not_equal, fill=1.0, base=0,
                                 pattern=[[-1, P]], channel_multiplier=1).then_inc(s_const, 1)
                g_.affine_select(out=before[:], in_=before[:], compare_op=ALU.is_ge, fill=1.0, base=0,
                                 pattern=[[-1, P]], channel_multiplier=1).then_inc(s_const, 1)
                g_.memset(ones_sq[:], 1.0).then_inc(s_const, 1)
                group_turns(pool, step)
                g_.memset(zero16[:], 0.0).then_inc(s_zero, 1)
                g_.memset(zero32[:], 0.0).then_inc(s_zero, 1)
                pool.wait_ge(s_zero, 6)
                for b in range(B):
                    for blk in (b * (NB + 2), b * (NB + 2) + NB + 1):
                        for a in range(2):
                            pool.dma_start(k_stack[a, :, blk * P:(blk + 1) * P].rearrange("(c p) t -> p c t", p=P),
                                           zero16[:].rearrange("p (c t) -> p c t", c=3)).then_inc(s_pad, 16)
                        pool.dma_start(v_rows[blk * P:(blk + 1) * P, :], zero32[:]).then_inc(s_pad, 16)
                pool.wait_ge(s_pad, 12 * 16)

            @block.scalar
            def _(act):
                a_ = nc.scalar

                def x_hi(i, r):
                    g = i * 2 + r
                    for u in range(GROUP):
                        act.wait_ge(s_xs, g * GROUP + u + 1)
                        wait(act, s_tr, g * 2)
                        a_.copy(x16[:, u, 0, :], pe_xs[:, r, u, :]).then_inc(s_hi, 1)

                def x_copy(i, r):
                    g = i * 2 + r
                    for b in range(2):
                        act.wait_ge(s_tr, g * 2 + b + 1)
                        wait(act, s_v[r], i * 2)
                        a_.copy(xT[:, r, :, b * 2 * P:(b + 1) * 2 * P].rearrange("p c (u t) -> p u c t", u=2),
                                psum16[:, b, :].rearrange("p (u c t) -> p u c t", u=2, c=4)).then_inc(s_xT, 1)

                def qk_hi(g, chunks):
                    for m in chunks:
                        act.wait_ge(s_qk, g * 4 + m + 1)
                        wait(act, s_qk_out, g * (12 * 16))
                        a_.activation(qk16[:, m, 0, :], psum[:, 2 + m, :], ACT.Copy, scale=1.0 / PS).then_inc(s_qk_hi, 1)

                def step(i, r):
                    g = i * 2 + r
                    qk_hi(g, (0, 1))
                    if not is_last(i, r):
                        x_hi(*after(i, r))
                    qk_hi(g, (2, 3))
                    if not is_last(i, r):
                        x_copy(*after(i, r))
                    for w in range(WROWS):
                        act.wait_ge(s_w_in[w], (g + 2) * 16)
                        src, dst = expert_row(g, w)
                        a_.activation(dst(0), src, ACT.Copy, scale=WS).then_inc(s_w_hi[w], 1)
                    for b in range(2):
                        act.wait_ge(s_v[r], i * 2 + b + 1)
                        wait(act, s_v_out, g * 16)
                        a_.activation(v_t[:, b * 2:b * 2 + 2, :, 0:DH],
                                      psum[:, 6 + b, :].rearrange("p (u h d) -> p u h d", u=2, h=H),
                                      ACT.Copy, scale=1.0 / PS).then_inc(s_v_cp, 1)

                for w, src, dst in own_weights:
                    act.wait_ge(s_w_in[w], 16)
                    a_.activation(dst(0), src, ACT.Copy, scale=WS).then_inc(s_w_hi[w], 1)
                act.wait_ge(s_ones, 1)
                x_hi(0, 0)
                x_copy(0, 0)
                group_turns(act, step)

            @block.vector
            def _(dve):
                v_ = nc.vector

                def statistics(i, r):
                    for u in range(GROUP):
                        t = (i * 2 + r) * GROUP + u
                        dve.wait_ge(s_emb[r][u], (i + 1) * 16)
                        dve.wait_ge(s_pe[r][u], (i + 1) * 16)
                        v_.tensor_tensor(h_t[:, r, u, :], h_t[:, r, u, :], pe_xs[:, r, u, :], ALU.add).then_inc(s_h, 1)
                        dve.wait_ge(s_h, t + 1)
                        wait(dve, s_xs, t + 1 - GROUP)
                        v_.bn_stats(stat[:, u, :], h_t[:, r, u, :]).then_inc(s_stat, 1)
                        held(dve, s_passed, (s_stat, t + 1))
                        v_.bn_aggr(mv[:, u, :], stat[:, u, :]).then_inc(s_mv, 1)
                        dve.wait_ge(s_mv, t + 1)
                        v_.tensor_scalar(rstd[:, u, 0:1], mv[:, u, 1:2], EPS, XS ** -2, ALU.add, ALU.mult).then_inc(s_var, 1)

                def normalise(i, r):
                    for u in range(GROUP):
                        dve.wait_ge(s_rstd, (i * 2 + r) * GROUP + u + 1)
                        v_.tensor_scalar(pe_xs[:, r, u, :], h_t[:, r, u, :], mv[:, u, 0:1], rstd[:, u, 1:2],
                                         ALU.subtract, ALU.mult).then_inc(s_xs, 1)
                    for u in range(GROUP):
                        dve.wait_ge(s_hi, (i * 2 + r) * GROUP + u + 1)
                        v_.tensor_tensor(x16[:, u, 1, :], pe_xs[:, r, u, :], x16[:, u, 0, :], ALU.subtract).then_inc(s_lo, 1)

                def low_part(w, src, dst):
                    v_.scalar_tensor_tensor(out=dst(1), in0=src, scalar=WS, in1=dst(0),
                                            op0=ALU.mult, op1=ALU.subtract).then_inc(s_w_lo[w], 1)

                def step(i, r):
                    g = i * 2 + r
                    if not is_last(i, r):
                        statistics(*after(i, r))
                        normalise(*after(i, r))
                    for m in range(4):
                        dve.wait_ge(s_qk_hi, g * 4 + m + 1)
                        v_.scalar_tensor_tensor(out=qk16[:, m, 1, :], in0=psum[:, 2 + m, :], scalar=1.0 / PS,
                                                in1=qk16[:, m, 0, :], op0=ALU.mult, op1=ALU.subtract).then_inc(s_qk_lo, 1)
                    for w in range(WROWS):
                        dve.wait_ge(s_w_hi[w], g + 2)
                        low_part(w, *expert_row(g, w))

                v_.memset(v_t[:, :, :, DH:VW], 1.0 / XS).then_inc(s_ones, 1)
                statistics(0, 0)
                for w, src, dst in own_weights:
                    dve.wait_ge(s_w_hi[w], 1)
                    low_part(w, src, dst)
                normalise(0, 0)
                dve.wait_ge(s_bias_in, 2 * 16)
                split_bias(dve, v_, brow[:], bs3[:], bias3[:], PS, sel, s_bias_step, s_bias)
                group_turns(dve, step)

            @block.tensor
            def _(pe):
                def transpose(i, r):
                    g = i * 2 + r
                    wait(pe, s_xT, g * 2)
                    for u in range(GROUP):
                        pe.wait_ge(s_lo, g * GROUP + u + 1)
                        for c in range(2 * DC):
                            at = ((u % 2) * 4 + c) * P
                            last = nc.tensor.transpose(psum16[:, u // 2, at:at + P],
                                                       x16[:, u, c // DC, (c % DC) * P:(c % DC + 1) * P], ident16[:])
                        if u % 2:
                            last.then_inc(s_tr, 1)

                def step(i, r):
                    g = i * 2 + r
                    pe.wait_ge(s_xT, g * 2 + 2)
                    for m in range(4):
                        wait(pe, s_qk_lo, (g - 1) * 4 + m + 1)
                        ps = psum[:, 2 + m, :]
                        nc.tensor.matmul(ps, bias3[:, OB_QKV + m * P:OB_QKV + (m + 1) * P], ones_g[:], start=True, stop=False)
                        for c in range(DC):
                            for wl, xl in ((0, 0), (0, 1), (1, 0)):
                                last = nc.tensor.matmul(ps, wq16[:, c, wl, m * P:(m + 1) * P], xT[:, r, xl * DC + c, :],
                                                        start=False, stop=(c == DC - 1 and wl == 1))
                        last.then_inc(s_qk, 1)
                    if not is_last(i, r):
                        transpose(*after(i, r))
                    for u in range(GROUP):
                        if u % 2 == 0:
                            wait(pe, s_v_cp, (g - 1) * 2 + u // 2 + 1)
                        ps = psum[:, 6 + u // 2, (u % 2) * D:(u % 2 + 1) * D]
                        nc.tensor.matmul(ps, ones3[:, 0:P], bias3[:, OB_QKV + 2 * D:OB_QKV + 3 * D], start=True, stop=False)
                        for c in range(DC):
                            for wl, xl in ((0, 0), (0, 1), (1, 0)):
                                last = nc.tensor.matmul(ps, xT[:, r, xl * DC + c, u * P:(u + 1) * P], wq16[:, c, wl, 2 * D:3 * D],
                                                        start=False, stop=(c == DC - 1 and wl == 1))
                        if u % 2:
                            last.then_inc(s_v[r], 1)

                pe.wait_ge(s_const, 3)
                transpose(0, 0)
                for w in range(WROWS):
                    pe.wait_ge(s_w_lo[w], 1)
                pe.wait_ge(s_bias, 1)
                group_turns(pe, step)

        shared = Shared(b1_col=b1_col, b2=b2, base=base, before=before, bias3=bias3,
                        h1_rows=h1_rows, h2_rows=h2_rows, ident16=ident16, ident32=ident32, iota_e=iota_e,
                        k_stack=k_stack, mask_tab=mask_tab, minus_half=minus_half, nc=nc, ones3=ones3,
                        ones_sq=ones_sq, out=out, part_col=part_col, pos_all=pos_all, psum=psum,
                        psum16=psum16, q_stack=q_stack, s_passed=s_passed, sem=sem, slot_iota=slot_iota,
                        slot_tab=slot_tab, v_rows=v_rows, valid_row=valid_row, w1_16=w1_16, w2_16=w2_16,
                        w_all=w_all, wg16=wg16, wo16=wo16, x_lists=x_lists, y_pos=y_pos, y_slots=y_slots)
        attend(shared)
        plan(shared)
        experts(shared)
        combine(shared)


class Shared:

    def __init__(self, b1_col, b2, base, before, bias3, h1_rows, h2_rows, ident16, ident32, iota_e,
                 k_stack, mask_tab, minus_half, nc, ones3, ones_sq, out, part_col, pos_all, psum, psum16,
                 q_stack, s_passed, sem, slot_iota, slot_tab, v_rows, valid_row, w1_16, w2_16, w_all, wg16,
                 wo16, x_lists, y_pos, y_slots):
        self.b1_col = b1_col
        self.b2 = b2
        self.base = base
        self.before = before
        self.bias3 = bias3
        self.h1_rows = h1_rows
        self.h2_rows = h2_rows
        self.ident16 = ident16
        self.ident32 = ident32
        self.iota_e = iota_e
        self.k_stack = k_stack
        self.mask_tab = mask_tab
        self.minus_half = minus_half
        self.nc = nc
        self.ones3 = ones3
        self.ones_sq = ones_sq
        self.out = out
        self.part_col = part_col
        self.pos_all = pos_all
        self.psum = psum
        self.psum16 = psum16
        self.q_stack = q_stack
        self.s_passed = s_passed
        self.sem = sem
        self.slot_iota = slot_iota
        self.slot_tab = slot_tab
        self.v_rows = v_rows
        self.valid_row = valid_row
        self.w1_16 = w1_16
        self.w2_16 = w2_16
        self.w_all = w_all
        self.wg16 = wg16
        self.wo16 = wo16
        self.x_lists = x_lists
        self.y_pos = y_pos
        self.y_slots = y_slots


def split_bias(dve, v_, row, tmp, out3, scale, sel, step, done):
    n = 0

    def then(ins, last=False):
        nonlocal n
        if last:
            ins.then_inc(done, 1)
            return
        ins.then_inc(step, 1)
        n += 1
        dve.wait_ge(step, n)

    then(v_.tensor_scalar(row, row, scale, None, ALU.mult))
    then(v_.tensor_copy(tmp, row))
    then(v_.tensor_scalar(out3, tmp, sel[:, 0:1], None, ALU.mult))
    then(v_.tensor_tensor(row, row, tmp, ALU.subtract))
    then(v_.tensor_copy(tmp, row))
    then(v_.scalar_tensor_tensor(out=out3, in0=tmp, scalar=sel[:, 1:2], in1=out3, op0=ALU.mult, op1=ALU.add))
    then(v_.tensor_tensor(row, row, tmp, ALU.subtract))
    then(v_.tensor_copy(tmp, row))
    then(v_.scalar_tensor_tensor(out=out3, in0=tmp, scalar=sel[:, 2:3], in1=out3, op0=ALU.mult, op1=ALU.add), last=True)


def held(eng, s_passed, *waits):
    for sem, v in waits:
        wait(eng, sem, v)
    eng.sem_inc(s_passed, 1)


def wait(eng, semaphore, value):
    if not isinstance(value, int) or value > 0:
        eng.wait_ge(semaphore, value)


def turns(eng, count, turn):
    turn(0)
    with eng.Fori(1, count) as i:
        turn(i)


ROUTE_STEPS = 16


def attend(k):
    nc, sem, psum, psum16 = k.nc, k.sem, k.psum, k.psum16
    ident16, ident32, bias3, ones3 = k.ident16, k.ident32, k.bias3, k.ones3
    with ExitStack() as ph:
        def sb(name, shape, dt):
            return ph.enter_context(nc.sbuf_tensor(name, shape, dt))

        RING = 4
        ks = sb("ks", [P, RING, PAIRS, 3 * P], F16)
        qz = sb("qz", [P, RING, PAIRS, 2, P], F16)
        vs = sb("vs", [P, 2, 3, H, VW], F32)
        masks = sb("masks", [P, 2, 3 * P], BF16)
        h1 = sb("h1", [P, 2, D], F32)
        mx = sb("mx", [P, 2, H], F32)
        mT = sb("mT", [H, P], F16)
        junk = sb("junk", [P, 3 * P], BF16)
        probs = sb("probs", [P, 4, 3, 2, P], F32)
        oT = sb("oT", [P, 4 * P], F32)
        rcp = sb("rcp", [P, H, 1], F32)
        a16 = sb("a16", [P, 2, D], F16)
        h2 = sb("h2", [P, D], F32)
        stat = sb("stat2", [P, 6], F32)
        mv = sb("mv2", [P, 2], F32)
        rstd = sb("rstd2", [P, 2], F32)
        xs2 = sb("xs2", [P, D], F32)
        x16 = sb("x16_2", [P, 2, 2 * D], F16)
        actT = sb("actT", [P, 2 * DC, P], F16)
        g8 = sb("g8", [P, 12, E], F32)
        gs = sb("gs", [P, 8], F32)
        gi = sb("gi", [P, 8], U32)
        member = sb("member", [P, E], BF16)
        pos_t = sb("pos_t", [P, 2, TOPK], I32)

        s_zero = sem("q_zeroed")
        s_stack = [sem(f"stacks_loaded{u}") for u in range(RING)]
        s_mask = [sem(f"mask_loaded{r}") for r in range(2)]
        s_vl = [sem(f"values_loaded{r}") for r in range(2)]
        s_h1 = [sem(f"h1_loaded{r}") for r in range(2)]
        s_sc, s_max = sem("scores_made"), sem("row_max_taken")
        s_mtr, s_mT = sem("max_transposed"), sem("max_negated")
        s_mrow = [sem(f"max_row_placed{u}") for u in range(RING)]
        s_pt, s_exp, s_sel, s_pv = sem("scores_T_made"), sem("exp_made"), sem("probs_masked"), sem("values_summed")
        s_oT, s_otr = sem("outputs_copied"), sem("outputs_transposed")
        s_rcp, s_att, s_ahi, s_alo = sem("sums_inverted"), sem("outputs_normalised"), sem("outputs_hi"), sem("outputs_lo")
        s_atr, s_aT, s_wo = sem("att_transposed"), sem("aT_copied"), sem("att_projected")
        s_h2 = sem("h2_added")
        s_h2o = sem("h2_stored")
        s_ln = sem("ln2_steps")
        s_var, s_rstd = sem("ln2_variance"), sem("ln2_inv_std")
        s_xlo, s_xtr, s_x2T, s_gate = sem("x2_split"), sem("x2_transposed"), sem("x2T_copied"), sem("gate_logits")
        s_gm, s_ge = sem("gate_max_negated"), sem("gate_exp")
        s_rt = sem("route_steps")
        s_mem, s_rank, s_pos = sem("members_marked"), sem("ranks_made"), sem("positions_made")
        s_sc1 = [sem(f"rows_scattered{r}") for r in range(2)]
        s_po = sem("output_bank_zeroed")

        block = ph.enter_context(nc.Block())

        def ahead(i, u, n):
            return i + (u + n) // RING, (u + n) % RING

        def over_tiles(eng, step):
            for u in range(RING):
                step(0, u, u)
            with eng.Fori(1, TILES // RING - 1) as i:
                for u in range(RING):
                    step(i, u, i * RING + u)
            for u in range(RING):
                step(TILES // RING - 1, u, TILES - RING + u)

        def known(t, n):
            return not isinstance(t, int) or 0 <= t + n < TILES

        def flat_pt(p):
            return psum[:].rearrange("p b n -> p (b n)")[:, (2 + 2 * (p % 2)) * 512:(2 + 2 * (p % 2)) * 512 + 3 * 2 * P]

        @block.sync
        def _(sp):
            def load(i, u):
                t = i * RING + u
                wait(sp, s_pv, (t - RING) * PAIRS + PAIRS)
                at = t * P + (t // NB) * 2 * P
                for a in range(2):
                    sp.dma_start(ks[a * 64:a * 64 + 48, u, :, :],
                                 k.k_stack[a, :, bass.ds(at, 3 * P)].rearrange("(r p) t -> r p t", p=PAIRS)).then_inc(s_stack[u], 16)
                    sp.dma_start(qz[a * 64:a * 64 + 48, u, :, a, :],
                                 k.q_stack[a, :, bass.ds(t * P, P)].rearrange("(r p) t -> r p t", p=PAIRS)).then_inc(s_stack[u], 16)
                sp.dma_start(ks[ONES_ROW:ONES_ROW + 1, u, :, :],
                             k.valid_row[:, :, bass.ds(at, 3 * P)]).then_inc(s_stack[u], 16)

            def load_mask(i, u):
                t = i * RING + u
                r = u % 2
                wait(sp, s_max, (t - 1) * H)
                sp.dma_start(masks[:, r, :], k.mask_tab[bass.ds(t * P, P), :].bitcast(BF16)).then_inc(s_mask[r], 16)

            def load_values(i, u):
                t = i * RING + u
                r = u % 2
                at = t * P + (t // NB) * 2 * P
                wait(sp, s_pv, (t - 1) * PAIRS)
                sp.dma_start(vs[:, r, :, :, :].rearrange("p j h w -> p j (h w)"),
                             k.v_rows[bass.ds(at, 3 * P), :].rearrange("(j p) n -> p j n", p=P)).then_inc(s_vl[r], 16)

            def load_residual(i, u):
                t = i * RING + u
                r = u % 2
                wait(sp, s_h2, t - 1)
                sp.dma_start(h1[:, r, :], k.h1_rows[bass.ds(t * P, P), :]).then_inc(s_h1[r], 16)

            def max_row(i, u):
                t = i * RING + u
                wait(sp, s_mT, t + 1)
                sp.dma_start(qz[ONES_ROW:ONES_ROW + 1, u, :, :, :].rearrange("o p a t -> o (p a) t"),
                             mT[:]).then_inc(s_mrow[u], 16)

            def store(i, u):
                t = i * RING + u
                wait(sp, s_h2, t + 1)
                sp.dma_start(k.h2_rows[bass.ds(t * P, P), :], h2[:]).then_inc(s_h2o, 16)

            def body(i, u, t):
                if known(t, 3):
                    load(*ahead(i, u, 3))
                    load_mask(*ahead(i, u, 3))
                load_residual(i, u)
                if known(t, 1):
                    load_values(*ahead(i, u, 1))
                if known(t, -2):
                    store(*ahead(i, u, -2))
                if known(t, 2):
                    max_row(*ahead(i, u, 2))

            sp.wait_ge(s_zero, 2)
            for t in range(3):
                load(0, t)
                load_mask(0, t) if t < 2 else None
            load_values(0, 0)
            for t in range(2):
                max_row(0, t)
            load_mask(0, 2)
            over_tiles(sp, body)
            for u in (RING - 2, RING - 1):
                store(TILES // RING - 1, u)
            sp.wait_ge(s_h2o, TILES * 16)

        @block.gpsimd
        def _(pool):
            g_ = nc.gpsimd
            g_.memset(qz[:], 0.0).then_inc(s_zero, 1)
            g_.memset(ks[:], 0.0).then_inc(s_zero, 1)

            def inv_std(t):
                wait(pool, s_var, t + 1)
                g_.tensor_tensor(rstd[:, 1:2], rstd[:, 0:1], k.minus_half[:], ALU.pow).then_inc(s_rstd, 1)

            def scatter(i, u, t):
                held(pool, k.s_passed, (s_pos, t + 1))
                for c in range(TOPK):
                    g_.indirect_dma_start(k.x_lists, bass.IndirectOffsetOnAxis(pos_t[:, u % 2, c:c + 1], 0), x16[:, u % 2, :], None)\
                      .then_inc(s_sc1[u % 2], 16)

            def body(i, u, t):
                for p in range(PAIRS):
                    held(pool, k.s_passed, (s_exp, t * PAIRS + p + 1))
                    pr = probs[:, p % 4, :, :, :]
                    g_.affine_select(out=pr[:, 0, :, :], in_=pr[:, 0, :, :], compare_op=ALU.is_ge, fill=0.0, base=0,
                                     pattern=[[0, 2], [-1, P]], channel_multiplier=1).then_inc(s_sel, 1)
                    g_.affine_select(out=pr[:, 2, :, :], in_=pr[:, 2, :, :], compare_op=ALU.is_ge, fill=0.0, base=0,
                                     pattern=[[0, 2], [1, P]], channel_multiplier=-1).then_inc(s_sel, 1)
                    if p == 5 and known(t, -2):
                        scatter(*ahead(i, u, -2), t - 2)
                if known(t, -1):
                    inv_std(t - 1)

            over_tiles(pool, body)
            last = TILES // RING - 1
            scatter(last, RING - 2, TILES - 2)
            inv_std(TILES - 1)
            scatter(last, RING - 1, TILES - 1)
            for r in range(2):
                pool.wait_ge(s_sc1[r], TILES // 2 * TOPK * 16)

        @block.scalar
        def _(act):
            a_ = nc.scalar

            def out_copy(t):
                wait(act, s_pv, t * PAIRS + PAIRS)
                wait(act, s_otr, t)
                a_.copy(oT[:], psum[:, 6, :]).then_inc(s_oT, 1)

            def att_copy(t):
                wait(act, s_atr, t + 1)
                a_.copy(actT[:].rearrange("p c t -> p (c t)"), psum16[:, 7, 0:4 * P]).then_inc(s_aT, 1)

            def x_copy(t):
                wait(act, s_xtr, t + 1)
                a_.copy(actT[:].rearrange("p c t -> p (c t)"), psum16[:, 7, 0:4 * P]).then_inc(s_x2T, 1)

            def gate_exp(t):
                wait(act, s_gm, t + 1)
                wait(act, s_rt, t * ROUTE_STEPS)
                a_.activation(g8[:, 1, :], psum[:, 7, 0:E], ACT.Exp, bias=gs[:, 0:1], scale=1.0 / PS,
                              accum_out=gs[:, 1:2]).then_inc(s_ge, 1)

            def body(i, u, t):
                for p in range(PAIRS):
                    wait(act, s_pt, t * PAIRS + p + 1)
                    wait(act, s_pv, t * PAIRS + p - 3)
                    a_.activation(probs[:, p % 4, :, :, :].rearrange("p j a t -> p (j a t)"),
                                  flat_pt(p), ACT.Exp, scale=SCALE).then_inc(s_exp, 1)
                    if p == 1:
                        if known(t, -1):
                            out_copy(t - 1)
                        if known(t, -2):
                            x_copy(t - 2)
                    if p == 3 and known(t, -2):
                        gate_exp(t - 2)
                    if p == 6 and known(t, -1):
                        att_copy(t - 1)

            over_tiles(act, body)
            out_copy(TILES - 1)
            x_copy(TILES - 2)
            gate_exp(TILES - 2)
            att_copy(TILES - 1)
            x_copy(TILES - 1)
            gate_exp(TILES - 1)

        @block.vector
        def _(dve):
            v_ = nc.vector
            v_.memset(psum[:, 6, :], 0.0).then_inc(s_po, 1)

            def maxima(i, u, t, s):
                r = u % 2
                if s == 0:
                    wait(dve, s_mask[r], (i * 2 + u // 2 + 1) * 16)
                    wait(dve, s_mtr, t - 1)
                held(dve, k.s_passed, (s_sc, t * H + s + 1), (s_max, t * H + s))
                v_.tensor_tensor_reduce(out=junk[:], in0=psum[:, s % 2, 0:3 * P], in1=masks[:, r, :], scale=1.0,
                                        scalar=-3.0e38, op0=ALU.add, op1=ALU.max, accum_out=mx[:, r, s:s + 1]).then_inc(s_max, 1)

            def negate_max(t):
                wait(dve, s_mtr, t + 1)
                v_.tensor_scalar(mT[:], psum[0:H, 0, 0:P], -1.0, -60000.0, ALU.mult, ALU.max).then_inc(s_mT, 1)

            def normalise(t):
                wait(dve, s_otr, t + 1)
                wait(dve, s_alo, t)
                bank = psum[:, 7, :]
                v_.reciprocal(rcp[:], bank.rearrange("p (s w) -> p s w", w=32)[:, :, DH:VW]).then_inc(s_rcp, 1)
                wait(dve, s_rcp, t + 1)
                v_.tensor_tensor(xs2[:].rearrange("p (a q d) -> p q a d", a=2, d=DH),
                                 bank.rearrange("p (q a w) -> p q a w", a=2, w=32)[:, :, :, 0:DH],
                                 rcp[:].rearrange("p (q a) o -> p q a o", a=2).to_broadcast([P, PAIRS, 2, DH]),
                                 ALU.mult).then_inc(s_att, 1)
                wait(dve, s_att, t + 1)
                v_.tensor_copy(a16[:, 0, :], xs2[:]).then_inc(s_ahi, 1)
                wait(dve, s_ahi, t + 1)
                v_.tensor_tensor(a16[:, 1, :], xs2[:], a16[:, 0, :], ALU.subtract).then_inc(s_alo, 1)

            def residual(i, u, t):
                r = u % 2
                n = i * 2 + u // 2
                wait(dve, s_wo, t + 1)
                wait(dve, s_xlo, t)
                wait(dve, s_h1[r], (n + 1) * 16)
                wait(dve, s_h2o, t * 16)
                v_.scalar_tensor_tensor(out=h2[:], in0=psum[:, 7, 0:D], scalar=1.0 / PS, in1=h1[:, r, :],
                                        op0=ALU.mult, op1=ALU.add).then_inc(s_h2, 1)
                wait(dve, s_h2, t + 1)
                v_.bn_stats(stat[:], h2[:]).then_inc(s_ln, 1)
                held(dve, k.s_passed, (s_ln, t * 4 + 1))
                v_.bn_aggr(mv[:], stat[:]).then_inc(s_ln, 1)
                wait(dve, s_ln, t * 4 + 2)
                v_.tensor_scalar(rstd[:, 0:1], mv[:, 1:2], EPS, XS ** -2, ALU.add, ALU.mult).then_inc(s_var, 1)

            def norm2(i, u, t):
                r = u % 2
                n = i * 2 + u // 2
                wait(dve, s_rstd, t + 1)
                v_.tensor_scalar(xs2[:], h2[:], mv[:, 0:1], rstd[:, 1:2], ALU.subtract, ALU.mult).then_inc(s_ln, 1)
                wait(dve, s_ln, t * 4 + 3)
                wait(dve, s_sc1[r], n * TOPK * 16)
                v_.tensor_copy(x16[:, r, 0:D], xs2[:]).then_inc(s_ln, 1)
                wait(dve, s_ln, t * 4 + 4)
                v_.tensor_tensor(x16[:, r, D:2 * D], xs2[:], x16[:, r, 0:D], ALU.subtract).then_inc(s_xlo, 1)

            def gate_max(t):
                held(dve, k.s_passed, (s_gate, t + 1))
                v_.max(g8[:, 0, :], psum[:, 7, 0:E]).then_inc(s_rt, 1)
                wait(dve, s_rt, t * ROUTE_STEPS + 1)
                wait(dve, s_ge, t)
                v_.tensor_scalar(gs[:, 0:1], g8[:, 0, 0:1], -1.0 / PS, None, ALU.mult).then_inc(s_gm, 1)

            def route(t):
                step = [1]

                def then(ins):
                    ins.then_inc(s_rt, 1)
                    step[0] += 1
                    held(dve, k.s_passed, (s_rt, t * ROUTE_STEPS + step[0]))

                wait(dve, s_ge, t + 1)
                then(v_.reciprocal(gs[:, 2:3], gs[:, 1:2]))
                then(v_.tensor_scalar(g8[:, 2, :], g8[:, 1, :], gs[:, 2:3], None, ALU.mult))
                then(v_.max(g8[:, 3, :], g8[:, 2, :]))
                then(v_.max_index(gi[:], g8[:, 3, :], g8[:, 2, :]))
                then(v_.tensor_copy(g8[:, 4, :], gi[:]))
                then(v_.tensor_scalar(g8[:, 5, :], k.iota_e[:], g8[:, 4, 0:1], None, ALU.is_equal))
                then(v_.tensor_scalar(g8[:, 6, :], k.iota_e[:], g8[:, 4, 1:2], None, ALU.is_equal))
                then(v_.scalar_tensor_tensor(out=gs[:, 3:4], in0=g8[:, 3, 0:1], scalar=1e-8, in1=g8[:, 3, 1:2],
                                             op0=ALU.add, op1=ALU.add))
                then(v_.reciprocal(gs[:, 4:5], gs[:, 3:4]))
                then(v_.tensor_scalar(k.w_all[:, bass.ds(t * TOPK, TOPK)], g8[:, 3, 0:TOPK], gs[:, 4:5], None, ALU.mult))
                wait(dve, s_rank, t)
                v_.tensor_tensor(member[:], g8[:, 5, :], g8[:, 6, :], ALU.add).then_inc(s_mem, 1)
                return step

            def place(i, u, t):
                step = [11]

                def then(ins):
                    ins.then_inc(s_rt, 1)
                    step[0] += 1
                    wait(dve, s_rt, t * ROUTE_STEPS + step[0])

                r, n = u % 2, i * 2 + u // 2
                wait(dve, s_rank, t + 1)
                wait(dve, s_pos, t)
                then(v_.tensor_tensor(g8[:, 7, :], psum[:, 7, 16:16 + E], k.base[:, r, :], ALU.add))
                then(v_.tensor_tensor(k.base[:, 1 - r, :], psum[:, 7, 16 + E:16 + 2 * E], k.base[:, r, :], ALU.add))
                for c in range(TOPK):
                    then(v_.tensor_tensor_reduce(out=g8[:, 8 + c, :], in0=g8[:, 5 + c, :], in1=g8[:, 7, :], scale=1.0, scalar=0.0,
                                                 op0=ALU.mult, op1=ALU.add, accum_out=g8[:, 10, c:c + 1]))
                then(v_.tensor_copy(k.pos_all[:, bass.ds(t * TOPK, TOPK)], g8[:, 10, 0:TOPK]))
                wait(dve, s_sc1[r], n * TOPK * 16)
                v_.tensor_copy(pos_t[:, r, :], g8[:, 10, 0:TOPK]).then_inc(s_pos, 1)
                assert step[0] == ROUTE_STEPS

            for t in range(2):
                for s in range(H):
                    maxima(0, t, t, s)
                if t:
                    wait(dve, s_mrow[t - 1], 16)
                negate_max(t)

            def step(i, u, t):
                j, w = ahead(i, u, 1)
                for p in range(PAIRS):
                    if known(t, 2):
                        for s in (2 * p, 2 * p + 1):
                            maxima(*ahead(i, u, 2), t + 2, s)
                    if known(t, -2):
                        if p == 0:
                            norm2(*ahead(i, u, -2), t - 2)
                        if p == 2:
                            gate_max(t - 2)
                        if p == 3:
                            route(t - 2)
                        if p == 4:
                            place(*ahead(i, u, -2), t - 2)
                    if p == 5 and known(t, -1):
                        normalise(t - 1)
                if known(t, 2):
                    wait(dve, s_mrow[w], (j + 1) * 16)
                    negate_max(t + 2)
                if known(t, -1):
                    residual(*ahead(i, u, -1), t - 1)

            over_tiles(dve, step)
            last = TILES // RING - 1
            norm2(last, RING - 2, TILES - 2)
            gate_max(TILES - 2)
            route(TILES - 2)
            place(last, RING - 2, TILES - 2)
            normalise(TILES - 1)
            residual(last, RING - 1, TILES - 1)
            norm2(last, RING - 1, TILES - 1)
            gate_max(TILES - 1)
            route(TILES - 1)
            place(last, RING - 1, TILES - 1)

        @block.tensor
        def _(pe):
            def scores(i, u, t, s):
                p, a = s // 2, s % 2
                if s == 0:
                    wait(pe, s_stack[u], (i + 1) * 5 * 16)
                    wait(pe, s_mT, t)
                wait(pe, s_max, t * H + s - 1)
                nc.tensor.matmul(psum[:, s % 2, 0:3 * P], qz[0:ONES_ROW, u, p, a, :], ks[0:ONES_ROW, u, p, :],
                                 start=True, stop=True).then_inc(s_sc, 1)

            def max_transpose(u, t):
                wait(pe, s_max, t * H + H)
                nc.tensor.transpose(psum[0:H, 0, 0:P], mx[:, u % 2, :], ident32[:]).then_inc(s_mtr, 1)

            def scores_t(i, u, t, p):
                if p == 0:
                    wait(pe, s_mrow[u], (i + 1) * 16)
                wait(pe, s_exp, t * PAIRS + p - 1)
                for j in range(3):
                    at = (2 + 2 * (p % 2)) * 512 + j * 2 * P
                    last = nc.tensor.matmul(psum[:, at // 512, at % 512:at % 512 + 2 * P], ks[0:ONES_ROW + 1, u, p, j * P:(j + 1) * P],
                                            qz[0:ONES_ROW + 1, u, p, :, :], start=True, stop=True)
                last.then_inc(s_pt, 1)

            def values(i, u, t, p):
                if p == 0:
                    wait(pe, s_vl[u % 2], (i * 2 + u // 2 + 1) * 16)
                    wait(pe, s_oT, t)
                wait(pe, s_sel, (t * PAIRS + p + 1) * 2)
                for j in range(3):
                    for a in range(2):
                        s = 2 * p + a
                        last = nc.tensor.matmul(psum[32 * (s % 4):32 * (s % 4) + VW, 6, (s // 4) * P:(s // 4 + 1) * P],
                                                vs[:, u % 2, j, a * PAIRS + p, :], probs[:, p % 4, j, a, :],
                                                start=(j == 0), stop=(j == 2), skip_group_check=True)
                last.then_inc(s_pv, 1)

            def out_transpose(t):
                wait(pe, s_oT, t + 1)
                wait(pe, s_rt, t * ROUTE_STEPS)
                for b in range(4):
                    last = nc.tensor.transpose(psum[:, 7, b * P:(b + 1) * P], oT[:, b * P:(b + 1) * P], ident32[:])
                last.then_inc(s_otr, 1)

            def att_transpose(t):
                wait(pe, s_alo, t + 1)
                for c in range(2 * DC):
                    last = nc.tensor.transpose(psum16[:, 7, c * P:(c + 1) * P], a16[:, c // DC, (c % DC) * P:(c % DC + 1) * P], ident16[:])
                last.then_inc(s_atr, 1)

            def three_pass(ps, left, right, bias_l, bias_r):
                nc.tensor.matmul(ps, bias_l, bias_r, start=True, stop=False)
                for c in range(DC):
                    for wl, xl in ((0, 0), (0, 1), (1, 0)):
                        last = nc.tensor.matmul(ps, left[:, xl * DC + c, :], right[:, c, wl, :],
                                                start=False, stop=(c == DC - 1 and wl == 1))
                return last

            def project(t):
                wait(pe, s_aT, t + 1)
                three_pass(psum[:, 7, 0:D], actT, k.wo16, ones3[:, 0:P], bias3[:, OB_OUT:OB_OUT + D]).then_inc(s_wo, 1)

            def x_transpose(u, t):
                wait(pe, s_xlo, t + 1)
                for c in range(2 * DC):
                    last = nc.tensor.transpose(psum16[:, 7, c * P:(c + 1) * P], x16[:, u % 2, c * P:(c + 1) * P], ident16[:])
                last.then_inc(s_xtr, 1)

            def gate(t):
                wait(pe, s_x2T, t + 1)
                three_pass(psum[:, 7, 0:E], actT, k.wg16, ones3[:, 0:P], bias3[:, OB_G:OB_G + E]).then_inc(s_gate, 1)

            def rank(t):
                wait(pe, s_mem, t + 1)
                nc.tensor.matmul(psum[:, 7, 16:16 + E], k.before[:], member[:], start=True, stop=True)
                nc.tensor.matmul(psum[:, 7, 16 + E:16 + 2 * E], k.ones_sq[:], member[:], start=True, stop=True).then_inc(s_rank, 1)

            pe.wait_ge(s_po, 1)
            for t in range(2):
                for s in range(H):
                    scores(0, t, t, s)
                max_transpose(t, t)

            def step(i, u, t):
                for p in range(PAIRS):
                    if known(t, 2):
                        for s in (2 * p, 2 * p + 1):
                            scores(*ahead(i, u, 2), t + 2, s)
                    scores_t(i, u, t, p)
                    if known(t, -2):
                        if p == 1:
                            x_transpose(u, t - 2)
                        if p == 2:
                            gate(t - 2)
                        if p == 4:
                            rank(t - 2)
                    if p == 5 and known(t, -1):
                        out_transpose(t - 1)
                    if p >= 2:
                        values(i, u, t, p - 2)
                    elif known(t, -1):
                        values(*ahead(i, u, -1), t - 1, p + PAIRS - 2)
                    if known(t, -1):
                        if p == 6:
                            att_transpose(t - 1)
                        if p == 7:
                            project(t - 1)
                if known(t, 2):
                    max_transpose(u, t + 2)

            over_tiles(pe, step)
            last = TILES // RING - 1
            values(last, RING - 1, TILES - 1, PAIRS - 2)
            values(last, RING - 1, TILES - 1, PAIRS - 1)
            x_transpose(RING - 2, TILES - 2)
            gate(TILES - 2)
            rank(TILES - 2)
            out_transpose(TILES - 1)
            att_transpose(TILES - 1)
            project(TILES - 1)
            x_transpose(RING - 1, TILES - 1)
            gate(TILES - 1)
            rank(TILES - 1)


def slot_table(dve, k, s_step, s_tail, s_in, pcol, tail, sl, sg, se, si, move):
    v_ = k.nc.vector
    n = SLOTS_RUN
    step = [0]

    def then(ins):
        ins.then_inc(s_step, 1)
        step[0] += 1
        dve.wait_ge(s_step, step[0])

    dve.wait_ge(s_in, 2 * 16)
    final = k.base[:, 0, :]
    v_.tensor_scalar(tail[:], final, pcol[:, 0:1], None, ALU.add).then_inc(s_tail, 1)
    up, rest, tiles, ends = (se[:, j, :] for j in range(4))
    iota, slot, exp_, skipped, row = (sl[0:1, j, :] for j in range(5))
    ends_0, tiles_0 = ends[0:1, :], tiles[0:1, :]
    then(v_.scalar_tensor_tensor(out=up, in0=k.iota_e[:], scalar=-float(REGION), in1=final,
                                 op0=ALU.mult, op1=ALU.add))
    then(v_.tensor_scalar(up, up, float(P - 1), None, ALU.add))
    then(v_.tensor_copy(si[:, 0, :], up))
    then(v_.tensor_scalar(si[:, 1, :], si[:, 0, :], P.bit_length() - 1, None, ALU.arith_shift_right))
    then(v_.tensor_copy(tiles, si[:, 1, :]))
    then(v_.tensor_copy(ends[:, 0:1], tiles[:, 0:1]))
    for e in range(1, E):
        then(v_.tensor_tensor(ends[:, e:e + 1], ends[:, e - 1:e], tiles[:, e:e + 1], ALU.add))
    then(v_.tensor_scalar(rest[:, 0:1], ends[:, E - 1:E], -1.0, None, ALU.add))
    then(v_.tensor_scalar(slot, iota, rest[0:1, 0:1], None, ALU.min))
    then(v_.tensor_tensor(sg[:, 0, :, :], slot.unsqueeze(2).to_broadcast([1, n, E]), ends_0.unsqueeze(1).to_broadcast([1, n, E]), ALU.is_ge))
    then(v_.tensor_tensor(sg[:, 1, :, :], sg[:, 0, :, :], tiles_0.unsqueeze(1).to_broadcast([1, n, E]), ALU.mult))
    then(v_.tensor_reduce(exp_, sg[:, 0, :, :], AX_X, ALU.add))
    then(v_.tensor_reduce(skipped, sg[:, 1, :, :], AX_X, ALU.add))
    then(v_.tensor_tensor(row, slot, skipped, ALU.subtract))
    then(v_.tensor_scalar(row, row, float(P), None, ALU.mult))
    then(v_.scalar_tensor_tensor(out=row, in0=exp_, scalar=float(REGION), in1=row, op0=ALU.mult, op1=ALU.add))
    then(v_.tensor_copy(k.slot_tab[:, 0, :], exp_))
    then(v_.tensor_copy(k.slot_tab[:, 1, :], row))
    gap = up
    then(v_.tensor_scalar(gap, tiles, float(P), -float(REGION), ALU.mult, ALU.add))
    for e in range(1, E):
        then(v_.tensor_scalar(move[:, 0, :], k.pos_all[:], float(e * REGION), gap[:, e - 1:e], ALU.is_ge, ALU.mult))
        then(v_.tensor_tensor(move[:, 1 + e % 2, :], move[:, 0, :], k.pos_all[:] if e == 1 else move[:, 1 + (e - 1) % 2, :], ALU.add))
    then(v_.tensor_copy(k.y_pos[:], move[:, 1 + (E - 1) % 2, :]))


def plan(k):
    nc, sem = k.nc, k.sem
    with ExitStack() as ph:
        def sb(name, shape, dt):
            return ph.enter_context(nc.sbuf_tensor(name, shape, dt))

        tail = sb("tail", [P, E], I32)
        pcol = sb("pcol", [P, 1], F32)
        zrow = sb("zrow", [P, 2 * D], F16)
        sl = sb("sl", [1, 5, SLOTS_RUN], F32)
        move = sb("move", [P, 3, TILES * TOPK], F32)
        sg = sb("sg", [1, 2, SLOTS_RUN, E], F32)
        se = sb("se", [P, 4, E], F32)
        si = sb("si", [P, 2, E], I32)
        s_in, s_zrow = sem("plan_constants_loaded"), sem("zero_row_made")
        s_tail, s_tail_out = sem("tail_rows_made"), sem("tails_zeroed")
        s_tab = sem("slot_table_steps")
        block = ph.enter_context(nc.Block())

        @block.sync
        def _(sp):
            sp.dma_start(pcol[:], k.part_col).then_inc(s_in, 16)
            sp.dma_start(sl[0:1, 0, :], k.slot_iota).then_inc(s_in, 16)

        @block.vector
        def _(dve):
            slot_table(dve, k, s_tab, s_tail, s_in, pcol, tail, sl, sg, se, si, move)

        @block.gpsimd
        def _(pool):
            nc.gpsimd.memset(zrow[:], 0.0).then_inc(s_zrow, 1)
            pool.wait_ge(s_zrow, 1)
            pool.wait_ge(s_tail, 1)
            for e in range(E):
                nc.gpsimd.indirect_dma_start(k.x_lists, bass.IndirectOffsetOnAxis(tail[:, e:e + 1], 0), zrow[:], None)\
                  .then_inc(s_tail_out, 16)
            pool.wait_ge(s_tail_out, E * 16)


def experts(k):
    nc, sem, psum, psum16 = k.nc, k.sem, k.psum, k.psum16
    with ExitStack() as ph:
        def sb(name, shape, dt):
            return ph.enter_context(nc.sbuf_tensor(name, shape, dt))

        xin = sb("xin", [P, 2, 2 * D], F16)
        xT = sb("xT_e", [P, 2, 2 * DC, P], F16)
        gel = sb("gel", [P, 2, FC, P], F32)
        h16 = sb("h16", [P, 2, 2, FC, P], F16)
        y = sb("y", [P, 2, D], F32)
        b2_all = sb("b2_all", [P, E * D], F32)
        s_b2 = sem("b2_loaded")

        s_x = [sem(f"rows_loaded{u}") for u in range(2)]
        s_tr = [sem(f"rows_transposed{u}") for u in range(2)]
        s_xT = [sem(f"rows_T_copied{u}") for u in range(2)]
        s_h = [sem(f"hidden_made{u}") for u in range(2)]
        s_g = [sem(f"gelu_made{u}") for u in range(2)]
        s_hi, s_lo = [sem(f"hidden_hi{u}") for u in range(2)], [sem(f"hidden_lo{u}") for u in range(2)]
        s_y = [sem(f"y_made{u}") for u in range(2)]
        s_yc = [sem(f"y_copied{u}") for u in range(2)]
        s_yo = [sem(f"y_stored{u}") for u in range(2)]

        block = ph.enter_context(nc.Block())

        def entry(eng, which, s):
            top = (E - 1, (E - 1) * REGION + TOKENS)[which]
            return eng.value_load(k.slot_tab[0:1, which, bass.ds(s, 1)], min_val=0, max_val=top)

        @block.sync
        def _(sp):
            sp.dma_start(b2_all[:], k.b2.to_broadcast([P, E * D])).then_inc(s_b2, 16)

            def turn(i):
                for u in range(2):
                    row = entry(sp, 1, i * 2 + u)
                    wait(sp, s_tr[u], i)
                    sp.dma_start(xin[:, u, :], k.x_lists[bass.ds(row, P), :]).then_inc(s_x[u], 16)

            turns(sp, SLOTS_RUN // 2, turn)

        @block.gpsimd
        def _(pool):

            def turn(i):
                for u in range(2):
                    wait(pool, s_yc[u], i + 1)
                    pool.dma_start(k.y_slots[bass.ds((i * 2 + u) * P, P), :], y[:, u, :]).then_inc(s_yo[u], 16)

            turns(pool, SLOTS_RUN // 2, turn)
            for u in range(2):
                pool.wait_ge(s_yo[u], SLOTS_RUN // 2 * 16)

        @block.scalar
        def _(act):

            def turn(i):
                for u in range(2):
                    e = entry(act, 0, i * 2 + u)
                    wait(act, s_lo[u], i * 2)
                    for f in range(FC):
                        wait(act, s_h[u], i * 2 + f // 4 + 1)
                        nc.scalar.activation(gel[:, u, f, :], psum[:, 2 + 2 * u + f // 4, (f % 4) * P:(f % 4 + 1) * P],
                                             ACT.Gelu_apprx_tanh, bias=k.b1_col[:, bass.ds(e * FC + f, 1)],
                                             scale=1.0 / PS).then_inc(s_g[u], 1)

            turns(act, SLOTS_RUN // 2, turn)

        @block.vector
        def _(dve):
            v_ = nc.vector

            def y_copy(i, u):
                dve.wait_ge(s_y[u], i + 1)
                wait(dve, s_yo[u], i * 16)
                e = entry(dve, 0, i * 2 + u)
                v_.scalar_tensor_tensor(out=y[:, u, :], in0=psum[:, 6 + u, 0:D], scalar=1.0 / YS,
                                        in1=b2_all[:, bass.ds(e * D, D)], op0=ALU.mult, op1=ALU.add).then_inc(s_yc[u], 1)

            def split(i, u):
                for half in range(2):
                    c = slice(half * 4, half * 4 + 4)
                    dve.wait_ge(s_g[u], i * FC + half * 4 + 4)
                    if half == 0:
                        wait(dve, s_y[u], i)
                    v_.tensor_scalar(h16[:, u, 0, c, :], gel[:, u, c, :], HS, None, ALU.mult).then_inc(s_hi[u], 1)
                    dve.wait_ge(s_hi[u], i * 2 + half + 1)
                    v_.scalar_tensor_tensor(out=h16[:, u, 1, c, :], in0=gel[:, u, c, :], scalar=HS, in1=h16[:, u, 0, c, :],
                                            op0=ALU.mult, op1=ALU.subtract).then_inc(s_lo[u], 1)

            def x_copy(i, u):
                dve.wait_ge(s_tr[u], i + 1)
                wait(dve, s_h[u], i * 2)
                v_.tensor_copy(xT[:, u, :, :].rearrange("p c t -> p (c t)"), psum16[:, u, 0:4 * P]).then_inc(s_xT[u], 1)

            dve.wait_ge(s_b2, 16)
            x_copy(0, 0)

            def step(i, u, first, last):
                if not last:
                    x_copy(*((i, 1) if u == 0 else (i + 1, 0)))
                split(i, u)
                if not first:
                    y_copy(*((i, 0) if u == 1 else (i - 1, 1)))

            step(0, 0, True, False)
            step(0, 1, False, False)
            with dve.Fori(1, SLOTS_RUN // 2 - 1) as i:
                step(i, 0, False, False)
                step(i, 1, False, False)
            step(SLOTS_RUN // 2 - 1, 0, False, False)
            step(SLOTS_RUN // 2 - 1, 1, False, True)
            y_copy(SLOTS_RUN // 2 - 1, 1)

        @block.tensor
        def _(pe):
            def transpose(i, u):
                pe.wait_ge(s_x[u], (i + 1) * 16)
                wait(pe, s_xT[u], i)
                for c in range(2 * DC):
                    last = nc.tensor.transpose(psum16[:, u, c * P:(c + 1) * P], xin[:, u, c * P:(c + 1) * P], k.ident16[:])
                last.then_inc(s_tr[u], 1)

            def hidden(i, u, e):
                pe.wait_ge(s_xT[u], i + 1)
                wait(pe, s_g[u], i * FC)
                for f in range(FC):
                    ps = psum[:, 2 + 2 * u + f // 4, (f % 4) * P:(f % 4 + 1) * P]
                    for c in range(DC):
                        for wl, xl in ((0, 0), (0, 1), (1, 0)):
                            last = nc.tensor.matmul(ps, k.w1_16[:, bass.ds(e * (DC * 2 * F) + ((c * 2 + wl) * F + f * P), P)],
                                                    xT[:, u, xl * DC + c, :], start=(c == 0 and wl == 0 and xl == 0),
                                                    stop=(c == DC - 1 and wl == 1))
                    if f % 4 == 3:
                        last.then_inc(s_h[u], 1)

            def outputs(i, u, e):
                wait(pe, s_yc[u], i)
                ps = psum[:, 6 + u, 0:D]
                for f in range(FC):
                    if f % 4 == 0:
                        pe.wait_ge(s_lo[u], i * 2 + f // 4 + 1)
                    for wl, hl in ((0, 0), (0, 1), (1, 0)):
                        last = nc.tensor.matmul(ps, h16[:, u, hl, f, :], k.w2_16[:, bass.ds(e * (FC * 2 * D) + (f * 2 + wl) * D, D)],
                                                start=(f == 0 and wl == 0 and hl == 0), stop=(f == FC - 1 and wl == 1))
                last.then_inc(s_y[u], 1)

            transpose(0, 0)

            def step(i, u, first, last):
                hidden(i, u, entry(pe, 0, i * 2 + u))
                if not last:
                    transpose(*((i, 1) if u == 0 else (i + 1, 0)))
                if not first:
                    outputs(*((i, 0) if u == 1 else (i - 1, 1)), entry(pe, 0, i * 2 + u - 1))

            step(0, 0, True, False)
            step(0, 1, False, False)
            with pe.Fori(1, SLOTS_RUN // 2 - 1) as i:
                step(i, 0, False, False)
                step(i, 1, False, False)
            step(SLOTS_RUN // 2 - 1, 0, False, False)
            step(SLOTS_RUN // 2 - 1, 1, False, True)
            outputs(SLOTS_RUN // 2 - 1, 1, entry(pe, 0, SLOTS_RUN - 1))


def combine(k):
    nc, sem = k.nc, k.sem
    with ExitStack() as ph:
        def sb(name, shape, dt):
            return ph.enter_context(nc.sbuf_tensor(name, shape, dt))

        R = 4
        idx = sb("idx_c", [P, R, TOPK], I32)
        yy = sb("yy", [P, R, TOPK, D], F32)
        h2 = sb("h2_c", [P, R, D], F32)
        o1 = sb("o1", [P, R, D], F32)
        o2 = sb("o2", [P, R, D], F32)
        s_idx = sem("combine_index_copied")
        s_y = [sem(f"expert_rows_gathered{u}") for u in range(R)]
        s_h2 = [sem(f"residual_loaded{u}") for u in range(R)]
        s_o1, s_o2 = sem("first_expert_added"), sem("second_expert_added")
        s_out = [sem(f"output_stored{u}") for u in range(R)]
        block = ph.enter_context(nc.Block())

        @block.gpsimd
        def _(pool):
            g_ = nc.gpsimd

            def turn(i):
                for u in range(R):
                    t = i * R + u
                    wait(pool, s_y[u], i * (TOPK * 16))
                    g_.tensor_copy(idx[:, u, :], k.y_pos[:, bass.ds(t * TOPK, TOPK)]).then_inc(s_idx, 1)
                    held(pool, k.s_passed, (s_idx, t + 1), (s_o2, i * R))
                    for c in range(TOPK):
                        g_.indirect_dma_start(yy[:, u, c, :], None, k.y_slots,
                                              bass.IndirectOffsetOnAxis(idx[:, u, c:c + 1], 0)).then_inc(s_y[u], 16)

            turns(pool, TILES // R, turn)

        @block.sync
        def _(sp):

            def turn(i):
                for u in range(R):
                    wait(sp, s_o1, i * R)
                    sp.dma_start(h2[:, u, :], k.h2_rows[bass.ds((i * R + u) * P, P), :]).then_inc(s_h2[u], 16)

            turns(sp, TILES // R, turn)

        @block.scalar
        def _(act):

            def turn(i):
                for u in range(R):
                    wait(act, s_o2, i * R + u + 1)
                    act.dma_start(k.out[bass.ds((i * R + u) * P, P), :], o2[:, u, :]).then_inc(s_out[u], 16)

            turns(act, TILES // R, turn)
            for u in range(R):
                act.wait_ge(s_out[u], TILES // R * 16)

        @block.vector
        def _(dve):
            v_ = nc.vector

            def turn(i):
                for u in range(R):
                    t = i * R + u
                    wait(dve, s_h2[u], (i + 1) * 16)
                    wait(dve, s_y[u], (i + 1) * (TOPK * 16))
                    wait(dve, s_o2, i * R)
                    v_.scalar_tensor_tensor(out=o1[:, u, :], in0=yy[:, u, 0, :], scalar=k.w_all[:, bass.ds(t * TOPK, 1)],
                                            in1=h2[:, u, :], op0=ALU.mult, op1=ALU.add).then_inc(s_o1, 1)
                    wait(dve, s_o1, t + 1)
                    wait(dve, s_out[u], i * 16)
                    v_.scalar_tensor_tensor(out=o2[:, u, :], in0=yy[:, u, 1, :], scalar=k.w_all[:, bass.ds(t * TOPK + 1, 1)],
                                            in1=o1[:, u, :], op0=ALU.mult, op1=ALU.add).then_inc(s_o2, 1)

            turns(dve, TILES // R, turn)

def position_table(np):
    pos = np.arange(S, dtype=np.float32)
    i = np.arange(D // 2, dtype=np.float32)
    inv = np.power(10000.0, (np.float32(-2.0) * i / np.float32(D)).astype(np.float64)).astype(np.float32)
    ang = pos[:, None] * inv[None, :]
    table = np.stack([np.sin(ang.astype(np.float64)), np.cos(ang.astype(np.float64))], axis=-1)
    return np.tile(table.reshape(S, D).astype(np.float32), (B, 1))


def window_masks(np):
    n = np.arange(NB)[:, None, None]
    i = np.arange(P)[None, :, None]
    j = np.arange(3 * P)[None, None, :]
    key = n * P - P + j
    inside = (np.abs(key - (n * P + i)) <= P) & (key >= 0) & (key < S)
    return np.tile(np.where(inside, 0, NEG_BITS).reshape(NB * P, 3 * P).astype(np.uint16), (B, 1))


def kernel(x, L0_tok_emb_table, L0_attn_Wqkv, L0_attn_bqkv, L0_attn_Wout, L0_attn_bout, L0_ffn_Wg, L0_ffn_bg,
           L0_ffn_W1, L0_ffn_b1, L0_ffn_W2, L0_ffn_b2):
    import numpy as np
    import concourse.bacc as bacc
    from concourse.bass_utils import run_bass_kernel_spmd

    def by_dim(w):
        w = np.asarray(w).reshape(-1, 2, PAIRS, DH)
        return w.transpose(0, 1, 3, 2).reshape(-1, D)

    wqkv = np.asarray(L0_attn_Wqkv)
    bqkv = np.asarray(L0_attn_bqkv).reshape(1, -1)
    lay = lambda w: np.concatenate([by_dim(w[:, 0:D]), by_dim(w[:, D:2 * D]), w[:, 2 * D:]], axis=1)
    row = np.concatenate([lay(bqkv)[0], np.asarray(L0_attn_bout), np.asarray(L0_ffn_bg)])
    valid = np.zeros((BLOCKS, P), np.float16)
    for b in range(B):
        valid[b * (NB + 2) + 1:b * (NB + 2) + 1 + NB] = 1
    arrays = {
        "x_idx": np.asarray(x).reshape(TILES, P).T,
        "emb": np.asarray(L0_tok_emb_table),
        "pe_tab": position_table(np),
        "wqkv": lay(wqkv),
        "wout": np.asarray(L0_attn_Wout),
        "wg": np.asarray(L0_ffn_Wg),
        "w1": np.asarray(L0_ffn_W1).reshape(E * D, F),
        "b1": np.asarray(L0_ffn_b1).reshape(E * FC, P).T,
        "w2": np.asarray(L0_ffn_W2).reshape(E * F, D),
        "b2": np.asarray(L0_ffn_b2).reshape(1, E * D),
        "biases": np.stack([row] * 3),
        "part_sel": np.eye(3, dtype=np.float32),
        "mask_tab": window_masks(np),
        "valid_row": np.tile(valid.reshape(1, 1, -1), (1, PAIRS, 1)),
        "iota8": np.tile(np.arange(E, dtype=np.float32), (P, 1)),
        "slot_iota": np.arange(SLOTS_RUN, dtype=np.float32).reshape(1, -1),
        "region_base": np.tile(np.arange(E, dtype=np.float32) * REGION, (P, 1)),
        "part_col": np.arange(P, dtype=np.float32).reshape(P, 1),
    }
    arrays = {n: np.ascontiguousarray(a) for n, a in arrays.items()}
    nc = bacc.Bacc("TRN2", target_bir_lowering=False, num_devices=1)
    ins = [nc.dram_tensor(n, a.shape, mybir.dt.from_np(a.dtype), kind="ExternalInput").ap() for n, a in arrays.items()]
    out = nc.dram_tensor("out", (TOKENS, D), F32, kind="ExternalOutput").ap()
    build(nc, *ins, out)
    r = run_bass_kernel_spmd(nc, [arrays], core_ids=[0])
    return r.results[0]["out"].reshape(B, S, D)
```

```python
from contextlib import ExitStack

import concourse.bass as bass
from concourse import mybir

F32 = mybir.dt.float32
F16 = mybir.dt.float16
BF16 = mybir.dt.bfloat16
I32 = mybir.dt.int32
U32 = mybir.dt.uint32
ALU = mybir.AluOpType
ACT = mybir.ActivationFunctionType
AX_X = mybir.AxisListType.X

P = 128
B, S, D = 2, 2048, 256
TOKENS = B * S
TILES = TOKENS // P
NB = S // P
DC = D // P
H, DH = 16, 16
PAIRS = H // 2
VW = DH + 1
E, F = 8, 1024
FC = F // P
TOPK = 2
GROUP = 4
GROUPS = TILES // GROUP
GT = GROUP * P
BLOCKS = B * (NB + 2)
PADDED = BLOCKS * P
REGION = TOKENS + P
SLOTS = TOPK * TOKENS // P + E - 1
SLOTS_RUN = SLOTS + SLOTS % 2
EPS = 1e-5
XS = 256.0
WS = 256.0
PS = XS * WS
HS = 16.0
YS = HS * WS
SCALE = 1.0 / D ** 0.5
NEG_BITS = 0xF149
ONES_ROW = 112

XW = D + 4
TOKEN, WEIGHTS, FIRST = D, D + 1, D + 3
OB_QKV, OB_OUT, OB_G, OB_2 = 0, 3 * D, 4 * D, 4 * D + E
KEPT_OUT, KEPT_G = 0, D
WROWS = 4


def build(nc, x_idx, emb, pe_tab, wqkv, wout, wg, w1, b1, w2, b2, biases, part_sel,
          mask_tab, valid_row, iota8, slot_iota, region_base, part_col, token_of, out):
    dram = lambda n, s, d: nc.dram_tensor(n, s, d, kind="Internal").ap()
    q_stack = dram("q_stack", (2, 3 * P, TOKENS), F16)
    k_stack = dram("k_stack", (2, 3 * P, PADDED), F16)
    v_rows = dram("v_rows", (PADDED, H * VW), F32)
    h1_rows = dram("h1_rows", (TOKENS, D), F32)
    x_lists = dram("x_lists", (E * REGION, XW), I32)

    with ExitStack() as top:
        def keep(name, shape, dt):
            return top.enter_context(nc.sbuf_tensor(name, shape, dt))

        def sem(name):
            return top.enter_context(nc.semaphore(name))

        psum = top.enter_context(nc.psum_tensor("psum", [P, 8, 512], F32))
        psum16 = psum[:].bitcast(F16)
        w1_16 = keep("w1_16", [P, E * DC * 2 * F], F16)
        w2_16 = keep("w2_16", [P, E * FC * 2 * D], F16)
        b1_col = keep("b1_col", [P, E * FC], F32)
        wo16 = keep("wo16", [P, DC, 2, D], F16)
        wg16 = keep("wg16", [P, DC, 2, E], F16)
        bias3 = keep("bias3", [3, D + E], BF16)
        ones3 = keep("ones3", [3, P], BF16)
        ident16 = keep("ident16", [P, P], F16)
        ident32 = keep("ident32", [P, P], F32)
        before = keep("before", [P, P], BF16)
        ones_sq = keep("ones_sq", [P, P], BF16)
        minus_half = keep("minus_half", [P, 1], F32)
        iota_e = keep("iota_e", [P, E], F32)
        base = keep("base", [P, 2, E], F32)
        token_no = keep("token_no", [P, TILES], I32)
        slot_expert = keep("slot_expert", [P, SLOTS_RUN], F32)
        slot_tab = keep("slot_tab", [1, 2, SLOTS_RUN], I32)

        s_passed = sem("waits_passed")

        with ExitStack() as ph:
            def sb(name, shape, dt):
                return ph.enter_context(nc.sbuf_tensor(name, shape, dt))

            idx_all = sb("idx_all", [P, TILES], I32)
            idx_col = sb("idx_col", [P, 2, GROUP], I32)
            h_t = sb("h_t", [P, 2, GROUP, D], F32)
            pe_xs = sb("pe_xs", [P, 2, GROUP, D], F32)
            x16 = sb("x16", [P, GROUP, 2, D], F16)
            stat = sb("stat", [P, GROUP, 6], F32)
            mv = sb("mv", [P, GROUP, 2], F32)
            rstd = sb("rstd", [P, GROUP, 2], F32)
            xT = sb("xT", [P, 2, 2 * DC, GT], F16)
            qk16 = sb("qk16", [P, 4, 2, GT], F16)
            v_t = sb("v_t", [P, GROUP, H, VW], F32)
            wq16 = sb("wq16", [P, DC, 2, 3 * D], F16)
            w_in = sb("w_in", [P, WROWS, F], F32)
            all_bias3 = sb("all_bias3", [3, OB_2], BF16)
            brow = sb("brow", [3, OB_2], F32)
            bs3 = sb("bs3", [3, OB_2], BF16)
            sel = sb("sel", [3, 3], F32)
            ones_g = sb("ones_g", [3, GT], BF16)
            zero16 = sb("zero16", [P, 3 * P], F16)
            zero32 = sb("zero32", [P, H * VW], F32)

            two = range(2)
            s_idx_in = sem("indices_loaded")
            s_small = sem("small_loaded")
            s_bias_in = sem("bias_loaded")
            s_bias_step = sem("bias_step")
            s_bias = sem("bias_split")
            s_const = sem("constants_made")
            s_zero = sem("zeros_made")
            s_pad = sem("padding_stored")
            s_idx = sem("index_column_copied")
            s_emb = [[sem(f"embedding_gathered{r}{u}") for u in range(GROUP)] for r in two]
            s_pe = [[sem(f"position_loaded{r}{u}") for u in range(GROUP)] for r in two]
            s_h = sem("h_added")
            s_h_out = [[sem(f"h_stored{r}{u}") for u in range(GROUP)] for r in two]
            s_stat, s_mv, s_var, s_rstd = sem("ln1_stats"), sem("ln1_mean_var"), sem("ln1_variance"), sem("ln1_inv_std")
            s_xs, s_hi, s_lo = sem("ln1_out"), sem("x_hi"), sem("x_lo")
            s_tr = sem("x_transposed")
            s_xT = sem("xT_copied")
            s_qk = sem("qk_projected")
            s_qk_hi, s_qk_lo = sem("qk_hi"), sem("qk_lo")
            s_qk_out = sem("qk_stored")
            s_v = [sem(f"v_projected{r}") for r in two]
            s_v_cp = sem("v_copied")
            s_v_out = sem("v_stored")
            s_w_in = [sem(f"weights_loaded{r}") for r in range(WROWS)]
            s_w_hi, s_w_lo = sem("weights_hi"), sem("weights_lo")
            s_ones = sem("v_ones_set")

            block = ph.enter_context(nc.Block())

            def group_turns(eng, step):
                for r in two:
                    step(0, r)
                with eng.Fori(1, GROUPS // 2 - 1) as i:
                    for r in two:
                        step(i, r)
                for r in two:
                    step(GROUPS // 2 - 1, r)

            def after(i, r):
                return i + r, 1 - r

            def is_last(i, r):
                return isinstance(i, int) and 2 * i + r == GROUPS - 1

            def in_last_two(i):
                return isinstance(i, int) and i == GROUPS // 2 - 1

            own_weights = [(c, w_in[:, c, 0:3 * D], lambda hl, c=c: wq16[:, c, hl, :]) for c in range(DC)]
            own_weights.append((2, w_in[:, 2, 0:DC * D].rearrange("p (c n) -> p c n", c=DC), lambda hl: wo16[:, :, hl, :]))
            own_weights.append((3, w_in[:, 3, 0:DC * E].rearrange("p (c n) -> p c n", c=DC), lambda hl: wg16[:, :, hl, :]))

            def expert_row(e, r):
                if r < 2:
                    src = w_in[:, r, :]
                    return src, lambda hl: w1_16[:, bass.ds(e * (DC * 2 * F) + (r * 2 + hl) * F, F)]
                src = w_in[:, r, :].rearrange("p (c n) -> p c n", c=4)
                at = e * (FC * 2 * D) + (r - 2) * (4 * 2 * D)
                return src, lambda hl: w2_16[:, bass.ds(at, 8 * D)].rearrange("p (c h n) -> p c h n", c=4, h=2)[:, :, hl, :]

            @block.sync
            def _(sp):
                def load_positions(i, r):
                    for u in range(GROUP):
                        wait(sp, s_hi, (i * 2 + r - 2) * GROUP + u + 1)
                        wait(sp, s_lo, (i * 2 + r - 2) * GROUP + u + 1)
                        sp.dma_start(pe_xs[:, r, u, :], pe_tab[bass.ds(((i * 2 + r) * GROUP + u) * P, P), :]).then_inc(s_pe[r][u], 16)

                def load_weights(e, rows):
                    for r in rows:
                        sp.wait_ge(s_w_hi, e * WROWS + r + 1)
                        sp.wait_ge(s_w_lo, e * WROWS + r + 1)
                        if r < 2:
                            sp.dma_start(w_in[:, r, :], w1[bass.ds(e * D + r * P, P), :]).then_inc(s_w_in[r], 16)
                        else:
                            src = w2[bass.ds(e * F + (r - 2) * 4 * P, 4 * P), :].rearrange("(c p) n -> p c n", p=P)
                            sp.dma_start(w_in[:, r, :].rearrange("p (c n) -> p c n", c=4), src).then_inc(s_w_in[r], 16)

                def store_h(i, r):
                    for u in range(GROUP):
                        t = (i * 2 + r) * GROUP + u
                        sp.wait_ge(s_h, t + 1)
                        sp.dma_start(h1_rows[bass.ds(t * P, P), :], h_t[:, r, u, :]).then_inc(s_h_out[r][u], 16)

                def step(i, r):
                    g = i * 2 + r
                    if not in_last_two(i):
                        load_positions(i + 1, r)
                    if not is_last(i, r):
                        store_h(*after(i, r))
                    for m in range(4):
                        sp.wait_ge(s_qk_lo, g * 4 + m + 1)
                        for part in range(3):
                            lo = (part == 2) if m < 2 else (part == 1)
                            if m < 2:
                                dst = q_stack[m % 2, part * P:(part + 1) * P, bass.ds(g * GT, GT)]
                            else:
                                dst = k_stack[m % 2, part * P:(part + 1) * P, bass.ds(g * GT + P + (g // (NB // GROUP)) * 2 * P, GT)]
                            sp.dma_start(dst, qk16[:, m, int(lo), :]).then_inc(s_qk_out, 16)
                    if not is_last(i, r):
                        load_weights(g + 1, (0, 1))
                    sp.wait_ge(s_v_cp, g * 2 + 2)
                    sp.dma_start(v_rows[bass.ds(g * GT + P + (g // (NB // GROUP)) * 2 * P, GT), :].rearrange("(u p) n -> p u n", p=P),
                                 v_t[:].rearrange("p u h w -> p u (h w)")).then_inc(s_v_out, 16)
                    if not is_last(i, r):
                        load_weights(g + 1, (2, 3))

                sp.dma_start(idx_all[:], x_idx).then_inc(s_idx_in, 16)
                load_positions(0, 0)
                for c in range(DC):
                    sp.dma_start(w_in[:, c, 0:3 * D], wqkv[c * P:(c + 1) * P, :]).then_inc(s_w_in[c], 16)
                sp.dma_start(own_weights[2][1], wout.rearrange("(c p) n -> p c n", p=P)).then_inc(s_w_in[2], 16)
                sp.dma_start(own_weights[3][1], wg.rearrange("(c p) n -> p c n", p=P)).then_inc(s_w_in[3], 16)
                sp.dma_start(sel[:], part_sel).then_inc(s_bias_in, 16)
                sp.dma_start(brow[:], biases).then_inc(s_bias_in, 16)
                load_positions(0, 1)
                for dst, src in ((iota_e[:], iota8), (base[:, 0, :], region_base), (b1_col[:], b1),
                                 (token_no[:], token_of)):
                    sp.dma_start(dst, src).then_inc(s_small, 16)
                store_h(0, 0)
                load_weights(0, range(WROWS))
                group_turns(sp, step)
                sp.wait_ge(s_small, 4 * 16)
                sp.wait_ge(s_qk_out, GROUPS * 12 * 16)
                sp.wait_ge(s_v_out, GROUPS * 16)
                for r in two:
                    for u in range(GROUP):
                        sp.wait_ge(s_h_out[r][u], GROUPS // 2 * 16)

            @block.gpsimd
            def _(pool):
                g_ = nc.gpsimd

                def gather(i, r, u):
                    t = (i * 2 + r) * GROUP + u
                    wait(pool, s_emb[r][u], i * 16)
                    g_.tensor_copy(idx_col[:, r, u:u + 1], idx_all[:, bass.ds(t, 1)]).then_inc(s_idx, 1)
                    held(pool, s_passed, (s_idx, t + 1), (s_h_out[r][u], i * 16), (s_xs, t + 1 - 2 * GROUP))
                    g_.indirect_dma_start(h_t[:, r, u, :], None, emb, bass.IndirectOffsetOnAxis(idx_col[:, r, u:u + 1], 0))\
                      .then_inc(s_emb[r][u], 16)

                def inv_std(i, r, u):
                    pool.wait_ge(s_var, (i * 2 + r) * GROUP + u + 1)
                    g_.tensor_tensor(rstd[:, u, 1:2], rstd[:, u, 0:1], minus_half[:], ALU.pow).then_inc(s_rstd, 1)

                def step(i, r):
                    for u in range(GROUP):
                        if not in_last_two(i):
                            gather(i + 1, r, u)
                        if not is_last(i, r):
                            inv_std(*after(i, r), u)

                g_.memset(minus_half[:], -0.5).then_inc(s_zero, 1)
                g_.memset(ident16[:], 0.0).then_inc(s_zero, 1)
                g_.memset(ident32[:], 0.0).then_inc(s_zero, 1)
                g_.memset(before[:], 0.0).then_inc(s_zero, 1)
                pool.wait_ge(s_idx_in, 16)
                for u in range(GROUP):
                    gather(0, 0, u)
                pool.wait_ge(s_zero, 4)
                g_.affine_select(out=ident16[:], in_=ident16[:], compare_op=ALU.not_equal, fill=1.0, base=0,
                                 pattern=[[-1, P]], channel_multiplier=1).then_inc(s_const, 1)
                g_.memset(ones3[:], 1.0).then_inc(s_const, 1)
                g_.memset(ones_g[:], 1.0).then_inc(s_const, 1)
                for u in range(GROUP):
                    inv_std(0, 0, u)
                for u in range(GROUP):
                    gather(0, 1, u)
                g_.affine_select(out=ident32[:], in_=ident32[:], compare_op=ALU.not_equal, fill=1.0, base=0,
                                 pattern=[[-1, P]], channel_multiplier=1).then_inc(s_const, 1)
                g_.affine_select(out=before[:], in_=before[:], compare_op=ALU.is_ge, fill=1.0, base=0,
                                 pattern=[[-1, P]], channel_multiplier=1).then_inc(s_const, 1)
                g_.memset(ones_sq[:], 1.0).then_inc(s_const, 1)
                group_turns(pool, step)
                g_.memset(zero16[:], 0.0).then_inc(s_zero, 1)
                g_.memset(zero32[:], 0.0).then_inc(s_zero, 1)
                pool.wait_ge(s_zero, 6)
                for b in range(B):
                    for blk in (b * (NB + 2), b * (NB + 2) + NB + 1):
                        for a in range(2):
                            pool.dma_start(k_stack[a, :, blk * P:(blk + 1) * P].rearrange("(c p) t -> p c t", p=P),
                                           zero16[:].rearrange("p (c t) -> p c t", c=3)).then_inc(s_pad, 16)
                        pool.dma_start(v_rows[blk * P:(blk + 1) * P, :], zero32[:]).then_inc(s_pad, 16)
                pool.wait_ge(s_pad, 12 * 16)

            @block.scalar
            def _(act):
                a_ = nc.scalar

                def x_hi(i, r):
                    g = i * 2 + r
                    for u in range(GROUP):
                        act.wait_ge(s_xs, g * GROUP + u + 1)
                        wait(act, s_tr, g * 2)
                        a_.copy(x16[:, u, 0, :], pe_xs[:, r, u, :]).then_inc(s_hi, 1)

                def x_copy(i, r):
                    g = i * 2 + r
                    for b in range(2):
                        act.wait_ge(s_tr, g * 2 + b + 1)
                        wait(act, s_v[r], i * 2)
                        a_.copy(xT[:, r, :, b * 2 * P:(b + 1) * 2 * P].rearrange("p c (u t) -> p u c t", u=2),
                                psum16[:, b, :].rearrange("p (u c t) -> p u c t", u=2, c=4)).then_inc(s_xT, 1)

                def qk_hi(g, chunks):
                    for m in chunks:
                        act.wait_ge(s_qk, g * 4 + m + 1)
                        wait(act, s_qk_out, g * (12 * 16))
                        a_.activation(qk16[:, m, 0, :], psum[:, 2 + m, :], ACT.Copy, scale=1.0 / PS).then_inc(s_qk_hi, 1)

                def step(i, r):
                    g = i * 2 + r
                    qk_hi(g, (0, 1))
                    if not is_last(i, r):
                        x_hi(*after(i, r))
                    qk_hi(g, (2, 3))
                    if not is_last(i, r):
                        x_copy(*after(i, r))
                    for w in range(WROWS):
                        act.wait_ge(s_w_in[w], (g + 2) * 16)
                        src, dst = expert_row(g, w)
                        a_.activation(dst(0), src, ACT.Copy, scale=WS).then_inc(s_w_hi, 1)
                    for b in range(2):
                        act.wait_ge(s_v[r], i * 2 + b + 1)
                        wait(act, s_v_out, g * 16)
                        a_.activation(v_t[:, b * 2:b * 2 + 2, :, 0:DH],
                                      psum[:, 6 + b, :].rearrange("p (u h d) -> p u h d", u=2, h=H),
                                      ACT.Copy, scale=1.0 / PS).then_inc(s_v_cp, 1)

                for w, src, dst in own_weights:
                    act.wait_ge(s_w_in[w], 16)
                    a_.activation(dst(0), src, ACT.Copy, scale=WS).then_inc(s_w_hi, 1)
                act.wait_ge(s_ones, 1)
                x_hi(0, 0)
                x_copy(0, 0)
                group_turns(act, step)

            @block.vector
            def _(dve):
                v_ = nc.vector

                def statistics(i, r):
                    for u in range(GROUP):
                        t = (i * 2 + r) * GROUP + u
                        dve.wait_ge(s_emb[r][u], (i + 1) * 16)
                        dve.wait_ge(s_pe[r][u], (i + 1) * 16)
                        v_.tensor_tensor(h_t[:, r, u, :], h_t[:, r, u, :], pe_xs[:, r, u, :], ALU.add).then_inc(s_h, 1)
                        dve.wait_ge(s_h, t + 1)
                        wait(dve, s_xs, t + 1 - GROUP)
                        v_.bn_stats(stat[:, u, :], h_t[:, r, u, :]).then_inc(s_stat, 1)
                        held(dve, s_passed, (s_stat, t + 1))
                        v_.bn_aggr(mv[:, u, :], stat[:, u, :]).then_inc(s_mv, 1)
                        dve.wait_ge(s_mv, t + 1)
                        v_.tensor_scalar(rstd[:, u, 0:1], mv[:, u, 1:2], EPS, XS ** -2, ALU.add, ALU.mult).then_inc(s_var, 1)

                def normalise(i, r):
                    for u in range(GROUP):
                        dve.wait_ge(s_rstd, (i * 2 + r) * GROUP + u + 1)
                        v_.tensor_scalar(pe_xs[:, r, u, :], h_t[:, r, u, :], mv[:, u, 0:1], rstd[:, u, 1:2],
                                         ALU.subtract, ALU.mult).then_inc(s_xs, 1)
                    for u in range(GROUP):
                        dve.wait_ge(s_hi, (i * 2 + r) * GROUP + u + 1)
                        v_.tensor_tensor(x16[:, u, 1, :], pe_xs[:, r, u, :], x16[:, u, 0, :], ALU.subtract).then_inc(s_lo, 1)

                def low_part(src, dst):
                    v_.scalar_tensor_tensor(out=dst(1), in0=src, scalar=WS, in1=dst(0),
                                            op0=ALU.mult, op1=ALU.subtract).then_inc(s_w_lo, 1)

                def step(i, r):
                    g = i * 2 + r
                    if not is_last(i, r):
                        statistics(*after(i, r))
                        normalise(*after(i, r))
                    for m in range(4):
                        dve.wait_ge(s_qk_hi, g * 4 + m + 1)
                        v_.scalar_tensor_tensor(out=qk16[:, m, 1, :], in0=psum[:, 2 + m, :], scalar=1.0 / PS,
                                                in1=qk16[:, m, 0, :], op0=ALU.mult, op1=ALU.subtract).then_inc(s_qk_lo, 1)
                    for w in range(WROWS):
                        dve.wait_ge(s_w_hi, (g + 1) * WROWS + w + 1)
                        low_part(*expert_row(g, w))

                v_.memset(v_t[:, :, :, DH:VW], 1.0 / XS).then_inc(s_ones, 1)
                statistics(0, 0)
                for w, src, dst in own_weights:
                    dve.wait_ge(s_w_hi, w + 1)
                    low_part(src, dst)
                normalise(0, 0)
                dve.wait_ge(s_bias_in, 2 * 16)
                split_bias(dve, v_, brow[:], bs3[:], all_bias3[:], PS, sel, s_bias_step, s_bias)
                dve.wait_ge(s_bias, 1)
                v_.tensor_copy(bias3[:], all_bias3[:, OB_OUT:OB_2]).then_inc(s_bias, 1)
                group_turns(dve, step)

            @block.tensor
            def _(pe):
                def transpose(i, r):
                    g = i * 2 + r
                    wait(pe, s_xT, g * 2)
                    for u in range(GROUP):
                        pe.wait_ge(s_lo, g * GROUP + u + 1)
                        for c in range(2 * DC):
                            at = ((u % 2) * 4 + c) * P
                            last = nc.tensor.transpose(psum16[:, u // 2, at:at + P],
                                                       x16[:, u, c // DC, (c % DC) * P:(c % DC + 1) * P], ident16[:])
                        if u % 2:
                            last.then_inc(s_tr, 1)

                def step(i, r):
                    g = i * 2 + r
                    pe.wait_ge(s_xT, g * 2 + 2)
                    for m in range(4):
                        wait(pe, s_qk_lo, (g - 1) * 4 + m + 1)
                        ps = psum[:, 2 + m, :]
                        nc.tensor.matmul(ps, all_bias3[:, OB_QKV + m * P:OB_QKV + (m + 1) * P], ones_g[:], start=True, stop=False)
                        for c in range(DC):
                            for wl, xl in ((0, 0), (0, 1), (1, 0)):
                                last = nc.tensor.matmul(ps, wq16[:, c, wl, m * P:(m + 1) * P], xT[:, r, xl * DC + c, :],
                                                        start=False, stop=(c == DC - 1 and wl == 1))
                        last.then_inc(s_qk, 1)
                    if not is_last(i, r):
                        transpose(*after(i, r))
                    for u in range(GROUP):
                        if u % 2 == 0:
                            wait(pe, s_v_cp, (g - 1) * 2 + u // 2 + 1)
                        ps = psum[:, 6 + u // 2, (u % 2) * D:(u % 2 + 1) * D]
                        nc.tensor.matmul(ps, ones3[:, 0:P], all_bias3[:, OB_QKV + 2 * D:OB_QKV + 3 * D], start=True, stop=False)
                        for c in range(DC):
                            for wl, xl in ((0, 0), (0, 1), (1, 0)):
                                last = nc.tensor.matmul(ps, xT[:, r, xl * DC + c, u * P:(u + 1) * P], wq16[:, c, wl, 2 * D:3 * D],
                                                        start=False, stop=(c == DC - 1 and wl == 1))
                        if u % 2:
                            last.then_inc(s_v[r], 1)

                pe.wait_ge(s_const, 3)
                transpose(0, 0)
                pe.wait_ge(s_w_lo, WROWS)
                pe.wait_ge(s_bias, 2)
                group_turns(pe, step)

        shared = Shared(b1_col=b1_col, b2=b2, base=base, before=before, bias3=bias3, h1_rows=h1_rows,
                        ident16=ident16, ident32=ident32, iota_e=iota_e, k_stack=k_stack, mask_tab=mask_tab,
                        minus_half=minus_half, nc=nc, ones3=ones3, ones_sq=ones_sq, out=out,
                        part_col=part_col, psum=psum, psum16=psum16, q_stack=q_stack, s_passed=s_passed,
                        sem=sem, slot_expert=slot_expert, slot_iota=slot_iota, slot_tab=slot_tab,
                        token_no=token_no, v_rows=v_rows, valid_row=valid_row, w1_16=w1_16, w2_16=w2_16,
                        wg16=wg16, wo16=wo16, x_lists=x_lists)
        attend(shared)
        plan(shared)
        experts(shared)


class Shared:

    def __init__(self, b1_col, b2, base, before, bias3, h1_rows, ident16, ident32, iota_e, k_stack, mask_tab,
                 minus_half, nc, ones3, ones_sq, out, part_col, psum, psum16, q_stack, s_passed, sem,
                 slot_expert, slot_iota, slot_tab, token_no, v_rows, valid_row, w1_16, w2_16, wg16, wo16,
                 x_lists):
        self.b1_col = b1_col
        self.b2 = b2
        self.base = base
        self.before = before
        self.bias3 = bias3
        self.h1_rows = h1_rows
        self.ident16 = ident16
        self.ident32 = ident32
        self.iota_e = iota_e
        self.k_stack = k_stack
        self.mask_tab = mask_tab
        self.minus_half = minus_half
        self.nc = nc
        self.ones3 = ones3
        self.ones_sq = ones_sq
        self.out = out
        self.part_col = part_col
        self.psum = psum
        self.psum16 = psum16
        self.q_stack = q_stack
        self.s_passed = s_passed
        self.sem = sem
        self.slot_expert = slot_expert
        self.slot_iota = slot_iota
        self.slot_tab = slot_tab
        self.token_no = token_no
        self.v_rows = v_rows
        self.valid_row = valid_row
        self.w1_16 = w1_16
        self.w2_16 = w2_16
        self.wg16 = wg16
        self.wo16 = wo16
        self.x_lists = x_lists


def split_bias(dve, v_, row, tmp, out3, scale, sel, step, done):
    n = 0

    def then(ins, last=False):
        nonlocal n
        if last:
            ins.then_inc(done, 1)
            return
        ins.then_inc(step, 1)
        n += 1
        dve.wait_ge(step, n)

    then(v_.tensor_scalar(row, row, scale, None, ALU.mult))
    then(v_.tensor_copy(tmp, row))
    then(v_.tensor_scalar(out3, tmp, sel[:, 0:1], None, ALU.mult))
    then(v_.tensor_tensor(row, row, tmp, ALU.subtract))
    then(v_.tensor_copy(tmp, row))
    then(v_.scalar_tensor_tensor(out=out3, in0=tmp, scalar=sel[:, 1:2], in1=out3, op0=ALU.mult, op1=ALU.add))
    then(v_.tensor_tensor(row, row, tmp, ALU.subtract))
    then(v_.tensor_copy(tmp, row))
    then(v_.scalar_tensor_tensor(out=out3, in0=tmp, scalar=sel[:, 2:3], in1=out3, op0=ALU.mult, op1=ALU.add), last=True)


def held(eng, s_passed, *waits):
    for sem, v in waits:
        wait(eng, sem, v)
    eng.sem_inc(s_passed, 1)


def halves(rows, u, start, end):
    return rows[:, u, start // 2:end // 2].bitcast(F16)


def wait(eng, semaphore, value):
    if not isinstance(value, int) or value > 0:
        eng.wait_ge(semaphore, value)


def turns(eng, count, turn):
    turn(0)
    with eng.Fori(1, count) as i:
        turn(i)


ROUTE_STEPS = 16


def attend(k):
    nc, sem, psum, psum16 = k.nc, k.sem, k.psum, k.psum16
    ident16, ident32, bias3, ones3 = k.ident16, k.ident32, k.bias3, k.ones3
    with ExitStack() as ph:
        def sb(name, shape, dt):
            return ph.enter_context(nc.sbuf_tensor(name, shape, dt))

        RING = 4
        ks = sb("ks", [P, RING, PAIRS, 3 * P], F16)
        qz = sb("qz", [P, RING, PAIRS, 2, P], F16)
        vs = sb("vs", [P, 2, 3, H, VW], F32)
        masks = sb("masks", [P, 2, 3 * P], BF16)
        hh = sb("hh", [P, 2, D], F32)
        mx = sb("mx", [P, 2, H], F32)
        mT = sb("mT", [H, P], F16)
        junk = sb("junk", [P, 2, 3 * P], BF16)
        probs = sb("probs", [P, 4, 3, 2, P], F32)
        oT = sb("oT", [P, 4 * P], F32)
        att = oT[:, 0:D]
        rcp = sb("rcp", [P, H, 1], F32)
        a16 = sb("a16", [P, 2, D], F16)
        stat = sb("stat2", [P, 6], F32)
        mv = sb("mv2", [P, 2], F32)
        rstd = sb("rstd2", [P, 2], F32)
        xs2 = sb("xs2", [P, D], F32)
        xrow = sb("xrow", [P, RING, XW], I32)
        actT = sb("actT", [P, 2 * DC, P], F16)
        g8 = sb("g8", [P, 12, E], F32)
        gs = sb("gs", [P, 8], F32)
        gi = sb("gi", [P, 8], U32)
        member = sb("member", [P, E], BF16)
        pos_t = sb("pos_t", [P, RING, TOPK], I32)

        s_zero = sem("q_zeroed")
        s_stack = [sem(f"stacks_loaded{u}") for u in range(RING)]
        s_mask = [sem(f"mask_loaded{r}") for r in range(2)]
        s_vl = [sem(f"values_loaded{r}") for r in range(2)]
        s_h1 = [sem(f"h1_loaded{r}") for r in range(2)]
        s_sc, s_max = sem("scores_made"), sem("row_max_taken")
        s_mtr, s_mT = sem("max_transposed"), sem("max_negated")
        s_mrow = [sem(f"max_row_placed{u}") for u in range(RING)]
        s_pt, s_exp, s_sel, s_pv = sem("scores_T_made"), sem("exp_made"), sem("probs_masked"), sem("values_summed")
        s_oT, s_otr = sem("outputs_copied"), sem("outputs_transposed")
        s_rcp, s_att, s_ahi, s_alo = sem("sums_inverted"), sem("outputs_normalised"), sem("outputs_hi"), sem("outputs_lo")
        s_atr, s_aT, s_wo = sem("att_transposed"), sem("aT_copied"), sem("att_projected")
        s_h2 = sem("h2_added")
        s_h2o = sem("h2_stored")
        s_ln = sem("ln2_steps")
        s_var, s_rstd = sem("ln2_variance"), sem("ln2_inv_std")
        s_xhi, s_xlo = sem("x2_hi"), sem("x2_lo")
        s_xtr, s_x2T, s_gate = sem("x2_transposed"), sem("x2T_copied"), sem("gate_logits")
        s_gm, s_ge = sem("gate_max_negated"), sem("gate_exp")
        s_rt = sem("route_steps")
        s_mem, s_rank, s_pos = sem("members_marked"), sem("ranks_made"), sem("positions_made")
        s_sc1 = [sem(f"rows_scattered{u}") for u in range(RING)]
        s_po = sem("output_bank_zeroed")
        s_tok = sem("token_number_copied")

        block = ph.enter_context(nc.Block())

        def ahead(i, u, n):
            return i + (u + n) // RING, (u + n) % RING

        def over_tiles(eng, step, peeled=1):
            for t in range(peeled * RING):
                step(t // RING, t % RING, t)
            with eng.Fori(peeled, TILES // RING - 1) as i:
                for u in range(RING):
                    step(i, u, i * RING + u)
            for u in range(RING):
                step(TILES // RING - 1, u, TILES - RING + u)

        def known(t, n):
            return not isinstance(t, int) or 0 <= t + n < TILES

        def flat_pt(p):
            return psum[:].rearrange("p b n -> p (b n)")[:, (2 + 2 * (p % 2)) * 512:(2 + 2 * (p % 2)) * 512 + 3 * 2 * P]

        @block.sync
        def _(sp):
            def load(i, u):
                t = i * RING + u
                wait(sp, s_pv, (t - RING) * PAIRS + PAIRS)
                at = t * P + (t // NB) * 2 * P
                for a in range(2):
                    sp.dma_start(ks[a * 64:a * 64 + 48, u, :, :],
                                 k.k_stack[a, :, bass.ds(at, 3 * P)].rearrange("(r p) t -> r p t", p=PAIRS)).then_inc(s_stack[u], 16)
                    sp.dma_start(qz[a * 64:a * 64 + 48, u, :, a, :],
                                 k.q_stack[a, :, bass.ds(t * P, P)].rearrange("(r p) t -> r p t", p=PAIRS)).then_inc(s_stack[u], 16)
                sp.dma_start(ks[ONES_ROW:ONES_ROW + 1, u, :, :],
                             k.valid_row[:, :, bass.ds(at, 3 * P)]).then_inc(s_stack[u], 16)

            def load_mask(i, u):
                t = i * RING + u
                r = u % 2
                wait(sp, s_max, (t - 1) * H)
                sp.dma_start(masks[:, r, :], k.mask_tab[bass.ds(t * P, P), :].bitcast(BF16)).then_inc(s_mask[r], 16)

            def load_values(i, u):
                t = i * RING + u
                r = u % 2
                at = t * P + (t // NB) * 2 * P
                wait(sp, s_pv, (t - 1) * PAIRS)
                sp.dma_start(vs[:, r, :, :, :].rearrange("p j h w -> p j (h w)"),
                             k.v_rows[bass.ds(at, 3 * P), :].rearrange("(j p) n -> p j n", p=P)).then_inc(s_vl[r], 16)

            def load_residual(i, u):
                t = i * RING + u
                r = u % 2
                wait(sp, s_h2o, (t - 1) * 16)
                sp.dma_start(hh[:, r, :], k.h1_rows[bass.ds(t * P, P), :]).then_inc(s_h1[r], 16)

            def max_row(i, u):
                t = i * RING + u
                wait(sp, s_mT, t + 1)
                sp.dma_start(qz[ONES_ROW:ONES_ROW + 1, u, :, :, :].rearrange("o p a t -> o (p a) t"),
                             mT[:]).then_inc(s_mrow[u], 16)

            def store(i, u):
                t = i * RING + u
                wait(sp, s_ln, t * 3 + 3)
                sp.dma_start(k.out[bass.ds(t * P, P), :], hh[:, u % 2, :]).then_inc(s_h2o, 16)

            def body(i, u, t):
                if known(t, 1):
                    max_row(*ahead(i, u, 1))
                if known(t, 3):
                    load(*ahead(i, u, 3))
                    load_mask(*ahead(i, u, 3))
                if known(t, 1):
                    load_values(*ahead(i, u, 1))
                if known(t, -2):
                    store(*ahead(i, u, -2))
                load_residual(i, u)

            sp.wait_ge(s_zero, 2)
            for t in range(3):
                load(0, t)
                load_mask(0, t) if t < 2 else None
            load_values(0, 0)
            max_row(0, 0)
            load_mask(0, 2)
            over_tiles(sp, body)
            for u in (RING - 2, RING - 1):
                store(TILES // RING - 1, u)
            sp.wait_ge(s_h2o, TILES * 16)

        @block.gpsimd
        def _(pool):
            g_ = nc.gpsimd
            g_.memset(ks[:].rearrange("p r q t -> p (r q t)").bitcast(F32), 0.0).then_inc(s_zero, 1)

            def inv_std(t):
                wait(pool, s_var, t + 1)
                g_.tensor_tensor(rstd[:, 1:2], rstd[:, 0:1], k.minus_half[:], ALU.pow).then_inc(s_rstd, 1)

            def scatter(i, u, t, experts=(0, 1)):
                wait(pool, s_pos, t + 1)
                if 0 in experts:
                    g_.tensor_copy(xrow[:, u, TOKEN:TOKEN + 1], k.token_no[:, bass.ds(t, 1)]).then_inc(s_tok, 1)
                held(pool, k.s_passed, (s_tok, t + 1))
                for c in experts:
                    g_.indirect_dma_start(k.x_lists, bass.IndirectOffsetOnAxis(pos_t[:, u, c:c + 1], 0), xrow[:, u, :], None)\
                      .then_inc(s_sc1[u], 16)

            def body(i, u, t):
                for p in range(PAIRS):
                    held(pool, k.s_passed, (s_exp, t * PAIRS + p + 1))
                    pr = probs[:, p % 4, :, :, :]
                    g_.affine_select(out=pr[:, 0, :, :], in_=pr[:, 0, :, :], compare_op=ALU.is_ge, fill=0.0, base=0,
                                     pattern=[[0, 2], [-1, P]], channel_multiplier=1).then_inc(s_sel, 1)
                    g_.affine_select(out=pr[:, 2, :, :], in_=pr[:, 2, :, :], compare_op=ALU.is_ge, fill=0.0, base=0,
                                     pattern=[[0, 2], [1, P]], channel_multiplier=-1).then_inc(s_sel, 1)
                    if p == 2 and known(t, -2):
                        inv_std(t - 2)
                    if p in (4, 6) and known(t, -4):
                        scatter(*ahead(i, u, -4), t - 4, (p // 2 - 2,))

            over_tiles(pool, body)
            last = TILES // RING - 1
            inv_std(TILES - 2)
            scatter(last, 0, TILES - 4)
            inv_std(TILES - 1)
            for u in range(1, RING):
                scatter(last, u, TILES - RING + u)
            for u in range(RING):
                pool.wait_ge(s_sc1[u], TILES // RING * TOPK * 16)

        @block.scalar
        def _(act):
            a_ = nc.scalar

            def out_copy(t):
                wait(act, s_pv, t * PAIRS + PAIRS)
                wait(act, s_alo, t)
                a_.copy(oT[:], psum[:, 6, :]).then_inc(s_oT, 1)

            def att_hi(t):
                wait(act, s_att, t + 1)
                wait(act, s_atr, t)
                a_.copy(a16[:, 0, :], att).then_inc(s_ahi, 1)

            def x_hi(i, u, t):
                wait(act, s_ln, t * 3 + 3)
                wait(act, s_sc1[u], i * TOPK * 16)
                a_.copy(halves(xrow, u, 0, D), xs2[:]).then_inc(s_xhi, 1)

            def att_copy(t):
                wait(act, s_atr, t + 1)
                a_.copy(actT[:].rearrange("p c t -> p (c t)"), psum16[:, 7, 0:4 * P]).then_inc(s_aT, 1)

            def x_copy(t):
                wait(act, s_xtr, t + 1)
                a_.copy(actT[:].rearrange("p c t -> p (c t)"), psum16[:, 7, 0:4 * P]).then_inc(s_x2T, 1)

            def gate_exp(t):
                wait(act, s_gm, t + 1)
                wait(act, s_rt, t * ROUTE_STEPS)
                a_.activation(g8[:, 1, :], psum[:, 7, 0:E], ACT.Exp, bias=gs[:, 0:1], scale=1.0 / PS,
                              accum_out=gs[:, 1:2]).then_inc(s_ge, 1)

            def body(i, u, t):
                for p in range(PAIRS):
                    if p == 0 and known(t, -2):
                        att_copy(t - 2)
                    wait(act, s_pt, t * PAIRS + p + 1)
                    wait(act, s_pv, t * PAIRS + p - 3)
                    a_.activation(probs[:, p % 4, :, :, :].rearrange("p j a t -> p (j a t)"),
                                  flat_pt(p), ACT.Exp, scale=SCALE).then_inc(s_exp, 1)
                    if p == 1 and known(t, -1):
                        out_copy(t - 1)
                    if p == 2 and known(t, -3):
                        x_copy(t - 3)
                    if p == 4 and known(t, -3):
                        gate_exp(t - 3)
                    if p == 5 and known(t, -2):
                        x_hi(*ahead(i, u, -2), t - 2)
                    if p == 6 and known(t, -1):
                        att_hi(t - 1)

            over_tiles(act, body, peeled=2)
            last = TILES // RING - 1
            att_copy(TILES - 2)
            out_copy(TILES - 1)
            x_hi(last, RING - 2, TILES - 2)
            x_copy(TILES - 3)
            gate_exp(TILES - 3)
            att_hi(TILES - 1)
            att_copy(TILES - 1)
            x_hi(last, RING - 1, TILES - 1)
            for t in (TILES - 2, TILES - 1):
                x_copy(t)
                gate_exp(t)

        @block.vector
        def _(dve):
            v_ = nc.vector
            v_.memset(qz[:].rearrange("p r q a t -> p (r q a t)").bitcast(F32), 0.0).then_inc(s_zero, 1)
            v_.memset(psum[:, 6, :], 0.0).then_inc(s_po, 1)

            def maxima(i, u, t, s):
                r = u % 2
                if s == 0:
                    wait(dve, s_mask[r], (i * 2 + u // 2 + 1) * 16)
                    wait(dve, s_mtr, t - 1)
                held(dve, k.s_passed, (s_sc, t * H + s + 1), (s_max, t * H + s - 1))
                v_.tensor_tensor_reduce(out=junk[:, s % 2, :], in0=psum[:, s % 2, 0:3 * P], in1=masks[:, r, :], scale=1.0,
                                        scalar=-3.0e38, op0=ALU.add, op1=ALU.max, accum_out=mx[:, r, s:s + 1]).then_inc(s_max, 1)

            def negate_max(t):
                wait(dve, s_mtr, t + 1)
                v_.tensor_scalar(mT[:], psum[0:H, 0, 0:P], -1.0, -60000.0, ALU.mult, ALU.max).then_inc(s_mT, 1)

            def normalise(t):
                wait(dve, s_otr, t + 1)
                wait(dve, s_alo, t)
                bank = psum[:, 7, :]
                v_.reciprocal(rcp[:], bank.rearrange("p (s w) -> p s w", w=32)[:, :, DH:VW]).then_inc(s_rcp, 1)
                wait(dve, s_rcp, t + 1)
                v_.tensor_tensor(att.rearrange("p (a q d) -> p q a d", a=2, d=DH),
                                 bank.rearrange("p (q a w) -> p q a w", a=2, w=32)[:, :, :, 0:DH],
                                 rcp[:].rearrange("p (q a) o -> p q a o", a=2).to_broadcast([P, PAIRS, 2, DH]),
                                 ALU.mult).then_inc(s_att, 1)

            def att_lo(t):
                wait(dve, s_ahi, t + 1)
                v_.tensor_tensor(a16[:, 1, :], att, a16[:, 0, :], ALU.subtract).then_inc(s_alo, 1)

            def residual(i, u, t):
                wait(dve, s_wo, t + 1)
                wait(dve, s_xlo, t)
                wait(dve, s_h1[u % 2], (i * 2 + u // 2 + 1) * 16)
                v_.scalar_tensor_tensor(out=hh[:, u % 2, :], in0=psum[:, 7, 0:D], scalar=1.0 / PS, in1=hh[:, u % 2, :],
                                        op0=ALU.mult, op1=ALU.add).then_inc(s_h2, 1)

            def statistics(u, t, n):
                if n == 0:
                    wait(dve, s_h2, t + 1)
                    v_.bn_stats(stat[:], hh[:, u % 2, :]).then_inc(s_ln, 1)
                if n == 1:
                    held(dve, k.s_passed, (s_ln, t * 3 + 1))
                    v_.bn_aggr(mv[:], stat[:]).then_inc(s_ln, 1)
                if n == 2:
                    wait(dve, s_ln, t * 3 + 2)
                    v_.tensor_scalar(rstd[:, 0:1], mv[:, 1:2], EPS, XS ** -2, ALU.add, ALU.mult).then_inc(s_var, 1)

            def norm2(u, t):
                wait(dve, s_rstd, t + 1)
                wait(dve, s_xlo, t)
                v_.tensor_scalar(xs2[:], hh[:, u % 2, :], mv[:, 0:1], rstd[:, 1:2], ALU.subtract, ALU.mult).then_inc(s_ln, 1)

            def x_lo(u, t):
                wait(dve, s_xhi, t + 1)
                v_.tensor_tensor(halves(xrow, u, D, 2 * D), xs2[:], halves(xrow, u, 0, D), ALU.subtract).then_inc(s_xlo, 1)

            def gate_max(t):
                held(dve, k.s_passed, (s_gate, t + 1))
                v_.max(g8[:, 0, :], psum[:, 7, 0:E]).then_inc(s_rt, 1)
                wait(dve, s_rt, t * ROUTE_STEPS + 1)
                wait(dve, s_ge, t)
                v_.tensor_scalar(gs[:, 0:1], g8[:, 0, 0:1], -1.0 / PS, None, ALU.mult).then_inc(s_gm, 1)

            def route(u, t, n):
                def made(m):
                    wait(dve, s_rt, t * ROUTE_STEPS + 2 + m)

                if n == 0:
                    wait(dve, s_ge, t + 1)
                    v_.reciprocal(gs[:, 2:3], gs[:, 1:2]).then_inc(s_rt, 1)
                if n == 1:
                    made(0)
                    v_.tensor_scalar(g8[:, 2, :], g8[:, 1, :], gs[:, 2:3], None, ALU.mult).then_inc(s_rt, 1)
                if n == 2:
                    held(dve, k.s_passed, (s_rt, t * ROUTE_STEPS + 2 + 1))
                    v_.max(g8[:, 3, :], g8[:, 2, :]).then_inc(s_rt, 1)
                if n == 3:
                    held(dve, k.s_passed, (s_rt, t * ROUTE_STEPS + 2 + 2))
                    v_.max_index(gi[:], g8[:, 3, :], g8[:, 2, :]).then_inc(s_rt, 1)
                if n == 4:
                    made(2)
                    v_.scalar_tensor_tensor(out=gs[:, 3:4], in0=g8[:, 3, 0:1], scalar=1e-8, in1=g8[:, 3, 1:2],
                                            op0=ALU.add, op1=ALU.add).then_inc(s_rt, 1)
                if n == 5:
                    made(3)
                    v_.tensor_copy(g8[:, 4, :], gi[:]).then_inc(s_rt, 1)
                if n == 6:
                    made(4)
                    v_.reciprocal(gs[:, 4:5], gs[:, 3:4]).then_inc(s_rt, 1)
                if n == 7:
                    made(5)
                    v_.tensor_scalar(g8[:, 5, :], k.iota_e[:], g8[:, 4, 0:1], None, ALU.is_equal).then_inc(s_rt, 1)
                if n == 8:
                    made(5)
                    v_.tensor_scalar(g8[:, 6, :], k.iota_e[:], g8[:, 4, 1:2], None, ALU.is_equal).then_inc(s_rt, 1)
                if n == 9:
                    made(6)
                    v_.tensor_scalar(xrow[:, u, WEIGHTS:WEIGHTS + TOPK].bitcast(F32), g8[:, 3, 0:TOPK], gs[:, 4:5], None,
                                     ALU.mult).then_inc(s_rt, 1)
                if n == 10:
                    v_.tensor_copy(xrow[:, u, FIRST:FIRST + 1].bitcast(F32), g8[:, 4, 0:1]).then_inc(s_rt, 1)
                if n == 11:
                    made(8)
                    wait(dve, s_rank, t)
                    v_.tensor_tensor(member[:], g8[:, 5, :], g8[:, 6, :], ALU.add).then_inc(s_mem, 1)

            def place(i, u, t, n):
                def made(m):
                    wait(dve, s_rt, t * ROUTE_STEPS + 13 + m)

                r = u % 2
                if n == 0:
                    wait(dve, s_rank, t + 1)
                    wait(dve, s_pos, t)
                    v_.tensor_tensor(g8[:, 7, :], psum[:, 7, 16:16 + E], k.base[:, r, :], ALU.add).then_inc(s_rt, 1)
                if n == 1:
                    v_.tensor_tensor(k.base[:, 1 - r, :], psum[:, 7, 16 + E:16 + 2 * E], k.base[:, r, :], ALU.add).then_inc(s_rt, 1)
                if n in (2, 3):
                    made(0)
                    c = n - 2
                    v_.tensor_tensor_reduce(out=g8[:, 8 + c, :], in0=g8[:, 5 + c, :], in1=g8[:, 7, :], scale=1.0, scalar=0.0,
                                            op0=ALU.mult, op1=ALU.add, accum_out=g8[:, 10, c:c + 1]).then_inc(s_rt, 1)
                if n == 4:
                    made(3)
                    wait(dve, s_sc1[u], i * TOPK * 16)
                    v_.tensor_copy(pos_t[:, u, :], g8[:, 10, 0:TOPK]).then_inc(s_pos, 1)

            for t in range(2):
                for s in range(H):
                    maxima(0, t, t, s)
                if t == 0:
                    negate_max(0)

            def step(i, u, t):
                if known(t, 1):
                    wait(dve, s_mrow[u], (i + 1) * 16)
                    negate_max(t + 1)
                for s in range(H):
                    if known(t, 2):
                        maxima(*ahead(i, u, 2), t + 2, s)
                    if known(t, -2):
                        at = ahead(i, u, -2)
                        if s == 1:
                            residual(*at, t - 2)
                        if s in (2, 3, 4):
                            statistics(at[1], t - 2, s - 2)
                    if known(t, -4) and s in (4, 5, 6):
                        for n in ((0, 1), (2, 3), (4,))[s - 4]:
                            place(*ahead(i, u, -4), t - 4, n)
                    if known(t, -2):
                        if s == 9:
                            norm2(at[1], t - 2)
                        if s == 12:
                            x_lo(at[1], t - 2)
                    if known(t, -3):
                        if s == 8:
                            gate_max(t - 3)
                        if s >= 10:
                            for n in ((0,), (1,), (2,), (3, 4), (5, 6), (7, 8))[s - 10]:
                                route(ahead(i, u, -3)[1], t - 3, n)
                    if known(t, -1):
                        if s == 11:
                            normalise(t - 1)
                        if s == 14:
                            att_lo(t - 1)
                if known(t, -3):
                    for n in (9, 10, 11):
                        route(ahead(i, u, -3)[1], t - 3, n)

            over_tiles(dve, step, peeled=2)
            last = TILES // RING - 1

            def add_residual(u, t):
                residual(last, u, t)
                for n in range(3):
                    statistics(u, t, n)

            def place_all(u, t):
                for n in range(5):
                    place(last, u, t, n)

            def route_all(t):
                gate_max(t)
                for n in range(12):
                    route(t % RING, t, n)

            add_residual(RING - 2, TILES - 2)
            place_all(RING - 4, TILES - 4)
            norm2(RING - 2, TILES - 2)
            x_lo(RING - 2, TILES - 2)
            route_all(TILES - 3)
            normalise(TILES - 1)
            att_lo(TILES - 1)
            add_residual(RING - 1, TILES - 1)
            place_all(RING - 3, TILES - 3)
            norm2(RING - 1, TILES - 1)
            x_lo(RING - 1, TILES - 1)
            route_all(TILES - 2)
            place_all(RING - 2, TILES - 2)
            route_all(TILES - 1)
            place_all(RING - 1, TILES - 1)

        @block.tensor
        def _(pe):
            def scores(i, u, t, s):
                p, a = s // 2, s % 2
                if s == 0:
                    wait(pe, s_stack[u], (i + 1) * 5 * 16)
                    wait(pe, s_mT, t)
                wait(pe, s_max, t * H + s - 1)
                nc.tensor.matmul(psum[:, s % 2, 0:3 * P], qz[0:ONES_ROW, u, p, a, :], ks[0:ONES_ROW, u, p, :],
                                 start=True, stop=True).then_inc(s_sc, 1)

            def max_transpose(u, t):
                wait(pe, s_max, t * H + H)
                nc.tensor.transpose(psum[0:H, 0, 0:P], mx[:, u % 2, :], ident32[:]).then_inc(s_mtr, 1)

            def scores_t(i, u, t, p):
                if p == 0:
                    wait(pe, s_mrow[u], (i + 1) * 16)
                wait(pe, s_exp, t * PAIRS + p - 1)
                for j in range(3):
                    at = (2 + 2 * (p % 2)) * 512 + j * 2 * P
                    last = nc.tensor.matmul(psum[:, at // 512, at % 512:at % 512 + 2 * P], ks[0:ONES_ROW + 1, u, p, j * P:(j + 1) * P],
                                            qz[0:ONES_ROW + 1, u, p, :, :], start=True, stop=True)
                last.then_inc(s_pt, 1)

            def values(i, u, t, p):
                if p == 0:
                    wait(pe, s_vl[u % 2], (i * 2 + u // 2 + 1) * 16)
                    wait(pe, s_oT, t)
                wait(pe, s_sel, (t * PAIRS + p + 1) * 2)
                for j in range(3):
                    for a in range(2):
                        s = 2 * p + a
                        last = nc.tensor.matmul(psum[32 * (s % 4):32 * (s % 4) + VW, 6, (s // 4) * P:(s // 4 + 1) * P],
                                                vs[:, u % 2, j, a * PAIRS + p, :], probs[:, p % 4, j, a, :],
                                                start=(j == 0), stop=(j == 2), skip_group_check=True)
                last.then_inc(s_pv, 1)

            def out_transpose(t):
                wait(pe, s_oT, t + 1)
                wait(pe, s_ge, t - 1)
                for b in range(4):
                    last = nc.tensor.transpose(psum[:, 7, b * P:(b + 1) * P], oT[:, b * P:(b + 1) * P], ident32[:])
                last.then_inc(s_otr, 1)

            def att_transpose(t):
                wait(pe, s_alo, t + 1)
                for c in range(2 * DC):
                    last = nc.tensor.transpose(psum16[:, 7, c * P:(c + 1) * P], a16[:, c // DC, (c % DC) * P:(c % DC + 1) * P], ident16[:])
                last.then_inc(s_atr, 1)

            def three_pass(ps, left, right, bias_l, bias_r):
                nc.tensor.matmul(ps, bias_l, bias_r, start=True, stop=False)
                for c in range(DC):
                    for wl, xl in ((0, 0), (0, 1), (1, 0)):
                        last = nc.tensor.matmul(ps, left[:, xl * DC + c, :], right[:, c, wl, :],
                                                start=False, stop=(c == DC - 1 and wl == 1))
                return last

            def project(t):
                wait(pe, s_aT, t + 1)
                three_pass(psum[:, 7, 0:D], actT, k.wo16, ones3[:, 0:P], bias3[:, KEPT_OUT:KEPT_OUT + D]).then_inc(s_wo, 1)

            def x_transpose(u, t):
                wait(pe, s_xlo, t + 1)
                projection_read(t + 1)
                wait(pe, s_rt, t * ROUTE_STEPS - (ROUTE_STEPS - 14))
                for c in range(2 * DC):
                    last = nc.tensor.transpose(psum16[:, 7, c * P:(c + 1) * P], halves(xrow, u, c * P, (c + 1) * P), ident16[:])
                last.then_inc(s_xtr, 1)

            def gate(t):
                wait(pe, s_x2T, t + 1)
                three_pass(psum[:, 7, 0:E], actT, k.wg16, ones3[:, 0:P], bias3[:, KEPT_G:KEPT_G + E]).then_inc(s_gate, 1)

            def projection_read(t):
                wait(pe, s_h2, min(t + 1, TILES) if isinstance(t, int) else t + 1)

            def rank(t):
                projection_read(t + 2)
                wait(pe, s_mem, t + 1)
                nc.tensor.matmul(psum[:, 7, 16:16 + E], k.before[:], member[:], start=True, stop=True)
                nc.tensor.matmul(psum[:, 7, 16 + E:16 + 2 * E], k.ones_sq[:], member[:], start=True, stop=True).then_inc(s_rank, 1)

            pe.wait_ge(s_po, 1)
            for t in range(2):
                for s in range(H):
                    scores(0, t, t, s)
                if t == 0:
                    max_transpose(0, 0)

            def step(i, u, t):
                for p in range(PAIRS):
                    if p == 0:
                        scores_t(i, u, t, p)
                        if known(t, 1):
                            max_transpose(ahead(i, u, 1)[1], t + 1)
                    if known(t, 2):
                        for s in (2 * p, 2 * p + 1):
                            scores(*ahead(i, u, 2), t + 2, s)
                    if p > 0:
                        scores_t(i, u, t, p)
                    if p >= 2:
                        values(i, u, t, p - 2)
                    elif known(t, -1):
                        values(*ahead(i, u, -1), t - 1, p + PAIRS - 2)
                    if p == 0 and known(t, -2):
                        project(t - 2)
                    if p == 1 and known(t, -4):
                        rank(t - 4)
                    if p == 2 and known(t, -3):
                        x_transpose(ahead(i, u, -3)[1], t - 3)
                    if p == 3 and known(t, -3):
                        gate(t - 3)
                    if p == 5 and known(t, -1):
                        out_transpose(t - 1)
                    if p == 7 and known(t, -1):
                        att_transpose(t - 1)

            over_tiles(pe, step)
            last = TILES // RING - 1
            values(last, RING - 1, TILES - 1, PAIRS - 2)
            values(last, RING - 1, TILES - 1, PAIRS - 1)
            project(TILES - 2)
            rank(TILES - 4)
            x_transpose(RING - 3, TILES - 3)
            gate(TILES - 3)
            out_transpose(TILES - 1)
            att_transpose(TILES - 1)
            project(TILES - 1)
            rank(TILES - 3)
            for u in (RING - 2, RING - 1):
                x_transpose(u, TILES - RING + u)
                gate(TILES - RING + u)
                rank(TILES - RING + u)


def slot_table(dve, k, s_step, s_tail, s_in, pcol, tail, sl, sg, se, si, rows, s_rows):
    v_ = k.nc.vector
    n = SLOTS_RUN
    step = [0]

    def then(ins):
        ins.then_inc(s_step, 1)
        step[0] += 1
        dve.wait_ge(s_step, step[0])

    dve.wait_ge(s_in, 2 * 16)
    final = k.base[:, 0, :]
    v_.tensor_scalar(tail[:], final, pcol[:, 0:1], None, ALU.add).then_inc(s_tail, 1)
    dve.wait_ge(s_rows, 1)
    v_.tensor_scalar(rows[:, TOKEN:TOKEN + 1], pcol[:, 0:1], float(TOKENS), None, ALU.add).then_inc(s_tail, 1)
    up, last, tiles, ends = (se[:, j, :] for j in range(4))
    slot, skipped, row, past, behind = (sl[:, j, :] for j in range(1, 6))
    iota, exp_ = sl[:, 0, :], k.slot_expert[:]
    then(v_.scalar_tensor_tensor(out=up, in0=k.iota_e[:], scalar=-float(REGION), in1=final,
                                 op0=ALU.mult, op1=ALU.add))
    then(v_.tensor_scalar(up, up, float(P - 1), None, ALU.add))
    then(v_.tensor_copy(si[:, 0, :], up))
    then(v_.tensor_scalar(si[:, 1, :], si[:, 0, :], P.bit_length() - 1, None, ALU.arith_shift_right))
    then(v_.tensor_copy(tiles, si[:, 1, :]))
    then(v_.tensor_copy(ends[:, 0:1], tiles[:, 0:1]))
    for e in range(1, E):
        then(v_.tensor_tensor(ends[:, e:e + 1], ends[:, e - 1:e], tiles[:, e:e + 1], ALU.add))
    then(v_.tensor_scalar(last[:, 0:1], ends[:, E - 1:E], -1.0, None, ALU.add))
    then(v_.tensor_scalar(slot, iota, last[:, 0:1], None, ALU.min))
    then(v_.tensor_tensor(sg[:, 0, :, :], slot.unsqueeze(2).to_broadcast([P, n, E]), ends.unsqueeze(1).to_broadcast([P, n, E]), ALU.is_ge))
    then(v_.tensor_tensor(sg[:, 1, :, :], sg[:, 0, :, :], tiles.unsqueeze(1).to_broadcast([P, n, E]), ALU.mult))
    then(v_.tensor_reduce(exp_, sg[:, 0, :, :], AX_X, ALU.add))
    then(v_.tensor_reduce(skipped, sg[:, 1, :, :], AX_X, ALU.add))
    then(v_.tensor_tensor(row, slot, skipped, ALU.subtract))
    then(v_.tensor_scalar(row, row, float(P), None, ALU.mult))
    then(v_.scalar_tensor_tensor(out=row, in0=exp_, scalar=float(REGION), in1=row, op0=ALU.mult, op1=ALU.add))
    then(v_.tensor_scalar(past, iota, ends[:, E - 1:E], None, ALU.is_ge))
    then(v_.tensor_scalar(behind, row, -1.0, final[:, E - 1:E], ALU.mult, ALU.add))
    then(v_.tensor_tensor(behind, behind, past, ALU.mult))
    then(v_.tensor_tensor(row, row, behind, ALU.add))
    then(v_.tensor_copy(k.slot_tab[:, 0, :], exp_[0:1, :]))
    then(v_.tensor_copy(k.slot_tab[:, 1, :], row[0:1, :]))


def plan(k):
    nc, sem = k.nc, k.sem
    with ExitStack() as ph:
        def sb(name, shape, dt):
            return ph.enter_context(nc.sbuf_tensor(name, shape, dt))

        tail = sb("tail", [P, E], I32)
        pcol = sb("pcol", [P, 1], F32)
        rows = sb("empty_rows", [P, XW], I32)
        spare = sb("spare_rows", [P, D], F32)
        sl = sb("sl", [P, 6, SLOTS_RUN], F32)
        sg = sb("sg", [P, 2, SLOTS_RUN, E], F32)
        se = sb("se", [P, 4, E], F32)
        si = sb("si", [P, 2, E], I32)
        s_in, s_rows, s_spare = sem("plan_constants_loaded"), sem("empty_rows_zeroed"), sem("spare_rows_zeroed")
        s_tail, s_tail_out, s_spare_out = sem("tail_rows_made"), sem("tails_stored"), sem("spare_rows_stored")
        s_tab = sem("slot_table_steps")
        block = ph.enter_context(nc.Block())

        @block.sync
        def _(sp):
            sp.dma_start(pcol[:], k.part_col).then_inc(s_in, 16)
            sp.dma_start(sl[:, 0, :], k.slot_iota.to_broadcast([P, SLOTS_RUN])).then_inc(s_in, 16)
            sp.wait_ge(s_spare, 1)
            sp.dma_start(k.out[TOKENS:TOKENS + P, :], spare[:]).then_inc(s_spare_out, 16)
            sp.wait_ge(s_spare_out, 16)

        @block.vector
        def _(dve):
            slot_table(dve, k, s_tab, s_tail, s_in, pcol, tail, sl, sg, se, si, rows, s_rows)

        @block.gpsimd
        def _(pool):
            nc.gpsimd.memset(rows[:], 0).then_inc(s_rows, 1)
            nc.gpsimd.memset(spare[:], 0.0).then_inc(s_spare, 1)
            pool.wait_ge(s_tail, 2)
            for e in range(E):
                nc.gpsimd.indirect_dma_start(k.x_lists, bass.IndirectOffsetOnAxis(tail[:, e:e + 1], 0), rows[:], None)\
                  .then_inc(s_tail_out, 16)
            pool.wait_ge(s_tail_out, E * 16)


def experts(k):
    nc, sem, psum, psum16 = k.nc, k.sem, k.psum, k.psum16
    with ExitStack() as ph:
        def sb(name, shape, dt):
            return ph.enter_context(nc.sbuf_tensor(name, shape, dt))

        xin = sb("xin", [P, 2, XW], I32)
        token = sb("token", [P, 2], I32)
        weight = sb("weight", [P, 2, 3], F32)
        xT = sb("xT_e", [P, 2, 2 * DC, P], F16)
        gel = sb("gel", [P, 2, FC, P], F32)
        h16 = sb("h16", [P, 2, 2, FC, P], F16)
        y = sb("y", [P, 2, D], F32)
        b2_all = sb("b2_all", [P, E * D], F32)
        s_b2 = sem("b2_loaded")

        s_x = [sem(f"rows_loaded{u}") for u in range(2)]
        s_tr = [sem(f"rows_transposed{u}") for u in range(2)]
        s_xT = [sem(f"rows_T_copied{u}") for u in range(2)]
        s_h = [sem(f"hidden_made{u}") for u in range(2)]
        s_g = [sem(f"gelu_made{u}") for u in range(2)]
        s_hi, s_lo = [sem(f"hidden_hi{u}") for u in range(2)], [sem(f"hidden_lo{u}") for u in range(2)]
        s_y = [sem(f"y_made{u}") for u in range(2)]
        s_m = [sem(f"token_and_weight_made{u}") for u in range(2)]
        s_yb = [sem(f"y_bias_added{u}") for u in range(2)]
        s_yc = [sem(f"y_copied{u}") for u in range(2)]
        s_yo = [sem(f"y_added_to_output{u}") for u in range(2)]

        block = ph.enter_context(nc.Block())

        def entry(eng, which, s):
            top = (E - 1, (E - 1) * REGION + TOKENS)[which]
            return eng.value_load(k.slot_tab[0:1, which, bass.ds(s, 1)], min_val=0, max_val=top)

        @block.sync
        def _(sp):
            sp.dma_start(b2_all[:], k.b2.to_broadcast([P, E * D])).then_inc(s_b2, 16)

            def turn(i):
                for u in range(2):
                    row = entry(sp, 1, i * 2 + u)
                    wait(sp, s_m[u], i * 4)
                    sp.dma_start(xin[:, u, :], k.x_lists[bass.ds(row, P), :]).then_inc(s_x[u], 16)

            turns(sp, SLOTS_RUN // 2, turn)

        @block.gpsimd
        def _(pool):

            def turn(i):
                for u in range(2):
                    held(pool, k.s_passed, (s_yc[u], i + 1), (s_yo[1 - u], (i + u) * 16))
                    nc.gpsimd.indirect_dma_start(k.out, bass.IndirectOffsetOnAxis(token[:, u:u + 1], 0), y[:, u, :], None,
                                                 compute_op=ALU.add).then_inc(s_yo[u], 16)

            turns(pool, SLOTS_RUN // 2, turn)
            for u in range(2):
                pool.wait_ge(s_yo[u], SLOTS_RUN // 2 * 16)

        @block.scalar
        def _(act):

            def turn(i):
                for u in range(2):
                    e = entry(act, 0, i * 2 + u)
                    wait(act, s_lo[u], i * 2)
                    for f in range(FC):
                        wait(act, s_h[u], i * 2 + f // 4 + 1)
                        nc.scalar.activation(gel[:, u, f, :], psum[:, 2 + 2 * u + f // 4, (f % 4) * P:(f % 4 + 1) * P],
                                             ACT.Gelu_apprx_tanh, bias=k.b1_col[:, bass.ds(e * FC + f, 1)],
                                             scale=1.0 / PS).then_inc(s_g[u], 1)

            turns(act, SLOTS_RUN // 2, turn)

        @block.vector
        def _(dve):
            v_ = nc.vector

            def y_copy(i, u):
                dve.wait_ge(s_y[u], i + 1)
                wait(dve, s_yo[u], i * 16)
                e = entry(dve, 0, i * 2 + u)
                v_.scalar_tensor_tensor(out=y[:, u, :], in0=psum[:, 6 + u, 0:D], scalar=1.0 / YS,
                                        in1=b2_all[:, bass.ds(e * D, D)], op0=ALU.mult, op1=ALU.add).then_inc(s_yb[u], 1)
                dve.wait_ge(s_yb[u], i + 1)
                v_.tensor_scalar(y[:, u, :], y[:, u, :], weight[:, u, 2:3], None, ALU.mult).then_inc(s_yc[u], 1)

            def tokens(i, u):
                dve.wait_ge(s_x[u], (i + 1) * 16)
                wait(dve, s_yo[u], i * 16)
                v_.tensor_copy(token[:, u:u + 1], xin[:, u, TOKEN:TOKEN + 1]).then_inc(s_m[u], 1)
                w = xin[:, u, WEIGHTS:FIRST + 1].bitcast(F32)
                e = k.slot_expert[:, bass.ds(i * 2 + u, 1)]
                v_.scalar_tensor_tensor(out=weight[:, u, 0:1], in0=w[:, 2:3], scalar=e, in1=w[:, 0:1],
                                        op0=ALU.is_equal, op1=ALU.mult).then_inc(s_m[u], 1)
                v_.scalar_tensor_tensor(out=weight[:, u, 1:2], in0=w[:, 2:3], scalar=e, in1=w[:, 1:2],
                                        op0=ALU.not_equal, op1=ALU.mult).then_inc(s_m[u], 1)
                dve.wait_ge(s_m[u], i * 4 + 3)
                v_.tensor_tensor(weight[:, u, 2:3], weight[:, u, 0:1], weight[:, u, 1:2], ALU.add).then_inc(s_m[u], 1)

            def split(i, u):
                for half in range(2):
                    c = slice(half * 4, half * 4 + 4)
                    dve.wait_ge(s_g[u], i * FC + half * 4 + 4)
                    if half == 0:
                        wait(dve, s_y[u], i)
                    v_.tensor_scalar(h16[:, u, 0, c, :], gel[:, u, c, :], HS, None, ALU.mult).then_inc(s_hi[u], 1)
                    dve.wait_ge(s_hi[u], i * 2 + half + 1)
                    v_.scalar_tensor_tensor(out=h16[:, u, 1, c, :], in0=gel[:, u, c, :], scalar=HS, in1=h16[:, u, 0, c, :],
                                            op0=ALU.mult, op1=ALU.subtract).then_inc(s_lo[u], 1)

            def x_copy(i, u):
                dve.wait_ge(s_tr[u], i + 1)
                wait(dve, s_h[u], i * 2)
                v_.tensor_copy(xT[:, u, :, :].rearrange("p c t -> p (c t)"), psum16[:, u, 0:4 * P]).then_inc(s_xT[u], 1)

            dve.wait_ge(s_b2, 16)
            x_copy(0, 0)

            def step(i, u, first, last):
                if not last:
                    x_copy(*((i, 1) if u == 0 else (i + 1, 0)))
                split(i, u)
                tokens(i, u)
                if not first:
                    y_copy(*((i, 0) if u == 1 else (i - 1, 1)))

            step(0, 0, True, False)
            step(0, 1, False, False)
            with dve.Fori(1, SLOTS_RUN // 2 - 1) as i:
                step(i, 0, False, False)
                step(i, 1, False, False)
            step(SLOTS_RUN // 2 - 1, 0, False, False)
            step(SLOTS_RUN // 2 - 1, 1, False, True)
            y_copy(SLOTS_RUN // 2 - 1, 1)

        @block.tensor
        def _(pe):
            def transpose(i, u):
                pe.wait_ge(s_x[u], (i + 1) * 16)
                wait(pe, s_xT[u], i)
                for c in range(2 * DC):
                    last = nc.tensor.transpose(psum16[:, u, c * P:(c + 1) * P], halves(xin, u, c * P, (c + 1) * P), k.ident16[:])
                last.then_inc(s_tr[u], 1)

            def hidden(i, u, e):
                pe.wait_ge(s_xT[u], i + 1)
                wait(pe, s_g[u], i * FC)
                for f in range(FC):
                    ps = psum[:, 2 + 2 * u + f // 4, (f % 4) * P:(f % 4 + 1) * P]
                    for c in range(DC):
                        for wl, xl in ((0, 0), (0, 1), (1, 0)):
                            last = nc.tensor.matmul(ps, k.w1_16[:, bass.ds(e * (DC * 2 * F) + ((c * 2 + wl) * F + f * P), P)],
                                                    xT[:, u, xl * DC + c, :], start=(c == 0 and wl == 0 and xl == 0),
                                                    stop=(c == DC - 1 and wl == 1))
                    if f % 4 == 3:
                        last.then_inc(s_h[u], 1)

            def outputs(i, u, e):
                wait(pe, s_yc[u], i)
                ps = psum[:, 6 + u, 0:D]
                for f in range(FC):
                    if f % 4 == 0:
                        pe.wait_ge(s_lo[u], i * 2 + f // 4 + 1)
                    for wl, hl in ((0, 0), (0, 1), (1, 0)):
                        last = nc.tensor.matmul(ps, h16[:, u, hl, f, :], k.w2_16[:, bass.ds(e * (FC * 2 * D) + (f * 2 + wl) * D, D)],
                                                start=(f == 0 and wl == 0 and hl == 0), stop=(f == FC - 1 and wl == 1))
                last.then_inc(s_y[u], 1)

            transpose(0, 0)

            def step(i, u, first, last):
                hidden(i, u, entry(pe, 0, i * 2 + u))
                if not last:
                    transpose(*((i, 1) if u == 0 else (i + 1, 0)))
                if not first:
                    outputs(*((i, 0) if u == 1 else (i - 1, 1)), entry(pe, 0, i * 2 + u - 1))

            step(0, 0, True, False)
            step(0, 1, False, False)
            with pe.Fori(1, SLOTS_RUN // 2 - 1) as i:
                step(i, 0, False, False)
                step(i, 1, False, False)
            step(SLOTS_RUN // 2 - 1, 0, False, False)
            step(SLOTS_RUN // 2 - 1, 1, False, True)
            outputs(SLOTS_RUN // 2 - 1, 1, entry(pe, 0, SLOTS_RUN - 1))


def position_table(np):
    pos = np.arange(S, dtype=np.float32)
    i = np.arange(D // 2, dtype=np.float32)
    inv = np.power(10000.0, (np.float32(-2.0) * i / np.float32(D)).astype(np.float64)).astype(np.float32)
    ang = pos[:, None] * inv[None, :]
    table = np.stack([np.sin(ang.astype(np.float64)), np.cos(ang.astype(np.float64))], axis=-1)
    return np.tile(table.reshape(S, D).astype(np.float32), (B, 1))


def window_masks(np):
    n = np.arange(NB)[:, None, None]
    i = np.arange(P)[None, :, None]
    j = np.arange(3 * P)[None, None, :]
    key = n * P - P + j
    inside = (np.abs(key - (n * P + i)) <= P) & (key >= 0) & (key < S)
    return np.tile(np.where(inside, 0, NEG_BITS).reshape(NB * P, 3 * P).astype(np.uint16), (B, 1))


def kernel(x, L0_tok_emb_table, L0_attn_Wqkv, L0_attn_bqkv, L0_attn_Wout, L0_attn_bout, L0_ffn_Wg, L0_ffn_bg,
           L0_ffn_W1, L0_ffn_b1, L0_ffn_W2, L0_ffn_b2):
    import numpy as np
    import concourse.bacc as bacc
    from concourse.bass_utils import run_bass_kernel_spmd

    def by_dim(w):
        w = np.asarray(w).reshape(-1, 2, PAIRS, DH)
        return w.transpose(0, 1, 3, 2).reshape(-1, D)

    wqkv = np.asarray(L0_attn_Wqkv)
    bqkv = np.asarray(L0_attn_bqkv).reshape(1, -1)
    lay = lambda w: np.concatenate([by_dim(w[:, 0:D]), by_dim(w[:, D:2 * D]), w[:, 2 * D:]], axis=1)
    row = np.concatenate([lay(bqkv)[0], np.asarray(L0_attn_bout), np.asarray(L0_ffn_bg)])
    valid = np.zeros((BLOCKS, P), np.float16)
    for b in range(B):
        valid[b * (NB + 2) + 1:b * (NB + 2) + 1 + NB] = 1
    arrays = {
        "x_idx": np.asarray(x).reshape(TILES, P).T,
        "emb": np.asarray(L0_tok_emb_table),
        "pe_tab": position_table(np),
        "wqkv": lay(wqkv),
        "wout": np.asarray(L0_attn_Wout),
        "wg": np.asarray(L0_ffn_Wg),
        "w1": np.asarray(L0_ffn_W1).reshape(E * D, F),
        "b1": np.asarray(L0_ffn_b1).reshape(E * FC, P).T,
        "w2": np.asarray(L0_ffn_W2).reshape(E * F, D),
        "b2": np.asarray(L0_ffn_b2).reshape(1, E * D),
        "biases": np.stack([row] * 3),
        "part_sel": np.eye(3, dtype=np.float32),
        "mask_tab": window_masks(np),
        "valid_row": np.tile(valid.reshape(1, 1, -1), (1, PAIRS, 1)),
        "iota8": np.tile(np.arange(E, dtype=np.float32), (P, 1)),
        "slot_iota": np.arange(SLOTS_RUN, dtype=np.float32).reshape(1, -1),
        "region_base": np.tile(np.arange(E, dtype=np.float32) * REGION, (P, 1)),
        "part_col": np.arange(P, dtype=np.float32).reshape(P, 1),
        "token_of": np.arange(TOKENS, dtype=np.int32).reshape(TILES, P).T,
    }
    arrays = {n: np.ascontiguousarray(a) for n, a in arrays.items()}
    nc = bacc.Bacc("TRN2", target_bir_lowering=False, num_devices=1)
    ins = [nc.dram_tensor(n, a.shape, mybir.dt.from_np(a.dtype), kind="ExternalInput").ap() for n, a in arrays.items()]
    out = nc.dram_tensor("out", (TOKENS + P, D), F32, kind="ExternalOutput").ap()
    build(nc, *ins, out)
    r = run_bass_kernel_spmd(nc, [arrays], core_ids=[0])
    return r.results[0]["out"][:TOKENS].reshape(B, S, D)
```
